# Optimizing a Trainium2 kernel written in Bass

```python
import numpy as np
import jax
import jax.numpy as jnp

def _softmax(x, axis=-1):
    return jax.nn.softmax(x, axis=axis)

def _gelu(x):
    return jax.nn.gelu(x, approximate=True)

def _silu(x):
    return jax.nn.silu(x)

def _sigmoid(x):
    return jax.nn.sigmoid(x)

def _layernorm(x, axis=-1, eps=1e-05):
    m = jnp.mean(x, axis=axis, keepdims=True)
    v = jnp.var(x, axis=axis, keepdims=True)
    return (x - m) / jnp.sqrt(v + eps)

def _scatter_add(tgt, idx, src, axis=0):
    return tgt.at[idx].add(src)

def _segment_sum(src, seg, n):
    return jax.ops.segment_sum(src, seg, n)
kernel_name = 'mk_hybrid_d1_jaxref_r8_ff9226'

def setup_inputs(seed: int=0):
    np.random.seed(seed)
    _w = jnp.asarray

    def _L0_attn_a_setup():
        import jax, jax.numpy as jnp
        import numpy as np
        import math
        B, L, D = (2, 256, 256)
        H, DH = (16, 128)
        R = 16
        WIN = 64
        EPS = 1e-06

        def _lora_proj(h, Wb, A, Bm, scale):
            return h @ Wb.T + h @ A.T @ Bm.T * scale

        def _rope_freqs(seq_len, d_head):
            half = d_head // 2
            theta = 1.0 / 10000.0 ** (jnp.arange(half, dtype=jnp.float32) / half)
            freqs = jnp.arange(seq_len, dtype=jnp.float32)[:, None] * theta[None, :]
            emb = jnp.concatenate([freqs, freqs], axis=-1)
            return (jnp.cos(emb), jnp.sin(emb))

        def _apply_rope(x, cos, sin):
            half = x.shape[-1] // 2
            x1, x2 = (x[..., :half], x[..., half:])
            rotated = jnp.concatenate([-x2, x1], axis=-1)
            return x * cos[None, None] + rotated * sin[None, None]
        key = jax.random.key(seed)
        ks = jax.random.split(key, 16)

        def rn(k, shape, s=1.0):
            return jax.random.normal(k, shape, dtype=jnp.float32) * s
        d_in_std = 1.0 / math.sqrt(D)
        return {'x': rn(ks[0], (B, L, D)), 'norm_w': jnp.ones((D,), jnp.float32), 'wq': rn(ks[1], (H * DH, D), d_in_std), 'wk': rn(ks[2], (H * DH, D), d_in_std), 'wv': rn(ks[3], (H * DH, D), d_in_std), 'wo': rn(ks[4], (D, H * DH), d_in_std), 'qA': rn(ks[5], (R, D), 0.02), 'qB': rn(ks[6], (H * DH, R), 0.02), 'kA': rn(ks[7], (R, D), 0.02), 'kB': rn(ks[8], (H * DH, R), 0.02), 'vA': rn(ks[9], (R, D), 0.02), 'vB': rn(ks[10], (H * DH, R), 0.02), 'oA': rn(ks[11], (R, H * DH), 0.02), 'oB': rn(ks[12], (D, R), 0.02)}
    _L0_attn_a_in = _L0_attn_a_setup()

    def _L0_attn_b_setup():
        import jax, jax.numpy as jnp
        import numpy as np
        B, S, E = (2, 256, 256)
        H, KVH, D = (32, 8, 64)
        ROPE_THETA = 10000.0

        def apply_rope(t, pos):
            d = t.shape[-1]
            half = d // 2
            inv_freq = 1.0 / ROPE_THETA ** (jnp.arange(half, dtype=jnp.float32) / half)
            ang = pos[:, None].astype(jnp.float32) * inv_freq[None, :]
            cos = jnp.cos(ang)[None, None]
            sin = jnp.sin(ang)[None, None]
            t1, t2 = (t[..., :half], t[..., half:])
            return jnp.concatenate([t1 * cos - t2 * sin, t1 * sin + t2 * cos], axis=-1).astype(t.dtype)
        key = jax.random.key(seed)
        ks = jax.random.split(key, 5)
        sc = 1.0 / np.sqrt(E)
        return {'x': jax.random.normal(ks[0], (B, S, E), jnp.float32), 'Wq': jax.random.normal(ks[1], (E, H * D), jnp.float32) * sc, 'Wk': jax.random.normal(ks[2], (E, KVH * D), jnp.float32) * sc, 'Wv': jax.random.normal(ks[3], (E, KVH * D), jnp.float32) * sc, 'Wo': jax.random.normal(ks[4], (H * D, E), jnp.float32) * sc}
    _L0_attn_b_in = _L0_attn_b_setup()

    def _L0_ffn_setup():
        import jax, jax.numpy as jnp
        import numpy as np
        B, S, H = (2, 256, 256)
        E, K = (16, 4)
        I = 176
        NS = 2
        SI = I * NS

        def _mlp(x, wg, wu, wd):
            return jax.nn.silu(x @ wg.T) * (x @ wu.T) @ wd.T
        key = jax.random.key(seed)
        ks = jax.random.split(key, 8)
        sc = lambda k, shape, fan: jax.random.normal(k, shape, jnp.float32) * fan ** (-0.5)
        return {'hidden_states': jax.random.normal(ks[0], (B, S, H), jnp.float32), 'gate_w': sc(ks[1], (E, H), H), 'w_gate': sc(ks[2], (E, I, H), H), 'w_up': sc(ks[3], (E, I, H), H), 'w_down': sc(ks[4], (E, H, I), I), 'sw_gate': sc(ks[5], (SI, H), H), 'sw_up': sc(ks[6], (SI, H), H), 'sw_down': sc(ks[7], (H, SI), SI)}
    _L0_ffn_in = _L0_ffn_setup()
    _d = {'L0_attn_a_x': _L0_attn_a_in['x'], 'L0_attn_a_norm_w': _L0_attn_a_in['norm_w'], 'L0_attn_a_wq': _L0_attn_a_in['wq'], 'L0_attn_a_wk': _L0_attn_a_in['wk'], 'L0_attn_a_wv': _L0_attn_a_in['wv'], 'L0_attn_a_wo': _L0_attn_a_in['wo'], 'L0_attn_a_qA': _L0_attn_a_in['qA'], 'L0_attn_a_qB': _L0_attn_a_in['qB'], 'L0_attn_a_kA': _L0_attn_a_in['kA'], 'L0_attn_a_kB': _L0_attn_a_in['kB'], 'L0_attn_a_vA': _L0_attn_a_in['vA'], 'L0_attn_a_vB': _L0_attn_a_in['vB'], 'L0_attn_a_oA': _L0_attn_a_in['oA'], 'L0_attn_a_oB': _L0_attn_a_in['oB'], 'L0_attn_b_Wq': _L0_attn_b_in['Wq'], 'L0_attn_b_Wk': _L0_attn_b_in['Wk'], 'L0_attn_b_Wv': _L0_attn_b_in['Wv'], 'L0_attn_b_Wo': _L0_attn_b_in['Wo'], 'L0_ffn_gate_w': _L0_ffn_in['gate_w'], 'L0_ffn_w_gate': _L0_ffn_in['w_gate'], 'L0_ffn_w_up': _L0_ffn_in['w_up'], 'L0_ffn_w_down': _L0_ffn_in['w_down'], 'L0_ffn_sw_gate': _L0_ffn_in['sw_gate'], 'L0_ffn_sw_up': _L0_ffn_in['sw_up'], 'L0_ffn_sw_down': _L0_ffn_in['sw_down']}
    _x0 = _d['L0_attn_a_x']
    _d['L0_attn_a_x'] = jax.random.normal(jax.random.fold_in(jax.random.key(seed), 1), (1, 1024, 256), dtype=_x0.dtype)
    del _x0
    return _d

def reference(L0_attn_a_x, L0_attn_a_norm_w, L0_attn_a_wq, L0_attn_a_wk, L0_attn_a_wv, L0_attn_a_wo, L0_attn_a_qA, L0_attn_a_qB, L0_attn_a_kA, L0_attn_a_kB, L0_attn_a_vA, L0_attn_a_vB, L0_attn_a_oA, L0_attn_a_oB, L0_attn_b_Wq, L0_attn_b_Wk, L0_attn_b_Wv, L0_attn_b_Wo, L0_ffn_gate_w, L0_ffn_w_gate, L0_ffn_w_up, L0_ffn_w_down, L0_ffn_sw_gate, L0_ffn_sw_up, L0_ffn_sw_down):

    def _L0_attn_a_ref(x, norm_w, wq, wk, wv, wo, qA, qB, kA, kB, vA, vB, oA, oB):
        import jax, jax.numpy as jnp
        import numpy as np
        import math
        B, L, D = (2, 256, 256)
        H, DH = (16, 128)
        R = 16
        WIN = 64
        EPS = 1e-06

        def _lora_proj(h, Wb, A, Bm, scale):
            return h @ Wb.T + h @ A.T @ Bm.T * scale

        def _rope_freqs(seq_len, d_head):
            half = d_head // 2
            theta = 1.0 / 10000.0 ** (jnp.arange(half, dtype=jnp.float32) / half)
            freqs = jnp.arange(seq_len, dtype=jnp.float32)[:, None] * theta[None, :]
            emb = jnp.concatenate([freqs, freqs], axis=-1)
            return (jnp.cos(emb), jnp.sin(emb))

        def _apply_rope(x, cos, sin):
            half = x.shape[-1] // 2
            x1, x2 = (x[..., :half], x[..., half:])
            rotated = jnp.concatenate([-x2, x1], axis=-1)
            return x * cos[None, None] + rotated * sin[None, None]
        lora_scale = 1.0 / qA.shape[0]
        residual = x
        h = x * jax.lax.rsqrt(jnp.mean(x * x, axis=-1, keepdims=True) + EPS) * norm_w
        Q = _lora_proj(h, wq, qA, qB, lora_scale)
        K = _lora_proj(h, wk, kA, kB, lora_scale)
        V = _lora_proj(h, wv, vA, vB, lora_scale)
        b, l, _ = x.shape
        Q = Q.reshape(b, l, H, DH).transpose(0, 2, 1, 3)
        K = K.reshape(b, l, H, DH).transpose(0, 2, 1, 3)
        V = V.reshape(b, l, H, DH).transpose(0, 2, 1, 3)
        cos, sin = _rope_freqs(l, DH)
        Q = _apply_rope(Q, cos, sin)
        K = _apply_rope(K, cos, sin)
        i = jnp.arange(l)[:, None]
        j = jnp.arange(l)[None, :]
        valid = (j <= i) & (j >= i - WIN + 1)
        mask = jnp.where(valid, 0.0, -jnp.inf).astype(x.dtype)
        scores = jnp.einsum('bhqd,bhkd->bhqk', Q, K) / math.sqrt(DH)
        attn = jax.nn.softmax(scores + mask[None, None], axis=-1)
        out = jnp.einsum('bhqk,bhkd->bhqd', attn, V)
        out = out.transpose(0, 2, 1, 3).reshape(b, l, H * DH)
        out = _lora_proj(out, wo, oA, oB, lora_scale)
        return residual + out

    def _L0_attn_b_ref(x, Wq, Wk, Wv, Wo):
        import jax, jax.numpy as jnp
        import numpy as np
        B, S, E = (2, 256, 256)
        H, KVH, D = (32, 8, 64)
        ROPE_THETA = 10000.0

        def apply_rope(t, pos):
            d = t.shape[-1]
            half = d // 2
            inv_freq = 1.0 / ROPE_THETA ** (jnp.arange(half, dtype=jnp.float32) / half)
            ang = pos[:, None].astype(jnp.float32) * inv_freq[None, :]
            cos = jnp.cos(ang)[None, None]
            sin = jnp.sin(ang)[None, None]
            t1, t2 = (t[..., :half], t[..., half:])
            return jnp.concatenate([t1 * cos - t2 * sin, t1 * sin + t2 * cos], axis=-1).astype(t.dtype)
        b, s, _ = x.shape
        g = H // KVH
        q = (x @ Wq).reshape(b, s, H, D).transpose(0, 2, 1, 3)
        k = (x @ Wk).reshape(b, s, KVH, D).transpose(0, 2, 1, 3)
        v = (x @ Wv).reshape(b, s, KVH, D).transpose(0, 2, 1, 3)
        pos = jnp.arange(s)
        q = apply_rope(q, pos)
        k = apply_rope(k, pos)
        k = jnp.repeat(k, g, axis=1)
        v = jnp.repeat(v, g, axis=1)
        scores = jnp.einsum('bhqd,bhkd->bhqk', q, k) / jnp.sqrt(jnp.float32(D))
        causal = jnp.tril(jnp.ones((s, s), dtype=bool))
        scores = jnp.where(causal[None, None], scores, jnp.finfo(x.dtype).min)
        attn = jax.nn.softmax(scores, axis=-1)
        out = jnp.einsum('bhqk,bhkd->bhqd', attn, v)
        out = out.transpose(0, 2, 1, 3).reshape(b, s, H * D)
        return out @ Wo

    def _L0_ffn_ref(hidden_states, gate_w, w_gate, w_up, w_down, sw_gate, sw_up, sw_down):
        import jax, jax.numpy as jnp
        import numpy as np
        B, S, H = (2, 256, 256)
        E, K = (16, 4)
        I = 176
        NS = 2
        SI = I * NS

        def _mlp(x, wg, wu, wd):
            return jax.nn.silu(x @ wg.T) * (x @ wu.T) @ wd.T
        x = hidden_states.reshape(-1, H)
        T = x.shape[0]
        scores = jax.nn.softmax(x @ gate_w.T, axis=-1)
        topk_w, topk_idx = jax.lax.top_k(scores, K)
        topk_w = topk_w / jnp.sum(topk_w, axis=-1, keepdims=True)
        cw = jnp.zeros((T, E), x.dtype).at[jnp.arange(T)[:, None], topk_idx].add(topk_w)

        def step(acc, p):
            wg, wu, wd, w = p
            return (acc + w[:, None] * _mlp(x, wg, wu, wd), None)
        y, _ = jax.lax.scan(step, jnp.zeros_like(x), (w_gate, w_up, w_down, cw.T))
        y = y.reshape(hidden_states.shape)
        return y + _mlp(hidden_states, sw_gate, sw_up, sw_down)
    x = L0_attn_a_x
    x = x + _L0_attn_a_ref(_layernorm(x, axis=-1), L0_attn_a_norm_w, L0_attn_a_wq, L0_attn_a_wk, L0_attn_a_wv, L0_attn_a_wo, L0_attn_a_qA, L0_attn_a_qB, L0_attn_a_kA, L0_attn_a_kB, L0_attn_a_vA, L0_attn_a_vB, L0_attn_a_oA, L0_attn_a_oB)
    x = x + _L0_ffn_ref(_layernorm(x, axis=-1), L0_ffn_gate_w, L0_ffn_w_gate, L0_ffn_w_up, L0_ffn_w_down, L0_ffn_sw_gate, L0_ffn_sw_up, L0_ffn_sw_down)
    x = x + _L0_attn_b_ref(_layernorm(x, axis=-1), L0_attn_b_Wq, L0_attn_b_Wk, L0_attn_b_Wv, L0_attn_b_Wo)
    x = x + _L0_ffn_ref(_layernorm(x, axis=-1), L0_ffn_gate_w, L0_ffn_w_gate, L0_ffn_w_up, L0_ffn_w_down, L0_ffn_sw_gate, L0_ffn_sw_up, L0_ffn_sw_down)
    return x

_drawn_inputs = setup_inputs


def setup_inputs(seed=0):
    import zlib

    import numpy as np

    out = dict(_drawn_inputs(seed))
    spreads = {'L0_attn_a_norm_w': (1.0, 0.2)}
    factors = {'L0_attn_a_qA': 8.0,
     'L0_attn_a_qB': 8.0,
     'L0_attn_a_kA': 8.0,
     'L0_attn_a_kB': 8.0,
     'L0_attn_a_vA': 8.0,
     'L0_attn_a_vB': 8.0,
     'L0_attn_a_oA': 8.0,
     'L0_attn_a_oB': 8.0}
    for name, (base, spread) in spreads.items():
        noise = np.random.default_rng([zlib.crc32(name.encode()), seed]).standard_normal(out[name].shape)
        drawn = base * np.exp(spread * noise) if base else spread * noise
        out[name] = jnp.asarray(drawn.astype(out[name].dtype))
    for name, factor in factors.items():
        out[name] = (out[name] * factor).astype(out[name].dtype)
    return out
```

```python
from contextlib import ExitStack

import numpy as np

import concourse.bass as bass
from concourse import mybir

F32 = mybir.dt.float32
F32R = mybir.dt.float32r
BF16 = mybir.dt.bfloat16
U32 = mybir.dt.uint32
ALU = mybir.AluOpType
ACT = mybir.ActivationFunctionType
AX = mybir.AxisListType

P = 128
T = 1024
NT = T // P
D = 256
NC = D // P
HALF = 512
LN_EPS = 1e-5
RMS_EPS = 1e-6

HA = 16
WIN = 64
PAD = WIN
TP = PAD + T + PAD
NV = TP // P
KW = WIN + P
RANK = 16
LORA_SCALE = 1.0 / RANK

NG = 8
QPG = 4
DB = 64
CHB = 12

NE = 16
TOPK = 4
I_E = 176
I_S = 352
NJ = (NE * I_E + I_S + P - 1) // P
NW = NE + 1


class Sems:

    def __init__(self, nc, ctx):
        self.nc, self.ctx, self.made = nc, ctx, {}

    def __call__(self, name):
        if name.startswith("g_"):
            name = "f" + name[1:]
        if name not in self.made:
            self.made[name] = self.ctx.enter_context(self.nc.semaphore(name))
        return self.made[name]


def build(nc, d, out, upto=99):
    ctx = ExitStack()
    with ctx:
        def sb(name, shape, dt=F32, c=ctx):
            return c.enter_context(nc.sbuf_tensor(name, shape, dt))

        sem = Sems(nc, ctx)
        ps = ctx.enter_context(nc.psum_tensor("ps", [P, 8, HALF], F32))

        x = sb("x_res", [P, NT, D])
        z = sb("z", [P, NT, D])
        xt_hi = sb("xt_hi", [P, NC, TP], F32R)
        xt_lo = sb("xt_lo", [P, NC, TP], F32R)
        ot = sb("ot", [P, HA, T])
        yt = sb("yt", [P, 2 * NC, HALF])
        idf = sb("idf", [P, P])
        idb = sb("idb", [P, P], BF16)
        norm_w = sb("norm_w", [P, NC])
        stats = sb("stats", [P, NT, 6])
        mv = sb("mv", [P, NT, 2])
        var = sb("var", [P, 2, NT])
        rstd = sb("rstd", [P, 2, NT])
        negh = sb("negh", [P, NT])
        rope = sb("rope", [P, 2, T])
        ra = sb("ra", [P, 2, HALF])
        rb = sb("rb", [P, 2, HALF])

        own = ExitStack()
        with own:
            wa = sb("wa", [P, 2, NC, 3, P], c=own)
            lb = sb("lb", [3 * RANK, 2, 3 * P], c=own)
            la = sb("la", [3 * RANK, NC, P], c=own)
            wef = sb("wef", [P, 2, NC, 3, P], c=own)
            wqk_hi = sb("wqk_hi", [P, 2, NC, 2, P], F32R, own)
            wqk_lo = sb("wqk_lo", [P, 2, NC, 2, P], F32R, own)
            wv_hi = sb("wv_hi", [P, NC, 2, P], F32R, own)
            wv_lo = sb("wv_lo", [P, NC, 2, P], F32R, own)
            qr = sb("qr", [P, 2, T], c=own)
            kr = sb("kr", [P, 2, PAD + T], c=own)
            va = sb("va", [P, NV, 2, P], c=own)
            pa = sb("pa", [P, NT, 2 * P], c=own)
            pta = sb("pta", [P, 2, HALF], c=own)
            nmax = sb("nmax", [P, NT], c=own)
            rsum = sb("rsum", [P, NT], c=own)
            rinv = sb("rinv", [P, NT], c=own)
            maska = sb("maska", [P, 2, KW], BF16, own)
            zt = sb("zt", [P, 2 * NC, HALF], c=own)
        own = ExitStack()
        with own:
            wo = sb("wo", [P, 2, D], c=own)
            oa = sb("oa", [RANK, 2, P], c=own)
            ob = sb("ob", [RANK, D], c=own)
            woe = sb("woe", [P, 2, D], c=own)
            wo_hi = sb("wo_hi", [P, 2, D], F32R, own)
            wo_lo = sb("wo_lo", [P, 2, D], F32R, own)
            ot_hi = sb("ot_hi", [P, 2, T], F32R, own)
            ot_lo = sb("ot_lo", [P, 2, T], F32R, own)
        own = ExitStack()
        with own:
            wf = sb("wf", [P, 2, 3 * D], c=own)
            wf_hi = sb("wf_hi", [P, 2, 3 * D], F32R, own)
            wf_lo = sb("wf_lo", [P, 2, 3 * D], F32R, own)
            sg = sb("sg", [P, 2, HALF], c=own)
            gu = sb("gu", [P, 2, HALF], c=own)
            hf = sb("hf", [P, 2, HALF], c=own)
            h_hi = sb("h_hi", [P, 2, HALF], F32R, own)
            h_lo = sb("h_lo", [P, 2, HALF], F32R, own)
            sel = sb("sel", [P, NJ * P], BF16, own)
            wg = sb("wg", [P, NC, NE], c=own)
            wg_hi = sb("wg_hi", [P, NC, NE], F32R, own)
            wg_lo = sb("wg_lo", [P, NC, NE], F32R, own)
            lg = sb("lg", [P, NT, NE], c=own)
            ex = sb("ex", [P, NT, NE], c=own)
            top = sb("top", [P, NT, 8], c=own)
            topi = sb("topi", [P, NT, 8], U32, own)
            topf = sb("topf", [P, NT, 8], c=own)
            iota = sb("iota", [P, NT * TOPK, NE], c=own)
            hit = sb("hit", [P, NT * TOPK, NE], c=own)
            chosen = sb("chosen", [P, NT, NE], c=own)
            cw = sb("cw", [P, NT, NW], c=own)
            cwr = sb("cwr", [P, NT, NW], c=own)
            csum = sb("csum", [P, NT], c=own)
            cinv = sb("cinv", [P, NT], c=own)
            cwb = sb("cwb", [P, NT, P], BF16, own)
            cwt = sb("cwt", [P, T], BF16, own)
        own = ExitStack()
        with own:
            wb = sb("wb", [P, NC, 3 * P], c=own)
            wb_hi = sb("wb_hi", [P, NC, 3 * P], F32R, own)
            wb_lo = sb("wb_lo", [P, NC, 3 * P], F32R, own)
            wvb = yt[:, 0:NC, :]
            vb = sb("vb", [P, NT, NG * DB], c=own)
            rr = sb("rr", [P, 2, HALF], c=own)
            qh = sb("qh", [P, 2, QPG, T], F32R, own)
            kh = sb("kh", [P, 2, 2, T], F32R, own)
            wvb_hi = qh[:, 1, 0, :].rearrange("p (c n) -> p c n", c=NC)
            wvb_lo = qh[:, 1, 1, :].rearrange("p (c n) -> p c n", c=NC)
            pb = yt[:, :, :].rearrange("p (k a) n -> p k (a n)", k=2)
            ptb = sb("ptb", [P, 2, HALF], c=own)
            nmb = sb("nmb", [P, 4], c=own)
            rsb = sb("rsb", [P, 2, NT], c=own)
            rib = sb("rib", [P, 2, NT], c=own)
            on = z[:, :, :].rearrange("p t (k a d) -> p k t a d", k=2, a=2)
            maskb = sb("maskb", [P, P], BF16, own)

        block = ctx.enter_context(nc.Block())

        STAGES = ["a", "f", "b", "g"][:upto]


        @block.sync
        def _(sp):
            sp.dma_start(x[:, :, :], d["x"].rearrange("t p d -> p t d")).then_inc(sem("x_loaded"), 16)
            sp.dma_start(idf[:, :], d["idf"]).then_inc(sem("ident_loaded"), 16)
            sp.dma_start(idb[:, :], d["idb"]).then_inc(sem("ident_loaded"), 16)
            sp.dma_start(norm_w[:, :], d["norm_w"]).then_inc(sem("a_consts"), 16)
            sp.dma_start(la[:, :, :], d["la"]).then_inc(sem("a_consts"), 16)
            sp.dma_start(maska[:, :, :], d["maska"]).then_inc(sem("a_consts"), 16)
            sp.dma_start(rope[:, :, :], d["rope_a"]).then_inc(sem("a_consts"), 16)

            def load_head(h, u, guard):
                if guard:
                    sp.wait_ge(sem("a_weff"), h - 1)
                    sp.wait_ge(sem("a_lora"), h - 1)
                sp.dma_start(wa[:, u, :, :, :], d["wa"][h]).then_inc(sem(f"wa_loaded{u}"), 16)
                sp.dma_start(lb[:, u, :], d["lb"][h]).then_inc(sem(f"wa_loaded{u}"), 16)

            load_head(0, 0, False)
            load_head(1, 1, False)
            with sp.Fori(1, HA // 2) as i:
                for u in range(2):
                    load_head(2 * i + u, u, True)

            def out_proj(s, w, lora):
                sp.wait_ge(sem(f"{s}_ot"), OT_ALL[s])
                if lora:
                    sp.dma_start(ob[:, :], d["ob"]).then_inc(sem(f"{s}_ob_loaded"), 16)

                def load(h, u, guard):
                    if guard:
                        sp.wait_ge(sem(f"{s}_woe"), h - 1)
                    sp.dma_start(wo[:, u, :], d[w][h]).then_inc(sem(f"{s}_wo_loaded{u}"), 16)
                    if lora:
                        sp.dma_start(oa[:, u, :], d["oa"][h]).then_inc(sem(f"{s}_wo_loaded{u}"), 16)

                load(0, 0, False)
                load(1, 1, False)
                with sp.Fori(1, HA // 2) as i:
                    for u in range(2):
                        load(2 * i + u, u, True)

            def ffn(s, before):
                sp.wait_ge(sem(f"{before}_yt"), since(before, "yt") + 4)
                sp.dma_start(wg[:, :, :], d["wg"]).then_inc(sem(f"{s}_consts"), 16)
                sp.dma_start(sel[:, :], d["sel"]).then_inc(sem(f"{s}_consts"), 16)
                sp.dma_start(iota[:, :, :], d["iota"]).then_inc(sem(f"{s}_consts"), 16)

                def load(j, u, guard):
                    if guard:
                        sp.wait_ge(sem(f"{s}_w_hi"), since(s, "w_hi") + j - 1)
                        sp.wait_ge(sem(f"{s}_w_lo"), since(s, "w_lo") + j - 1)
                    sp.dma_start(wf[:, u, :], d["wf"][j]).then_inc(sem(f"{s}_wf_loaded{u}"), 16)

                load(0, 0, False)
                load(1, 1, False)
                with sp.Fori(1, NJ // 2) as i:
                    for u in range(2):
                        load(2 * i + u, u, True)
                load(NJ - 1, 0, True)

            out_proj("a", "wo_a", True)
            if "f" in STAGES:
                ffn("f", "a")
            if "b" in STAGES:
                sp.wait_ge(sem("f_added"), NT // 2)
                sp.dma_start(rope[:, :, :], d["rope_b"]).then_inc(sem("b_consts"), 16)
                sp.dma_start(wvb[:, :, :], d["wvb"]).then_inc(sem("b_consts"), 16)
                sp.dma_start(maskb[:, :], d["maskb"]).then_inc(sem("b_consts"), 16)

                def load_group(g, gp, guard):
                    if guard:
                        sp.wait_ge(sem("b_w_hi"), g)
                        sp.wait_ge(sem("b_w_lo"), g)
                    sp.dma_start(wb[:, :, :], d["wb"][g]).then_inc(sem("wb_loaded"), 16)

                load_group(0, 0, False)
                load_group(1, 1, True)
                with sp.Fori(1, NG // 2) as i:
                    for gp in range(2):
                        load_group(2 * i + gp, gp, True)
                out_proj("b", "wo_b", False)
            if "g" in STAGES:
                ffn("g", "b")
            sp.wait_ge(sem(f"{STAGES[-1]}_added"), since(STAGES[-1], "added") + NT // 2)
            sp.dma_start(out.rearrange("t p d -> p t d"), x[:, :, :]).then_inc(sem("stored"), 16)
            sp.wait_ge(sem("stored"), 16)

        @block.vector
        def _(dve):
            v = nc.vector
            v.memset(xt_hi[:, :, 0:PAD].bitcast(F32), 0.0)
            v.memset(xt_hi[:, :, PAD + T:TP].bitcast(F32), 0.0)
            v.memset(xt_lo[:, :, 0:PAD].bitcast(F32), 0.0)
            v.memset(xt_lo[:, :, PAD + T:TP].bitcast(F32), 0.0)
            v.memset(kr[:, :, 0:PAD], 0.0)
            v.memset(pa[:, :, KW:2 * P], 0.0)
            v.memset(negh[:, :], -0.5).then_inc(sem("padded"), 1)

            def norm(s, before):
                me = sem(f"{s}_ln")
                if before is None:
                    dve.wait_ge(sem("x_loaded"), 16)
                for t in range(NT):
                    if before is not None and t % 2 == 0:
                        dve.wait_ge(sem(f"{before}_added"), since(before, "added") + t // 2 + 1)
                    v.bn_stats(stats[:, t, :], x[:, t, :]).then_inc(me, 1)
                for t in range(NT):
                    dve.wait_ge(me, since(s, "ln") + t + 1)
                    v.bn_aggr(mv[:, t, :], stats[:, t, :]).then_inc(me, 1)
                dve.wait_ge(me, since(s, "ln") + 2 * NT)
                v.tensor_scalar(var[:, 0, :], mv[:, :, 1], LN_EPS, None, ALU.add).then_inc(sem(f"{s}_var"), 1)
                dve.wait_ge(sem(f"{s}_rstd"), since(s, "rstd") + 1)
                if s != "a":
                    for t in range(NT):
                        v.tensor_scalar(z[:, t, :], x[:, t, :], mv[:, t, 0:1], rstd[:, 0, t:t + 1],
                                        ALU.subtract, ALU.mult).then_inc(sem(f"{s}_z"), 1)
                    for q in range(2 * NC):
                        dve.wait_ge(sem(f"{s}_xt_hi"), since(s, "xt_hi") + q + 1)
                        at = slice(PAD + HALF * (q % 2), PAD + HALF * (q % 2) + HALF)
                        v.tensor_tensor(xt_lo[:, q // 2, at], ps[:, q, :], xt_hi[:, q // 2, at].bitcast(F32),
                                        ALU.subtract).then_inc(sem(f"{s}_xt_lo"), 1)
                    return
                for t in range(NT):
                    v.tensor_scalar(z[:, t, :], x[:, t, :], mv[:, t, 0:1], rstd[:, 0, t:t + 1],
                                    ALU.subtract, ALU.mult).then_inc(sem("a_zz"), 1)
                dve.wait_ge(sem("padded"), 1)
                for t in range(NT):
                    dve.wait_ge(sem("a_zz"), t + 1)
                    v.tensor_tensor_reduce(out=yt[:, t % 4, 0:D], in0=z[:, t, :], in1=z[:, t, :], scale=1.0 / D,
                                           scalar=0.0, op0=ALU.mult, op1=ALU.add,
                                           accum_out=rsum[:, t:t + 1]).then_inc(sem("a_sq"), 1)
                    dve.wait_ge(sem("a_sq"), t + 1)
                v.tensor_scalar(var[:, 1, :], rsum[:, :], RMS_EPS, None, ALU.add).then_inc(sem("a_var2"), 1)
                for t in range(NT):
                    v.tensor_tensor(x[:, t, :], x[:, t, :], z[:, t, :], ALU.add).then_inc(sem("a_xz"), 1)
                dve.wait_ge(sem("a_rstd2"), 1)
                dve.wait_ge(sem("a_xz"), NT)
                for t in range(NT):
                    v.tensor_scalar(z[:, t, :], z[:, t, :], rstd[:, 1, t:t + 1], None,
                                    ALU.mult).then_inc(sem("a_z"), 1)
                dve.wait_ge(sem("a_consts"), 64)
                for q in range(2 * NC):
                    dve.wait_ge(sem("a_zt"), q + 1)
                    v.tensor_scalar(zt[:, q, :], ps[:, q, :], norm_w[:, q // 2:q // 2 + 1], None,
                                    ALU.mult).then_inc(sem("a_ztw"), 1)
                for q in range(2 * NC):
                    dve.wait_ge(sem("a_xt_hi"), q + 1)
                    at = slice(PAD + HALF * (q % 2), PAD + HALF * (q % 2) + HALF)
                    v.tensor_tensor(xt_lo[:, q // 2, at], zt[:, q, :], xt_hi[:, q // 2, at].bitcast(F32),
                                    ALU.subtract).then_inc(sem("a_xt_lo"), 1)

            def residual(s):
                for n in range(NT // 2):
                    dve.wait_ge(sem(f"{s}_y_turned"), since(s, "y_turned") + n + 1)
                    v.tensor_tensor(x[:, 2 * n:2 * n + 2, :], x[:, 2 * n:2 * n + 2, :],
                                    ps[:, n, :].rearrange("p (t d) -> p t d", t=2),
                                    ALU.add).then_inc(sem(f"{s}_added"), 1)

            def rope_piece(bank, r, half, swaps):
                at = slice(HALF * half, HALF * half + HALF)
                v.tensor_tensor(ra[:, r, :], ps[:, bank, :], rope[:, 0, at], ALU.mult)
                for src, dst, n in swaps:
                    last = v.tensor_tensor(rb[dst:dst + n, r, :], ps[src:src + n, bank, :],
                                           rope[src:src + n, 1, at], ALU.mult)
                return last

            norm("a", None)

            def weff(h, u):
                dve.wait_ge(sem("a_lora"), h + 1)
                dve.wait_ge(sem(f"wa_loaded{u}"), loads(h, u, 32))
                dve.wait_ge(sem("a_w_hi"), h)
                dve.wait_ge(sem("a_w_lo"), h)
                for c in range(NC):
                    last = v.scalar_tensor_tensor(out=wef[:, u, c, :, :].rearrange("p m d -> p (m d)"),
                                                  in0=ps[:, c, 0:3 * P], scalar=LORA_SCALE,
                                                  in1=wa[:, u, c, :, :].rearrange("p m d -> p (m d)"),
                                                  op0=ALU.mult, op1=ALU.add)
                last.then_inc(sem("a_weff"), 1)

            def rope_a(h, piece):
                dve.wait_ge(sem("a_qk"), 4 * h + piece + 1)
                if piece < 2:
                    dve.wait_ge(sem("a_rot"), 4 * h)
                else:
                    dve.wait_ge(sem("a_rot"), 4 * h + piece - 1)
                rope_piece(piece % 2, piece % 2, piece % 2,
                           [(64, 0, 64), (0, 64, 64)]).then_inc(sem("a_mul"), 1)

            def row_max(h, u, n):
                dve.wait_ge(sem("a_scores"), 4 * h + n + 1)
                dve.wait_ge(sem("a_exp"), 4 * h)
                bank = 2 + (n + 2 * u) % 4
                v.tensor_reduce(nmax[:, 2 * n:2 * n + 2], ps[:, bank, 0:2 * KW].rearrange("p (t k) -> p t k", t=2),
                                AX.X, ALU.max, negate=True).then_inc(sem("a_max"), 1)

            def row_inv(h, n):
                dve.wait_ge(sem("a_exp"), 4 * h + n + 1)
                dve.wait_ge(sem("a_pn"), 4 * h)
                v.reciprocal(rinv[:, 2 * n:2 * n + 2], rsum[:, 2 * n:2 * n + 2]).then_inc(sem("a_inv"), 1)

            def head_a(h, u, ahead1, ahead2):
                for n in range(4):
                    row_max(h, u, n)
                if ahead1:
                    rope_a(h + 1, 0)
                row_inv(h, 0)
                row_inv(h, 1)
                if ahead1:
                    rope_a(h + 1, 1)
                row_inv(h, 2)
                row_inv(h, 3)
                if ahead1:
                    rope_a(h + 1, 2)
                    rope_a(h + 1, 3)
                if ahead2:
                    weff(h + 2, u)

            dve.wait_ge(sem("a_consts"), 64)
            weff(0, 0)
            weff(1, 1)
            for piece in range(4):
                rope_a(0, piece)
            with dve.Fori(0, HA // 2 - 1) as i:
                for u in range(2):
                    head_a(2 * i + u, u, True, True)
            head_a(HA - 2, 0, True, False)
            head_a(HA - 1, 1, False, False)

            def out_proj(s, lora):
                def step(h, u):
                    if lora:
                        dve.wait_ge(sem(f"{s}_ol"), h + 1)
                    dve.wait_ge(sem(f"{s}_wo_loaded{u}"), loads(h, u, 32 if lora else 16))
                    dve.wait_ge(sem(f"{s}_wo_hi"), h)
                    dve.wait_ge(sem(f"{s}_wo_lo"), h)
                    if lora:
                        v.scalar_tensor_tensor(out=woe[:, u, :], in0=ps[:, u, 0:D], scalar=LORA_SCALE,
                                               in1=wo[:, u, :], op0=ALU.mult,
                                               op1=ALU.add).then_inc(sem(f"{s}_woe"), 1)
                    else:
                        v.tensor_copy(woe[:, u, :], wo[:, u, :]).then_inc(sem(f"{s}_woe"), 1)
                    dve.wait_ge(sem(f"{s}_ot_hi"), h + 1)
                    v.tensor_tensor(ot_lo[:, u, :], ot[:, h, :], ot_hi[:, u, :].bitcast(F32),
                                    ALU.subtract).then_inc(sem(f"{s}_ot_lo"), 1)

                with dve.Fori(0, HA // 2) as i:
                    for u in range(2):
                        step(2 * i + u, u)

            dve.wait_ge(sem("a_ot"), 2 * HA)
            out_proj("a", True)
            residual("a")

            def router(s):
                me = sem(f"{s}_route")
                n = 0

                def link(ins):
                    nonlocal n
                    n += 1
                    ins.then_inc(me, 1)
                    dve.wait_ge(me, since(s, "route") + n)

                dve.wait_ge(sem(f"{s}_consts"), since(s, "consts") + 48)
                dve.wait_ge(sem(f"{s}_wg_hi"), since(s, "wg_hi") + 1)
                v.tensor_tensor(wg_lo[:, :, :], wg[:, :, :], wg_hi[:, :, :].bitcast(F32),
                                ALU.subtract).then_inc(sem(f"{s}_wg_lo"), 1)
                v.memset(cwb[:, :, :], 0.0)
                v.memset(cw[:, :, :], 1.0)
                dve.wait_ge(sem(f"{s}_logits"), since(s, "logits") + 1)
                link(v.tensor_copy(lg[:, :, :], ps[:, 3, 0:NT * NE].rearrange("p (t e) -> p t e", e=NE)))
                for t in range(NT):
                    ins = v.max(top[:, t, :], lg[:, t, :])
                link(ins)
                for t in range(NT):
                    ins = v.max_index(topi[:, t, :], top[:, t, :], lg[:, t, :])
                link(ins)
                link(v.tensor_copy(topf[:, :, :], topi[:, :, :]))
                link(v.tensor_tensor(hit[:, :, :].rearrange("p (t k) e -> p t k e", t=NT),
                                     iota[:, :, :].rearrange("p (t k) e -> p t k e", t=NT),
                                     topf[:, :, 0:TOPK].unsqueeze(3).broadcast_to([P, NT, TOPK, NE]),
                                     ALU.is_equal))
                link(v.tensor_reduce(chosen[:, :, :], hit[:, :, :].rearrange("p (t k) e -> p t e k", t=NT),
                                     AX.X, ALU.add))
                v.tensor_tensor(lg[:, :, :], lg[:, :, :], top[:, :, 0:1].broadcast_to([P, NT, NE]),
                                ALU.subtract).then_inc(sem(f"{s}_shifted"), 1)
                dve.wait_ge(sem(f"{s}_ex"), since(s, "ex") + 1)
                link(v.tensor_tensor(ex[:, :, :], ex[:, :, :], chosen[:, :, :], ALU.mult))
                link(v.tensor_reduce(csum[:, :], ex[:, :, :], AX.X, ALU.add))
                link(v.reciprocal(cinv[:, :], csum[:, :]))
                link(v.tensor_tensor(cw[:, :, 0:NE], ex[:, :, :],
                                     cinv[:, :].unsqueeze(2).broadcast_to([P, NT, NE]), ALU.mult))
                for part in range(3):
                    at = slice(NW * part, NW * part + NW)
                    src = cw if part == 0 else cwr
                    link(v.tensor_copy(cwb[:, :, at], src[:, :, :]))
                    if part < 2:
                        link(v.tensor_tensor(cwr[:, :, :], src[:, :, :], cwb[:, :, at], ALU.subtract))
                ins = v.tensor_copy(top[:, 0, 0:1], cinv[:, 0:1])
                ins.then_inc(sem(f"{s}_cwb"), 1)
                dve.wait_ge(sem(f"{s}_cwt_turned"), since(s, "cwt_turned") + 1)
                v.tensor_copy(cwt[:, :], ps[:, 3, :].bitcast(BF16)[:, 0:T]).then_inc(sem(f"{s}_cwt"), 1)

            def ffn(s):
                def tile(j, u):
                    for half in range(2):
                        k = 2 * j + half
                        b = half
                        dve.wait_ge(sem(f"{s}_silu"), since(s, "silu") + k + 1)
                        dve.wait_ge(sem(f"{s}_u"), since(s, "u") + k + 1)
                        v.tensor_tensor(gu[:, b, :], ps[:, 1, :], sg[:, b, :], ALU.mult).then_inc(sem(f"{s}_gu"), 1)
                        dve.wait_ge(sem(f"{s}_gu"), since(s, "gu") + k + 1)
                        dve.wait_ge(sem(f"{s}_c"), since(s, "c") + k + 1)
                        dve.wait_ge(sem(f"{s}_h_hi"), since(s, "h_hi") + k)
                        dve.wait_ge(sem(f"{s}_h_lo"), since(s, "h_lo") + k)
                        v.tensor_tensor(hf[:, b, :], ps[:, 2, :], gu[:, b, :], ALU.mult).then_inc(sem(f"{s}_h"), 1)
                        dve.wait_ge(sem(f"{s}_h_hi"), since(s, "h_hi") + k + 1)
                        dve.wait_ge(sem(f"{s}_down"), since(s, "down") + k)
                        v.tensor_tensor(h_lo[:, b, :], hf[:, b, :], h_hi[:, b, :].bitcast(F32),
                                        ALU.subtract).then_inc(sem(f"{s}_h_lo"), 1)

                with dve.Fori(0, NJ // 2) as i:
                    for u in range(2):
                        tile(2 * i + u, u)
                tile(NJ - 1, 0)

            if "f" in STAGES:
                norm("f", "a")
                router("f")
                ffn("f")
                residual("f")

            if "b" in STAGES:
                norm("b", "f")
                dve.wait_ge(sem("b_consts"), 48)
                dve.wait_ge(sem("b_wv_hi"), 1)
                v.tensor_tensor(wvb_lo[:, :, :], wvb[:, :, :], wvb_hi[:, :, :].bitcast(F32),
                                ALU.subtract).then_inc(sem("b_wv_lo"), 1)

                def rope_b(g, gp, piece):
                    dve.wait_ge(sem("b_proj"), 6 * g + piece + 1)
                    if piece < 2:
                        dve.wait_ge(sem("b_rot"), 6 * g)
                    else:
                        dve.wait_ge(sem("b_rot"), 6 * g + piece - 1)
                    rope_piece(7, piece % 2, piece % 2,
                               [(32, 0, 32), (0, 32, 32), (96, 64, 32), (64, 96, 32)]).then_inc(sem("b_mul"), 1)

                def low_b(g, gp, piece):
                    dve.wait_ge(sem("b_hi"), 6 * g + piece + 1)
                    at = slice(HALF * (piece % 2), HALF * (piece % 2) + HALF)
                    r = piece % 2
                    if piece < 2:
                        ins = v.tensor_tensor(kh[:, gp, 1, at], rr[:, r, :], kh[:, gp, 0, at].bitcast(F32),
                                              ALU.subtract)
                    else:
                        h = 2 * (piece // 2 - 1)
                        v.tensor_tensor(qh[64:128, gp, h, at], rr[0:64, r, :], qh[0:64, gp, h, at].bitcast(F32),
                                        ALU.subtract)
                        ins = v.tensor_tensor(qh[0:64, gp, h + 1, at], rr[64:128, r, :],
                                              qh[64:128, gp, h + 1, at].bitcast(F32), ALU.subtract)
                    ins.then_inc(sem("b_lo"), 1)

                def row_max_b(g, local):
                    k = 32 * g + local
                    t = local % NT
                    dve.wait_ge(sem("b_scores"), k + 1)
                    b = 2 * (local % 2)
                    v.tensor_reduce(nmb[:, local % 4:local % 4 + 1],
                                    ps[:, b:b + 2, :].rearrange("p b k -> p (b k)")[:, 0:P * (t + 1)],
                                    AX.X, ALU.max, negate=True).then_inc(sem("b_max"), 1)

                def head_norm(g, hh):
                    h = QPG * g + hh
                    dve.wait_ge(sem("b_exp"), NT * (h + 1))
                    v.reciprocal(rib[:, hh % 2, :], rsb[:, hh % 2, :]).then_inc(sem("b_inv"), 1)
                    dve.wait_ge(sem("b_inv"), h + 1)
                    dve.wait_ge(sem("b_prod"), CHB * (h + 1))
                    dve.wait_ge(sem("b_on_turned"), 4 * g if hh < 2 else 4 * g + 2)
                    v.tensor_tensor(on[:, hh // 2, :, hh % 2, :], ps[:, 6, :].rearrange("p (t d) -> p t d", t=NT),
                                    rib[:, hh % 2, :].unsqueeze(2).broadcast_to([P, NT, DB]),
                                    ALU.mult).then_inc(sem("b_on"), 1)

                def group(g, gp, ahead):
                    for local in range(QPG * NT):
                        if local + 2 < QPG * NT:
                            row_max_b(g, local + 2)
                        elif ahead:
                            row_max_b(g + 1, local + 2 - QPG * NT)
                        if ahead and local in PROJ_AT:
                            rope_b(g + 1, 1 - gp, PROJ_AT.index(local))
                        if ahead and local - 1 in PROJ_AT:
                            low_b(g + 1, 1 - gp, PROJ_AT.index(local - 1))
                        if local % NT == NT - 1:
                            head_norm(g, local // NT)

                for piece in range(6):
                    rope_b(0, 0, piece)
                    low_b(0, 0, piece)
                row_max_b(0, 0)
                row_max_b(0, 1)
                with dve.Fori(0, NG // 2 - 1) as i:
                    for gp in range(2):
                        group(2 * i + gp, gp, True)
                group(NG - 2, 0, True)
                group(NG - 1, 1, False)
                dve.wait_ge(sem("b_ot"), 4 * NG)
                out_proj("b", False)
                residual("b")
            if "g" in STAGES:
                norm("g", "b")
                router("g")
                ffn("g")
                residual("g")

        @block.gpsimd
        def _(pool):
            g_ = nc.gpsimd

            def root(s, k=0):
                if k == 0:
                    pool.wait_ge(sem(f"{s}_var"), since(s, "var") + 1)
                else:
                    pool.wait_ge(sem("a_var2"), 1)
                g_.tensor_tensor(rstd[:, k, :], var[:, k, :], negh[:, :],
                                 ALU.pow).then_inc(sem(f"{s}_rstd" if k == 0 else "a_rstd2"), 1)

            pool.wait_ge(sem("padded"), 1)
            root("a")
            root("a", 1)

            def w_lo(h, u):
                pool.wait_ge(sem("a_w_hi"), h + 1)
                pool.wait_ge(sem("a_qk"), 4 * h - 4 if not isinstance(h, int) or h else 0)
                g_.tensor_tensor(wqk_lo[:, u, :, :, :], wef[:, u, :, 0:2, :], wqk_hi[:, u, :, :, :].bitcast(F32),
                                 ALU.subtract)
                g_.tensor_tensor(wv_lo[:, :, u, :], wef[:, u, :, 2, :], wv_hi[:, :, u, :].bitcast(F32),
                                 ALU.subtract).then_inc(sem("a_w_lo"), 1)

            def rot(h, u, piece):
                pool.wait_ge(sem("a_mul"), 4 * h + piece + 1)
                at = HALF * (piece % 2)
                dst = qr[:, u, at:at + HALF] if piece < 2 else kr[:, u, PAD + at:PAD + at + HALF]
                g_.tensor_tensor(dst, ra[:, piece % 2, :], rb[:, piece % 2, :], ALU.add).then_inc(sem("a_rot"), 1)

            def p_norm(h, n):
                pool.wait_ge(sem("a_inv"), 4 * h + n + 1)
                two = slice(2 * n, 2 * n + 2)
                g_.tensor_tensor(pa[:, two, 0:KW], pa[:, two, 0:KW],
                                 rinv[:, two].unsqueeze(2).broadcast_to([P, 2, KW]),
                                 ALU.mult).then_inc(sem("a_pn"), 1)

            def head_a(h, u, ahead1, ahead2):
                if ahead1:
                    pool.wait_ge(sem("a_scores"), 4 * h)
                    rot(h + 1, 1 - u, 0)
                p_norm(h, 0)
                p_norm(h, 1)
                if ahead1:
                    rot(h + 1, 1 - u, 1)
                p_norm(h, 2)
                p_norm(h, 3)
                if ahead1:
                    rot(h + 1, 1 - u, 2)
                    rot(h + 1, 1 - u, 3)
                if ahead2:
                    w_lo(h + 2, u)

            w_lo(0, 0)
            w_lo(1, 1)
            for piece in range(4):
                rot(0, 0, piece)
            with pool.Fori(0, HA // 2 - 1) as i:
                for u in range(2):
                    head_a(2 * i + u, u, True, True)
            head_a(HA - 2, 0, True, False)
            head_a(HA - 1, 1, False, False)

            def out_proj(s):
                def step(h, u):
                    pool.wait_ge(sem(f"{s}_wo_hi"), h + 1)
                    g_.tensor_tensor(wo_lo[:, u, :], woe[:, u, :], wo_hi[:, u, :].bitcast(F32),
                                     ALU.subtract).then_inc(sem(f"{s}_wo_lo"), 1)

                with pool.Fori(0, HA // 2) as i:
                    for u in range(2):
                        step(2 * i + u, u)

            def ffn(s):
                root(s)

                def tile(j, u, first):
                    pool.wait_ge(sem(f"{s}_w_hi"), since(s, "w_hi") + j + 1)
                    g_.tensor_tensor(wf_lo[:, u, :], wf[:, u, :], wf_hi[:, u, :].bitcast(F32),
                                     ALU.subtract).then_inc(sem(f"{s}_w_lo"), 1)

                with pool.Fori(0, NJ // 2) as i:
                    for u in range(2):
                        tile(2 * i + u, u, False)
                tile(NJ - 1, 0, False)

            out_proj("a")
            if "f" in STAGES:
                ffn("f")
            if "b" in STAGES:
                root("b")

                def w_lo_b(g, gp):
                    pool.wait_ge(sem("b_w_hi"), g + 1)
                    g_.tensor_tensor(wb_lo[:, :, :], wb[:, :, :], wb_hi[:, :, :].bitcast(F32),
                                     ALU.subtract).then_inc(sem("b_w_lo"), 1)

                def rot_b(g, piece):
                    pool.wait_ge(sem("b_mul"), 6 * g + piece + 1)
                    if piece < 2:
                        pool.wait_ge(sem("b_lo"), 6 * g)
                    else:
                        pool.wait_ge(sem("b_lo"), 6 * g + piece - 1)
                    r = piece % 2
                    g_.tensor_tensor(rr[:, r, :], ra[:, r, :], rb[:, r, :], ALU.add).then_inc(sem("b_rot"), 1)

                w_lo_b(0, 0)
                for piece in range(6):
                    rot_b(0, piece)
                w_lo_b(1, 1)

                def group(g, gp, ahead1, ahead2):
                    if ahead1:
                        for piece in range(6):
                            rot_b(g + 1, piece)
                    if ahead2:
                        w_lo_b(g + 2, gp)

                with pool.Fori(0, NG // 2 - 1) as i:
                    for gp in range(2):
                        group(2 * i + gp, gp, True, True)
                group(NG - 2, 0, True, False)
                out_proj("b")
            if "g" in STAGES:
                ffn("g")

        @block.scalar
        def _(act):
            s_ = nc.scalar

            def norm(s):
                for q in range(2 * NC):
                    at = slice(PAD + HALF * (q % 2), PAD + HALF * (q % 2) + HALF)
                    if s == "a":
                        act.wait_ge(sem("a_ztw"), q + 1)
                        src = zt[:, q, :]
                    else:
                        act.wait_ge(sem(f"{s}_zt"), since(s, "zt") + q + 1)
                        src = ps[:, q, :]
                    s_.copy(xt_hi[:, q // 2, at], src).then_inc(sem(f"{s}_xt_hi"), 1)

            def y_out(s, acc, n):
                act.wait_ge(acc, n)
                for q in range(4):
                    s_.copy(yt[:, q, :], ps[:, 4 + q, :]).then_inc(sem(f"{s}_yt"), 1)

            norm("a")

            def w_hi(h, u):
                act.wait_ge(sem("a_weff"), h + 1)
                s_.copy(wqk_hi[:, u, :, :, :], wef[:, u, :, 0:2, :])
                s_.copy(wv_hi[:, :, u, :], wef[:, u, :, 2, :]).then_inc(sem("a_w_hi"), 1)

            def v_out(i, piece):
                act.wait_ge(sem("a_v"), 5 * i + piece + 1)
                act.wait_ge(sem("a_pv"), 8 * i)
                n = 2 if piece < 4 else 1
                s_.copy(va[:, 2 * piece:2 * piece + n, :, :].rearrange("p t u d -> p (t u d)"),
                        ps[:, piece % 2, 0:n * 2 * P]).then_inc(sem("a_vout"), 1)

            def exps(h, u, n):
                act.wait_ge(sem("a_max"), 4 * h + n + 1)
                act.wait_ge(sem("a_turned"), 4 * h)
                bank = 2 + (n + 2 * u) % 4
                for m in range(2):
                    t = 2 * n + m
                    last = s_.activation(pa[:, t, 0:KW], ps[:, bank, KW * m:KW * m + KW], ACT.Exp,
                                         bias=nmax[:, t:t + 1], accum_out=rsum[:, t:t + 1])
                last.then_inc(sem("a_exp"), 1)

            def head_a(i, h, u, ahead1, ahead2):
                for n in range(4):
                    exps(h, u, n)
                if ahead2:
                    w_hi(h + 2, u)
                for n in range(4):
                    act.wait_ge(sem("a_turned"), 4 * h + n + 1)
                    if n < 2:
                        act.wait_ge(sem("a_pv"), 4 * h)
                    else:
                        act.wait_ge(sem("a_pv"), 4 * h + n - 1)
                    s_.copy(pta[:, n % 2, :], ps[:, 6 + n % 2, :]).then_inc(sem("a_pt"), 1)
                    if n == 2:
                        o_out(h, u, 0)
                o_out(h, u, 1)
                if u == 1 and ahead2:
                    for piece in range(5):
                        v_out(i + 1, piece)

            def o_out(h, u, half):
                act.wait_ge(sem("a_pv"), 4 * h + 2 * half + 2)
                s_.copy(ot[:, h, HALF * half:HALF * half + HALF],
                        ps[:, 2 + 2 * u + half, :]).then_inc(sem("a_ot"), 1)

            w_hi(0, 0)
            w_hi(1, 1)
            for piece in range(5):
                v_out(0, piece)
            with act.Fori(0, HA // 2 - 1) as i:
                for u in range(2):
                    head_a(i, 2 * i + u, u, True, True)
            head_a(HA // 2 - 1, HA - 2, 0, True, False)
            head_a(HA // 2 - 1, HA - 1, 1, False, False)

            def out_proj(s):
                def step(h, u):
                    act.wait_ge(sem(f"{s}_oacc"), h - 1 if not isinstance(h, int) or h else 0)
                    s_.copy(ot_hi[:, u, :], ot[:, h, :]).then_inc(sem(f"{s}_ot_hi"), 1)
                    act.wait_ge(sem(f"{s}_woe"), h + 1)
                    s_.copy(wo_hi[:, u, :], woe[:, u, :]).then_inc(sem(f"{s}_wo_hi"), 1)

                step(0, 0)
                step(1, 1)
                with act.Fori(1, HA // 2) as i:
                    for u in range(2):
                        step(2 * i + u, u)

            out_proj("a")
            y_out("a", sem("a_oacc"), HA)

            def ffn(s):
                norm(s)
                act.wait_ge(sem(f"{s}_consts"), since(s, "consts") + 48)
                s_.copy(wg_hi[:, :, :], wg[:, :, :]).then_inc(sem(f"{s}_wg_hi"), 1)

                def w_hi_f(j, u):
                    act.wait_ge(sem(f"{s}_wf_loaded{u}"), since(s, f"wf_loaded{u}") + loads(j, u, 16))
                    act.wait_ge(sem(f"{s}_down"), since(s, "down") + (2 * j - 2 if not isinstance(j, int) or j else 0))
                    s_.copy(wf_hi[:, u, :], wf[:, u, :]).then_inc(sem(f"{s}_w_hi"), 1)

                w_hi_f(0, 0)
                act.wait_ge(sem(f"{s}_shifted"), since(s, "shifted") + 1)
                s_.activation(ex[:, :, :], lg[:, :, :], ACT.Exp).then_inc(sem(f"{s}_ex"), 1)

                def tile(j, u, more):
                    for half in range(2):
                        k = 2 * j + half
                        b = half
                        act.wait_ge(sem(f"{s}_g"), since(s, "g") + k + 1)
                        act.wait_ge(sem(f"{s}_gu"), since(s, "gu") + k)
                        s_.activation(sg[:, b, :], ps[:, 0, :], ACT.Silu).then_inc(sem(f"{s}_silu"), 1)
                        if half == 0 and more:
                            w_hi_f(j + 1, 1 - u)
                        act.wait_ge(sem(f"{s}_h"), since(s, "h") + k + 1)
                        act.wait_ge(sem(f"{s}_down"), since(s, "down") + k)
                        s_.copy(h_hi[:, b, :], hf[:, b, :]).then_inc(sem(f"{s}_h_hi"), 1)

                with act.Fori(0, NJ // 2) as i:
                    for u in range(2):
                        tile(2 * i + u, u, True)
                tile(NJ - 1, 0, False)
                y_out(s, sem(f"{s}_down"), since(s, "down") + 2 * NJ)

            if "f" in STAGES:
                ffn("f")
            if "b" in STAGES:
                norm("b")
                act.wait_ge(sem("b_consts"), 48)
                s_.copy(wvb_hi[:, :, :], wvb[:, :, :]).then_inc(sem("b_wv_hi"), 1)

                def w_hi_b(g, gp):
                    act.wait_ge(sem("wb_loaded"), 16 * (g + 1))
                    act.wait_ge(sem("b_proj"), 6 * g)
                    s_.copy(wb_hi[:, :, :], wb[:, :, :]).then_inc(sem("b_w_hi"), 1)

                def high_b(g, gp, piece):
                    act.wait_ge(sem("b_rot"), 6 * g + piece + 1)
                    at = slice(HALF * (piece % 2), HALF * (piece % 2) + HALF)
                    r = piece % 2
                    if piece < 2:
                        ins = s_.copy(kh[:, gp, 0, at], rr[:, r, :])
                    else:
                        h = 2 * (piece // 2 - 1)
                        s_.copy(qh[0:64, gp, h, at], rr[0:64, r, :])
                        ins = s_.copy(qh[64:128, gp, h + 1, at], rr[64:128, r, :])
                    ins.then_inc(sem("b_hi"), 1)

                def exp_b(g, local):
                    k = 32 * g + local
                    t = local % NT
                    act.wait_ge(sem("b_max"), k + 1)
                    act.wait_ge(sem("b_inv"), QPG * g + (local // NT) - 1 if local // NT > 0 else QPG * g)
                    b = 2 * (local % 2)
                    s_.activation(pb[:, local % 2, 0:P * (t + 1)],
                                  ps[:, b:b + 2, :].rearrange("p b k -> p (b k)")[:, 0:P * (t + 1)], ACT.Exp,
                                  bias=nmb[:, local % 4:local % 4 + 1],
                                  accum_out=rsb[:, (local // NT) % 2, t:t + 1]).then_inc(sem("b_exp"), 1)

                def pt_b(g, local):
                    for cc in chunks(local % NT):
                        c = CHB * (QPG * g + local // NT) + cc[0]
                        act.wait_ge(sem("b_turned"), c + 1)
                        if local // NT == 0 and cc[0] < 2:
                            act.wait_ge(sem("b_prod"), CHB * QPG * g)
                        else:
                            act.wait_ge(sem("b_prod"), c - 1)
                        s_.copy(ptb[:, cc[0] % 2, 0:P * cc[2]],
                                ps[:, 4 + cc[0] % 2, 0:P * cc[2]]).then_inc(sem("b_pt"), 1)

                def ot_b(g, pair, half):
                    act.wait_ge(sem("b_on_turned"), 4 * g + 2 * pair + half + 1)
                    s_.copy(ot[:, 2 * g + pair, HALF * half:HALF * half + HALF],
                            ps[:, 7, :]).then_inc(sem("b_ot"), 1)

                def group(g, gp, first, ahead1, ahead2):
                    for local in range(QPG * NT):
                        pt_b(g, local)
                        if local + 2 < QPG * NT:
                            exp_b(g, local + 2)
                        elif ahead1:
                            exp_b(g + 1, local + 2 - QPG * NT)
                        if not first and local in LATE_AT:
                            ot_b(g - 1, 1, LATE_AT.index(local))
                        if ahead1 and local in PROJ_AT:
                            high_b(g + 1, 1 - gp, PROJ_AT.index(local))
                        if local in EARLY_AT:
                            ot_b(g, 0, EARLY_AT.index(local))
                    if ahead2:
                        w_hi_b(g + 2, gp)

                w_hi_b(0, 0)
                for t in range(NT):
                    act.wait_ge(sem("b_v"), t + 1)
                    s_.copy(vb[:, t, :], ps[:, t % 4, :]).then_inc(sem("b_vout"), 1)
                for piece in range(6):
                    high_b(0, 0, piece)
                w_hi_b(1, 1)
                exp_b(0, 0)
                exp_b(0, 1)
                group(0, 0, True, True, True)
                group(1, 1, False, True, True)
                with act.Fori(1, NG // 2 - 1) as i:
                    for gp in range(2):
                        group(2 * i + gp, gp, False, True, True)
                group(NG - 2, 0, False, True, False)
                group(NG - 1, 1, False, False, False)
                ot_b(NG - 1, 1, 0)
                ot_b(NG - 1, 1, 1)
                out_proj("b")
                y_out("b", sem("b_oacc"), HA)
            if "g" in STAGES:
                ffn("g")

        @block.tensor
        def _(pe):
            t_ = nc.tensor

            def mm(o, l, r, start=True, stop=True):
                return t_.matmul(o, l, r, start=start, stop=stop)

            def norm(s):
                for q in range(2 * NC):
                    for m in range(4):
                        t = 4 * (q % 2) + m
                        pe.wait_ge(sem(f"{s}_z"), since(s, "z") + t + 1)
                        last = t_.transpose(ps[:, q, P * m:P * m + P], z[:, t, P * (q // 2):P * (q // 2) + P],
                                            idf[:, :])
                    last.then_inc(sem(f"{s}_zt"), 1)

            def turn_back(s):
                for n in range(NT // 2):
                    for m in range(2):
                        t = 2 * n + m
                        for c in range(NC):
                            pe.wait_ge(sem(f"{s}_yt"), since(s, "yt") + 2 * c + t // 4 + 1)
                            last = t_.transpose(ps[:, n, D * m + P * c:D * m + P * c + P],
                                                yt[:, 2 * c + t // 4, P * (t % 4):P * (t % 4) + P], idf[:, :])
                    last.then_inc(sem(f"{s}_y_turned"), 1)

            def three(o, lhs, rhs, first=True, last=True):
                terms = [(lhs(c, a), rhs(c, b)) for c in range(NC) for a, b in ((0, 0), (0, 1), (1, 0))]
                for n, (l, r) in enumerate(terms):
                    ins = mm(o, l, r, start=first and n == 0, stop=last and n == len(terms) - 1)
                return ins

            def xt(part, c, a, n):
                return (xt_hi, xt_lo)[part][:, c, PAD + a:PAD + a + n]

            pe.wait_ge(sem("ident_loaded"), 32)
            norm("a")
            pe.wait_ge(sem("a_consts"), 64)

            def lora(h, u, busy):
                pe.wait_ge(sem(f"wa_loaded{u}"), loads(h, u, 32))
                for wait in busy:
                    wait()
                for c in range(NC):
                    last = mm(ps[:, c, 0:3 * P], la[:, c, :], lb[:, u, :])
                last.then_inc(sem("a_lora"), 1)

            def qk(h, u, piece):
                w = piece // 2
                at = HALF * (piece % 2)
                three(ps[:, piece % 2, :],
                      lambda c, a: (wqk_hi, wqk_lo)[a][:, u, c, w, :],
                      lambda c, b: xt(b, c, at, HALF)).then_inc(sem("a_qk"), 1)

            def values(i, piece):
                for m in range(2 if piece < 4 else 1):
                    t = 2 * piece + m
                    last = three(ps[:, piece % 2, 2 * P * m:2 * P * m + 2 * P],
                                 lambda c, a: xt(a, c, P * t - PAD, P),
                                 lambda c, b: (wv_hi, wv_lo)[b][:, c, :, :].rearrange("p u d -> p (u d)"))
                last.then_inc(sem("a_v"), 1)

            def head_a(i, h, u, ahead1, ahead2):
                pe.wait_ge(sem("a_rot"), 4 * h + 4)
                pe.wait_ge(sem("a_exp"), 4 * h)
                for n in range(4):
                    if n == 2:
                        pe.wait_ge(sem("a_ot"), 2 * h)
                    bank = 2 + (n + 2 * u) % 4
                    for m in range(2):
                        t = 2 * n + m
                        o = ps[:, bank, KW * m:KW * m + KW]
                        mm(o, qr[:, u, P * t:P * t + P], kr[:, u, P * t:P * t + KW], True, False)
                        last = mm(o, idb[:, :], maska[:, 0 if t == 0 else 1, :], False, True)
                    last.then_inc(sem("a_scores"), 1)
                if ahead1:
                    pe.wait_ge(sem("a_w_lo"), h + 2)
                    if u == 0:
                        pe.wait_ge(sem("a_vout"), 5 * i + 5)
                    for piece in range(4):
                        if piece >= 2:
                            pe.wait_ge(sem("a_mul"), 4 * h + 4 + piece - 1)
                        qk(h + 1, 1 - u, piece)
                if ahead2:
                    lora(h + 2, u, [lambda: pe.wait_ge(sem("a_mul"), 4 * h + 8)])
                for n in range(5):
                    if n < 4:
                        pe.wait_ge(sem("a_pn"), 4 * h + n + 1)
                        if n < 2:
                            pe.wait_ge(sem("a_pt"), 4 * h)
                        else:
                            pe.wait_ge(sem("a_pt"), 4 * h + n - 1)
                        for m in range(4):
                            last = t_.transpose(ps[:, 6 + n % 2, P * m:P * m + P],
                                                pa[:, 2 * n + m // 2, P * (m % 2):P * (m % 2) + P], idf[:, :])
                        last.then_inc(sem("a_turned"), 1)
                    if n > 0:
                        n0 = n - 1
                        pe.wait_ge(sem("a_pt"), 4 * h + n0 + 1)
                        if n0 == 0:
                            pe.wait_ge(sem("a_vout"), 5 * i + 5)
                        for m in range(2):
                            t = 2 * n0 + m
                            o = ps[:, 2 + 2 * u + t // 4, P * (t % 4):P * (t % 4) + P]
                            for b in range(2):
                                last = mm(o, va[:, t + b, u, :], pta[:, n0 % 2, P * (2 * m + b):P * (2 * m + b) + P],
                                          b == 0, b == 1)
                        last.then_inc(sem("a_pv"), 1)
                if u == 1 and ahead2:
                    pe.wait_ge(sem("a_w_lo"), h + 3)
                    for piece in range(5):
                        if piece >= 2:
                            pe.wait_ge(sem("a_vout"), 5 * i + 5 + piece - 1)
                        values(i + 1, piece)

            for q in range(2 * NC):
                pe.wait_ge(sem("a_xt_lo"), q + 1)
            lora(0, 0, [])
            lora(1, 1, [lambda: pe.wait_ge(sem("a_weff"), 1)])
            pe.wait_ge(sem("a_w_lo"), 2)
            pe.wait_ge(sem("a_weff"), 2)
            for piece in range(5):
                if piece >= 2:
                    pe.wait_ge(sem("a_vout"), piece - 1)
                values(0, piece)
            pe.wait_ge(sem("a_vout"), 5)
            for piece in range(4):
                if piece >= 2:
                    pe.wait_ge(sem("a_mul"), piece - 1)
                qk(0, 0, piece)
            with pe.Fori(0, HA // 2 - 1) as i:
                for u in range(2):
                    head_a(i, 2 * i + u, u, True, True)
            head_a(HA // 2 - 1, HA - 2, 0, True, False)
            head_a(HA // 2 - 1, HA - 1, 1, False, False)

            def out_proj(s, has_lora):
                pe.wait_ge(sem(f"{s}_ot"), OT_ALL[s])
                if has_lora:
                    pe.wait_ge(sem(f"{s}_ob_loaded"), 16)

                def low_rank(h, u):
                    if has_lora:
                        pe.wait_ge(sem(f"{s}_wo_loaded{u}"), loads(h, u, 32))
                        pe.wait_ge(sem(f"{s}_woe"), h - 1 if not isinstance(h, int) or h else 0)
                        mm(ps[:, u, 0:D], oa[:, u, :], ob[:, :]).then_inc(sem(f"{s}_ol"), 1)

                def step(h, u, first, last):
                    pe.wait_ge(sem(f"{s}_wo_lo"), h + 1)
                    pe.wait_ge(sem(f"{s}_ot_lo"), h + 1)
                    for c in range(NC):
                        for half in range(2):
                            at = slice(HALF * half, HALF * half + HALF)
                            for n, (a, b) in enumerate(((0, 0), (0, 1), (1, 0))):
                                ins = mm(ps[:, 4 + 2 * c + half, :], (wo_hi, wo_lo)[a][:, u, P * c:P * c + P],
                                         (ot_hi, ot_lo)[b][:, u, at], first and n == 0, last and n == 2)
                    ins.then_inc(sem(f"{s}_oacc"), 1)

                low_rank(0, 0)
                low_rank(1, 1)
                step(0, 0, True, False)
                low_rank(2, 0)
                step(1, 1, False, False)
                low_rank(3, 1)
                with pe.Fori(1, HA // 2 - 1) as i:
                    for u in range(2):
                        step(2 * i + u, u, False, False)
                        low_rank(2 * i + u + 2, u)
                step(HA - 2, 0, False, False)
                step(HA - 1, 1, False, True)

            out_proj("a", True)
            turn_back("a")

            def ffn(s):
                norm(s)
                for q in range(2 * NC):
                    pe.wait_ge(sem(f"{s}_xt_lo"), since(s, "xt_lo") + q + 1)
                pe.wait_ge(sem(f"{s}_wg_lo"), since(s, "wg_lo") + 1)
                for t in range(NT):
                    last = three(ps[:, 3, NE * t:NE * t + NE],
                                 lambda c, a: xt(a, c, P * t, P),
                                 lambda c, b: (wg_hi, wg_lo)[b][:, c, :])
                last.then_inc(sem(f"{s}_logits"), 1)
                pe.wait_ge(sem(f"{s}_cwb"), since(s, "cwb") + 1)
                for t in range(NT):
                    last = t_.transpose(ps[:, 3, :].bitcast(BF16)[:, P * t:P * t + P], cwb[:, t, :], idb[:, :])
                last.then_inc(sem(f"{s}_cwt_turned"), 1)
                pe.wait_ge(sem(f"{s}_cwt"), since(s, "cwt") + 1)

                def up(j, u, half):
                    k = 2 * j + half
                    if half == 0:
                        pe.wait_ge(sem(f"{s}_w_lo"), since(s, "w_lo") + j + 1)
                    at = HALF * half
                    pe.wait_ge(sem(f"{s}_silu"), since(s, "silu") + k)
                    three(ps[:, 0, :], lambda c, a: (wf_hi, wf_lo)[a][:, u, P * c:P * c + P],
                          lambda c, b: xt(b, c, at, HALF)).then_inc(sem(f"{s}_g"), 1)
                    pe.wait_ge(sem(f"{s}_h"), since(s, "h") + k)
                    three(ps[:, 1, :], lambda c, a: (wf_hi, wf_lo)[a][:, u, D + P * c:D + P * c + P],
                          lambda c, b: xt(b, c, at, HALF)).then_inc(sem(f"{s}_u"), 1)
                    mm(ps[:, 2, :], sel[:, P * j:P * j + P] if isinstance(j, int) else sel[:, bass.ts(j, P)],
                       cwt[:, at:at + HALF]).then_inc(sem(f"{s}_c"), 1)

                def down(j, u, half, first, last):
                    k = 2 * j + half
                    pe.wait_ge(sem(f"{s}_h_lo"), since(s, "h_lo") + k + 1)
                    for c in range(NC):
                        for n, (a, b) in enumerate(((0, 0), (0, 1), (1, 0))):
                            ins = mm(ps[:, 4 + 2 * c + half, :],
                                     (wf_hi, wf_lo)[a][:, u, 2 * D + P * c:2 * D + P * c + P],
                                     (h_hi, h_lo)[b][:, half, :], first and n == 0, last and n == 2)
                    ins.then_inc(sem(f"{s}_down"), 1)

                up(0, 0, 0)
                up(0, 0, 1)
                down(0, 0, 0, True, False)
                up(1, 1, 0)
                down(0, 0, 1, True, False)
                up(1, 1, 1)
                down(1, 1, 0, False, False)
                with pe.Fori(1, NJ // 2) as i:
                    for u in range(2):
                        j = 2 * i + u
                        up(j, u, 0)
                        down(j - 1, 1 - u, 1, False, False)
                        up(j, u, 1)
                        down(j, u, 0, False, False)
                j = NJ - 1
                up(j, 0, 0)
                down(j - 1, 1, 1, False, False)
                up(j, 0, 1)
                down(j, 0, 0, False, True)
                down(j, 0, 1, False, True)
                turn_back(s)

            if "f" in STAGES:
                ffn("f")
            if "b" in STAGES:
                norm("b")
                for q in range(2 * NC):
                    pe.wait_ge(sem("b_xt_lo"), q + 1)
                pe.wait_ge(sem("b_wv_lo"), 1)
                for t in range(NT):
                    if t >= 4:
                        pe.wait_ge(sem("b_vout"), t - 3)
                    three(ps[:, t % 4, :], lambda c, a: xt(a, c, P * t, P),
                          lambda c, b: (wvb_hi, wvb_lo)[b][:, c, :]).then_inc(sem("b_v"), 1)
                pe.wait_ge(sem("b_vout"), NT)

                def proj(g, gp, piece):
                    if piece == 0:
                        pe.wait_ge(sem("b_w_lo"), g + 1)
                    at = HALF * (piece % 2)
                    col = (2 * P, 0, P)[piece // 2]
                    three(ps[:, 7, :], lambda c, a: (wb_hi, wb_lo)[a][:, c, col:col + P],
                          lambda c, b: xt(b, c, at, HALF)).then_inc(sem("b_proj"), 1)

                def scores(g, gp, local):
                    h, t = local // NT, local % NT
                    k = 32 * g + local
                    if local < 2:
                        pe.wait_ge(sem("b_exp"), 32 * g)
                        pe.wait_ge(sem("b_lo"), 6 * g + 6)
                    else:
                        pe.wait_ge(sem("b_exp"), k - 1)
                    for n0 in range(0, t + 1, 4):
                        w = min(4, t + 1 - n0) * P
                        o = ps[:, 2 * (local % 2) + n0 // 4, 0:w]
                        for b in range(2):
                            last_one = n0 + 4 > t and b == 1
                            ins = mm(o, qh[:, gp, h, P * t:P * t + P], kh[:, gp, b, P * n0:P * n0 + w],
                                     b == 0, b == 1 and not last_one)
                    ins = mm(ps[:, 2 * (local % 2) + t // 4, P * (t % 4):P * (t % 4) + P],
                             idb[:, :], maskb[:, :], False, True)
                    ins.then_inc(sem("b_scores"), 1)

                def turn(g, local):
                    h, t = local // NT, local % NT
                    k = 32 * g + local
                    pe.wait_ge(sem("b_exp"), k + 1)
                    for cc, n0, n in chunks(t):
                        c = CHB * (QPG * g + h) + cc
                        if h == 0 and cc < 2:
                            pe.wait_ge(sem("b_pt"), CHB * QPG * g)
                        else:
                            pe.wait_ge(sem("b_pt"), c - 1)
                        for m in range(n):
                            last = t_.transpose(ps[:, 4 + cc % 2, P * m:P * m + P],
                                                pb[:, local % 2, P * (n0 + m):P * (n0 + m) + P], idf[:, :])
                        last.then_inc(sem("b_turned"), 1)

                def products(g, local):
                    h, t = local // NT, local % NT
                    if t == 0:
                        pe.wait_ge(sem("b_on"), QPG * g + h)
                    for cc, n0, n in chunks(t):
                        c = CHB * (QPG * g + h) + cc
                        pe.wait_ge(sem("b_pt"), c + 1)
                        for m in range(n):
                            ins = mm(ps[:, 6, DB * t:DB * t + DB], ptb[:, cc % 2, P * m:P * m + P],
                                     vb[:, n0 + m, bass.ds(DB * g, DB)], n0 + m == 0, n0 + m == t)
                        ins.then_inc(sem("b_prod"), 1)

                def o_turn(g, pair, half, free):
                    pe.wait_ge(sem("b_on"), QPG * g + 2 * pair + 2)
                    free()
                    for m in range(4):
                        last = t_.transpose(ps[:, 7, P * m:P * m + P],
                                            on[:, pair, 4 * half + m, :, :].rearrange("p a d -> p (a d)"), idf[:, :])
                    last.then_inc(sem("b_on_turned"), 1)

                def group(g, gp, first, ahead):
                    for local in range(QPG * NT):
                        turn(g, local)
                        if local + 2 < QPG * NT:
                            scores(g, gp, local + 2)
                        elif ahead:
                            scores(g + 1, 1 - gp, local + 2 - QPG * NT)
                        products(g, local)
                        if local in LATE_AT and not first:
                            o_turn(g - 1, 1, LATE_AT.index(local), lambda: (
                                pe.wait_ge(sem("b_mul"), 6 * g + 6),
                                pe.wait_ge(sem("b_ot"), 4 * g - 2 + LATE_AT.index(local))))
                        if ahead and local in PROJ_AT:
                            piece = PROJ_AT.index(local)
                            pe.wait_ge(sem("b_mul"), 6 * (g + 1) + piece)
                            pe.wait_ge(sem("b_ot"), 4 * g + (2 if local > EARLY_AT[-1] else 0))
                            proj(g + 1, 1 - gp, piece)
                        if local in EARLY_AT:
                            n_proj = sum(q < local for q in PROJ_AT)
                            o_turn(g, 0, EARLY_AT.index(local), lambda: (
                                pe.wait_ge(sem("b_mul"), 6 * (g + 1) + (n_proj if ahead else 0)),
                                pe.wait_ge(sem("b_ot"), 4 * g + EARLY_AT.index(local))))

                for piece in range(6):
                    pe.wait_ge(sem("b_mul"), piece) if piece else None
                    proj(0, 0, piece)
                scores(0, 0, 0)
                scores(0, 0, 1)
                group(0, 0, True, True)
                group(1, 1, False, True)
                with pe.Fori(1, NG // 2 - 1) as i:
                    for gp in range(2):
                        group(2 * i + gp, gp, False, True)
                group(NG - 2, 0, False, True)
                group(NG - 1, 1, False, False)
                for half in range(2):
                    o_turn(NG - 1, 1, half, lambda: pe.wait_ge(sem("b_ot"), 4 * NG - 2 + half))
                out_proj("b", False)
                turn_back("b")
            if "g" in STAGES:
                ffn("g")


PROJ_AT = [5, 8, 11, 14, 24, 27]
EARLY_AT = [18, 21]
LATE_AT = [1, 3]


OT_ALL = {"a": 2 * HA, "b": 4 * NG}


F_TOTAL = {"ln": 2 * NT, "var": 1, "rstd": 1, "z": NT, "zt": 4, "xt_hi": 4, "xt_lo": 4,
           "consts": 48, "wg_hi": 1, "wg_lo": 1, "logits": 1, "route": 15, "shifted": 1, "ex": 1,
           "cwb": 1, "cwt_turned": 1, "cwt": 1,
           "wf_loaded0": 16 * (NJ - NJ // 2), "wf_loaded1": 16 * (NJ // 2), "w_hi": NJ, "w_lo": NJ,
           "g": 2 * NJ, "u": 2 * NJ, "c": 2 * NJ, "silu": 2 * NJ, "gu": 2 * NJ, "h": 2 * NJ,
           "h_hi": 2 * NJ, "h_lo": 2 * NJ, "down": 2 * NJ,
           "yt": 4, "y_turned": 4, "added": 4}


def since(s, name):
    return F_TOTAL[name] if s == "g" else 0


def loads(n, u, each):
    return (each // 2) * n + each - (each // 2) * u


def chunks(t):
    if t < 4:
        return [(t, 0, t + 1)]
    return [(4 + 2 * (t - 4), 0, 4), (5 + 2 * (t - 4), 4, t - 3)]


def rope_table(half, copies, scale):
    inv = (1.0 / 10000.0 ** (np.arange(half, dtype=np.float32) / half)).astype(np.float32)
    ang = (np.arange(T, dtype=np.float32)[:, None] * inv[None, :]).astype(np.float32)
    cos = np.cos(ang.astype(np.float64)).T
    sin = np.sin(ang.astype(np.float64)).T
    c = np.concatenate([cos, cos] * copies)
    s = np.concatenate([sin, -sin] * copies)
    return np.ascontiguousarray(np.stack([c, s], 1) * scale).astype(np.float32)


def kernel(**inputs):
    import ml_dtypes
    import concourse.bacc as _bacc
    from concourse.bass_utils import run_bass_kernel_spmd as _run

    bf16 = ml_dtypes.bfloat16
    a = {k.replace("L0_", ""): np.asarray(v) for k, v in inputs.items()}
    f = np.float32
    m = {}
    m["x"] = a["attn_a_x"].reshape(NT, P, D)
    m["idf"] = np.eye(P, dtype=f)
    m["idb"] = np.eye(P, dtype=f).astype(bf16)
    m["norm_w"] = a["attn_a_norm_w"].reshape(NC, P).T
    w = np.stack([a["attn_a_wq"], a["attn_a_wk"], a["attn_a_wv"]]).reshape(3, HA, P, NC, P)
    m["wa"] = w.transpose(1, 4, 3, 0, 2)
    m["la"] = np.concatenate([a["attn_a_qA"], a["attn_a_kA"], a["attn_a_vA"]]).reshape(3 * RANK, NC, P)
    lb = np.zeros((HA, 3, RANK, 3, P), f)
    for n, key in enumerate(("qB", "kB", "vB")):
        lb[:, n, :, n, :] = a[f"attn_a_{key}"].reshape(HA, P, RANK).transpose(0, 2, 1)
    m["lb"] = lb.reshape(HA, 3 * RANK, 3 * P)
    m["wo_a"] = a["attn_a_wo"].T.reshape(HA, P, D)
    m["oa"] = a["attn_a_oA"].reshape(RANK, HA, P).transpose(1, 0, 2)
    m["ob"] = a["attn_a_oB"].T
    m["rope_a"] = rope_table(64, 1, 128.0 ** -0.25)
    m["rope_b"] = rope_table(32, 2, 64.0 ** -0.25)
    q, k = np.arange(P)[:, None], np.arange(KW)[None, :]
    seen = (k > q) & (k <= q + WIN)
    NEG = -1e30
    m["maska"] = np.where(np.stack([seen & (k >= WIN), seen], 1), 0.0, NEG).astype(bf16)
    m["maskb"] = np.where(np.arange(P)[None, :] <= q, 0.0, NEG).astype(bf16)
    rows = NJ * P - NE * I_E - I_S
    pad = np.zeros((rows, D), f)
    gate = np.concatenate([a["ffn_w_gate"].reshape(-1, D), a["ffn_sw_gate"], pad]).reshape(NJ, P, NC, P)
    upw = np.concatenate([a["ffn_w_up"].reshape(-1, D), a["ffn_sw_up"], pad]).reshape(NJ, P, NC, P)
    dn = np.concatenate([a["ffn_w_down"].transpose(0, 2, 1).reshape(-1, D), a["ffn_sw_down"].T, pad])
    m["wf"] = np.concatenate([gate.transpose(0, 3, 2, 1).reshape(NJ, P, D),
                              upw.transpose(0, 3, 2, 1).reshape(NJ, P, D), dn.reshape(NJ, P, D)], 2)
    m["wg"] = a["ffn_gate_w"].T.reshape(NC, P, NE).transpose(1, 0, 2)
    expert = np.minimum(np.arange(NJ * P) // I_E, NE)
    one = (np.arange(NW)[:, None] == expert[None, :]).astype(f)
    m["sel"] = np.concatenate([one, one, one, np.zeros((P - 3 * NW, NJ * P), f)]).astype(bf16)
    m["iota"] = np.broadcast_to(np.arange(NE, dtype=f), (P, NT * TOPK, NE))
    wq = a["attn_b_Wq"].reshape(NC, P, NG, QPG * DB)
    wk = a["attn_b_Wk"].reshape(NC, P, NG, DB)
    m["wb"] = np.concatenate([wq, wk, wk], 3).transpose(2, 1, 0, 3)
    m["wvb"] = a["attn_b_Wv"].reshape(NC, P, NG * DB).transpose(1, 0, 2)
    m["wo_b"] = a["attn_b_Wo"].reshape(HA, P, D)

    nc = _bacc.Bacc("TRN2", target_bir_lowering=False, num_devices=1)
    arrays, args = {}, {}
    for name, v in m.items():
        arrays[f"in_{name}"] = np.ascontiguousarray(v)
        args[name] = nc.dram_tensor(f"in_{name}", v.shape, mybir.dt.from_np(v.dtype), kind="ExternalInput").ap()
    out = nc.dram_tensor("out", (NT, P, D), F32, kind="ExternalOutput").ap()
    build(nc, args, out)
    r = _run(nc, [arrays], core_ids=[0])
    return r.results[0]["out"].reshape(1, T, D)
```

```python
from contextlib import ExitStack

import numpy as np

import concourse.bass as bass
from concourse import mybir

F32 = mybir.dt.float32
F32R = mybir.dt.float32r
BF16 = mybir.dt.bfloat16
U32 = mybir.dt.uint32
ALU = mybir.AluOpType
ACT = mybir.ActivationFunctionType
AX = mybir.AxisListType

P = 128
T = 1024
NT = T // P
D = 256
NC = D // P
HALF = 512
LN_EPS = 1e-5
RMS_EPS = 1e-6

HA = 16
WIN = 64
PAD = WIN
TP = PAD + T + PAD
NV = TP // P
KW = WIN + P
RANK = 16
LORA_SCALE = 1.0 / RANK

NG = 8
QPG = 4
DB = 64
CHB = 12

NE = 16
TOPK = 4
I_E = 176
I_S = 352
NJ = (NE * I_E + I_S + P - 1) // P
NW = NE + 1


class Sems:

    def __init__(self, nc, ctx):
        self.nc, self.ctx, self.made = nc, ctx, {}

    def __call__(self, name):
        if name.startswith("g_"):
            name = "f" + name[1:]
        if name not in self.made:
            self.made[name] = self.ctx.enter_context(self.nc.semaphore(name))
        return self.made[name]


def build(nc, d, out, upto=99):
    ctx = ExitStack()
    with ctx:
        def sb(name, shape, dt=F32, c=ctx):
            return c.enter_context(nc.sbuf_tensor(name, shape, dt))

        sem = Sems(nc, ctx)
        ps = ctx.enter_context(nc.psum_tensor("ps", [P, 8, HALF], F32))

        x = sb("x_res", [P, NT, D])
        z = sb("z", [P, NT, D])
        xt_hi = sb("xt_hi", [P, NC, TP], F32R)
        xt_lo = sb("xt_lo", [P, NC, TP], F32R)
        ot = sb("ot", [P, HA, T])
        yt = sb("yt", [P, 2 * NC, HALF])
        idf = sb("idf", [P, P])
        idb = sb("idb", [P, P], BF16)
        norm_w = sb("norm_w", [P, NC])
        stats = sb("stats", [P, NT, 6])
        mv = sb("mv", [P, NT, 2])
        var = sb("var", [P, 2, NT])
        rstd = sb("rstd", [P, 2, NT])
        negh = sb("negh", [P, NT])
        rope = sb("rope", [P, 2, T])
        ra = sb("ra", [P, 2, HALF])
        rb = sb("rb", [P, 2, HALF])

        own = ExitStack()
        with own:
            wa = sb("wa", [P, 2, NC, 3, P], c=own)
            lb = sb("lb", [3 * RANK, 2, 3 * P], c=own)
            la = sb("la", [3 * RANK, NC, P], c=own)
            wef = sb("wef", [P, 2, NC, 3, P], c=own)
            wqk_hi = sb("wqk_hi", [P, 2, NC, 2, P], F32R, own)
            wqk_lo = sb("wqk_lo", [P, 2, NC, 2, P], F32R, own)
            wv_hi = sb("wv_hi", [P, NC, 2, P], F32R, own)
            wv_lo = sb("wv_lo", [P, NC, 2, P], F32R, own)
            qr = sb("qr", [P, 2, T], c=own)
            kr = sb("kr", [P, 2, PAD + T], c=own)
            va = sb("va", [P, NV, 2, P], c=own)
            pa = sb("pa", [P, NT, 2 * P], c=own)
            pta = sb("pta", [P, 2, HALF], c=own)
            nmax = sb("nmax", [P, NT], c=own)
            rsum = sb("rsum", [P, NT], c=own)
            rinv = sb("rinv", [P, NT], c=own)
            maska = sb("maska", [P, 2, KW], BF16, own)
            zt = sb("zt", [P, 2 * NC, HALF], c=own)
        own = ExitStack()
        with own:
            wo = sb("wo", [P, 2, D], c=own)
            oa = sb("oa", [RANK, 2, P], c=own)
            ob = sb("ob", [RANK, D], c=own)
            woe = sb("woe", [P, 2, D], c=own)
            wo_hi = sb("wo_hi", [P, 2, D], F32R, own)
            wo_lo = sb("wo_lo", [P, 2, D], F32R, own)
            ot_hi = sb("ot_hi", [P, 2, T], F32R, own)
            ot_lo = sb("ot_lo", [P, 2, T], F32R, own)
        own = ExitStack()
        with own:
            wf = sb("wf", [P, 2, 3 * D], c=own)
            wf_hi = sb("wf_hi", [P, 2, 3 * D], F32R, own)
            wf_lo = sb("wf_lo", [P, 2, 3 * D], F32R, own)
            sg = sb("sg", [P, 2, HALF], c=own)
            gu = sb("gu", [P, 2, HALF], c=own)
            hf = sb("hf", [P, 2, HALF], c=own)
            h_hi = sb("h_hi", [P, 2, HALF], F32R, own)
            h_lo = sb("h_lo", [P, 2, HALF], F32R, own)
            sel = sb("sel", [P, NJ * P], BF16, own)
            wg = sb("wg", [P, NC, NE], c=own)
            wg_hi = sb("wg_hi", [P, NC, NE], F32R, own)
            wg_lo = sb("wg_lo", [P, NC, NE], F32R, own)
            lg = sb("lg", [P, NT, NE], c=own)
            ex = sb("ex", [P, NT, NE], c=own)
            top = sb("top", [P, NT, 8], c=own)
            topi = sb("topi", [P, NT, 8], U32, own)
            topf = sb("topf", [P, NT, 8], c=own)
            iota = sb("iota", [P, NT * TOPK, NE], c=own)
            hit = sb("hit", [P, NT * TOPK, NE], c=own)
            chosen = sb("chosen", [P, NT, NE], c=own)
            cw = sb("cw", [P, NT, NW], c=own)
            cwr = sb("cwr", [P, NT, NW], c=own)
            csum = sb("csum", [P, NT], c=own)
            cinv = sb("cinv", [P, NT], c=own)
            cwb = sb("cwb", [P, NT, P], BF16, own)
            cwt = sb("cwt", [P, T], BF16, own)
        own = ExitStack()
        with own:
            wb = sb("wb", [P, NC, 3 * P], c=own)
            wb_hi = sb("wb_hi", [P, NC, 3 * P], F32R, own)
            wb_lo = sb("wb_lo", [P, NC, 3 * P], F32R, own)
            wvb = yt[:, 0:NC, :]
            vb = ot[:, :, :].rearrange("p (g k) (t d) -> p g k t d", k=2, d=DB)[:, :, 1, 0:NT, :]
            raw = sb("raw", [P, 2, HALF], c=own)
            qh = sb("qh", [P, 2, 2, T], F32R, own)
            kh = sb("kh", [P, 2, 2, T], F32R, own)
            wvb_hi = qh[:, 1, 0, :].rearrange("p (c n) -> p c n", c=NC)
            wvb_lo = qh[:, 1, 1, :].rearrange("p (c n) -> p c n", c=NC)
            vst = sb("vst", [P, 2, NT, 2 * DB], F32R, own)
            pb_low = sb("pb_low", [P, 6, P], c=own)
            pb_odd = sb("pb_odd", [P, 26, P], c=own)
            pt_hi = sb("pt_hi", [P, 3, HALF], F32R, own)
            pt_lo = sb("pt_lo", [P, 3, HALF], F32R, own)
            o_low = sb("o_low", [DB, HALF], c=own)
            nmb = sb("nmb", [P, 2, NT], c=own)
            rsb = sb("rsb", [P, 2, NT], c=own)
            rib = sb("rib", [P, 2, NT], c=own)
            maskb = sb("maskb", [P, P], BF16, own)

        def pb(par, t):
            if t < 3:
                flat, at = pb_low[:, :, :].rearrange("p n k -> p (n k)"), (0, 1, 3)[t]
            elif t == 3:
                flat, at = yt[:, :, :].rearrange("p a n -> p (a n)"), 11
            elif par:
                flat, at = pb_odd[:, :, :].rearrange("p n k -> p (n k)"), (0, 5, 11, 18)[t - 4]
            elif t < 6:
                flat, at = yt[:, :, :].rearrange("p a n -> p (a n)"), (0, 5)[t - 4]
            else:
                flat, at = z[:, :, :].rearrange("p a n -> p (a n)"), (0, 7)[t - 6]
            return flat[:, P * at:P * (at + t + 1)]

        def after(engine, name, n):
            if not isinstance(n, int) or n > 0:
                engine.wait_ge(sem(name), n)

        def all_groups(engine, group, head=None):
            if head:
                head(-1, 1, QPG - 2)
                head(-1, 1, QPG - 1)
            group(0, 0)
            group(1, 1)
            with engine.Fori(1, NG // 2 - 1) as i:
                for gp in range(2):
                    group(2 * i + gp, gp)
            group(NG - 2, 0)
            group(NG - 1, 1)
            if head:
                head(NG, 0, 0)
                head(NG, 0, 1)

        block = ctx.enter_context(nc.Block())

        STAGES = ["a", "f", "b", "g"][:upto]


        @block.sync
        def _(sp):
            sp.dma_start(x[:, :, :], d["x"].rearrange("t p d -> p t d")).then_inc(sem("x_loaded"), 16)
            sp.dma_start(idf[:, :], d["idf"]).then_inc(sem("ident_loaded"), 16)
            sp.dma_start(idb[:, :], d["idb"]).then_inc(sem("ident_loaded"), 16)
            sp.dma_start(norm_w[:, :], d["norm_w"]).then_inc(sem("a_consts"), 16)
            sp.dma_start(la[:, :, :], d["la"]).then_inc(sem("a_consts"), 16)
            sp.dma_start(maska[:, :, :], d["maska"]).then_inc(sem("a_consts"), 16)
            sp.dma_start(rope[:, :, :], d["rope_a"]).then_inc(sem("a_consts"), 16)

            def load_head(h, u, guard):
                if guard:
                    sp.wait_ge(sem("a_weff"), h - 1)
                    sp.wait_ge(sem("a_lora"), h - 1)
                sp.dma_start(wa[:, u, :, :, :], d["wa"][h]).then_inc(sem(f"wa_loaded{u}"), 16)
                sp.dma_start(lb[:, u, :], d["lb"][h]).then_inc(sem(f"wa_loaded{u}"), 16)

            load_head(0, 0, False)
            load_head(1, 1, False)
            with sp.Fori(1, HA // 2) as i:
                for u in range(2):
                    load_head(2 * i + u, u, True)

            def out_proj(s, w, lora):
                sp.wait_ge(sem(f"{s}_ot"), OT_ALL[s])
                if lora:
                    sp.dma_start(ob[:, :], d["ob"]).then_inc(sem(f"{s}_ob_loaded"), 16)

                def load(h, u, guard):
                    if guard:
                        sp.wait_ge(sem(f"{s}_woe"), h - 1)
                    sp.dma_start(wo[:, u, :], d[w][h]).then_inc(sem(f"{s}_wo_loaded{u}"), 16)
                    if lora:
                        sp.dma_start(oa[:, u, :], d["oa"][h]).then_inc(sem(f"{s}_wo_loaded{u}"), 16)

                load(0, 0, False)
                load(1, 1, False)
                with sp.Fori(1, HA // 2) as i:
                    for u in range(2):
                        load(2 * i + u, u, True)

            def ffn(s, before):
                sp.wait_ge(sem(f"{before}_yt"), since(before, "yt") + 4)
                sp.dma_start(wg[:, :, :], d["wg"]).then_inc(sem(f"{s}_consts"), 16)
                sp.dma_start(sel[:, :], d["sel"]).then_inc(sem(f"{s}_consts"), 16)
                sp.dma_start(iota[:, :, :], d["iota"]).then_inc(sem(f"{s}_consts"), 16)

                def load(j, u, guard):
                    if guard:
                        sp.wait_ge(sem(f"{s}_w_hi"), since(s, "w_hi") + j - 1)
                        sp.wait_ge(sem(f"{s}_w_lo"), since(s, "w_lo") + j - 1)
                    sp.dma_start(wf[:, u, :], d["wf"][j]).then_inc(sem(f"{s}_wf_loaded{u}"), 16)

                load(0, 0, False)
                load(1, 1, False)
                with sp.Fori(1, NJ // 2) as i:
                    for u in range(2):
                        load(2 * i + u, u, True)
                load(NJ - 1, 0, True)

            out_proj("a", "wo_a", True)
            if "f" in STAGES:
                ffn("f", "a")
            if "b" in STAGES:
                sp.wait_ge(sem("f_added"), NT // 2)
                sp.dma_start(rope[:, :, :], d["rope_b"]).then_inc(sem("b_consts"), 16)
                sp.dma_start(wvb[:, :, :], d["wvb"]).then_inc(sem("b_consts"), 16)
                sp.dma_start(maskb[:, :], d["maskb"]).then_inc(sem("b_consts"), 16)

                def load_group(g):
                    if not (isinstance(g, int) and g == 0):
                        sp.wait_ge(sem("b_w_hi"), g)
                        sp.wait_ge(sem("b_w_lo"), g)
                    sp.dma_start(wb[:, :, :], d["wb"][g]).then_inc(sem("wb_loaded"), 16)

                def swap(n, r):
                    sp.wait_ge(sem("b_raw"), n + 1)
                    for src, dst in ((32, 0), (0, 32), (96, 64), (64, 96)):
                        sp.dma_start(rb[dst:dst + 32, r, :], raw[src:src + 32, r, :]).then_inc(
                            sem(f"b_swapped{r}"), 16)

                def group(g, gp):
                    if not (isinstance(g, int) and g >= NG - 2):
                        load_group(g + 2)
                    if not (isinstance(g, int) and g == NG - 1):
                        for piece in range(6):
                            swap(6 * (g + 1) + piece, piece % 2)

                load_group(0)
                load_group(1)
                for piece in range(6):
                    swap(piece, piece % 2)
                all_groups(sp, group)
                out_proj("b", "wo_b", False)
            if "g" in STAGES:
                ffn("g", "b")
            sp.wait_ge(sem(f"{STAGES[-1]}_added"), since(STAGES[-1], "added") + NT // 2)
            sp.dma_start(out.rearrange("t p d -> p t d"), x[:, :, :]).then_inc(sem("stored"), 16)
            sp.wait_ge(sem("stored"), 16)

        @block.vector
        def _(dve):
            v = nc.vector
            v.memset(xt_hi[:, :, 0:PAD].bitcast(F32), 0.0)
            v.memset(xt_hi[:, :, PAD + T:TP].bitcast(F32), 0.0)
            v.memset(xt_lo[:, :, 0:PAD].bitcast(F32), 0.0)
            v.memset(xt_lo[:, :, PAD + T:TP].bitcast(F32), 0.0)
            v.memset(kr[:, :, 0:PAD], 0.0)
            v.memset(pa[:, :, KW:2 * P], 0.0)
            v.memset(negh[:, :], -0.5).then_inc(sem("padded"), 1)

            def norm(s, before):
                me = sem(f"{s}_ln")
                if before is None:
                    dve.wait_ge(sem("x_loaded"), 16)
                for t in range(NT):
                    if before is not None and t % 2 == 0:
                        dve.wait_ge(sem(f"{before}_added"), since(before, "added") + t // 2 + 1)
                    v.bn_stats(stats[:, t, :], x[:, t, :]).then_inc(me, 1)
                for t in range(NT):
                    dve.wait_ge(me, since(s, "ln") + t + 1)
                    v.bn_aggr(mv[:, t, :], stats[:, t, :]).then_inc(me, 1)
                dve.wait_ge(me, since(s, "ln") + 2 * NT)
                v.tensor_scalar(var[:, 0, :], mv[:, :, 1], LN_EPS, None, ALU.add).then_inc(sem(f"{s}_var"), 1)
                dve.wait_ge(sem(f"{s}_rstd"), since(s, "rstd") + 1)
                if s != "a":
                    for t in range(NT):
                        v.tensor_scalar(z[:, t, :], x[:, t, :], mv[:, t, 0:1], rstd[:, 0, t:t + 1],
                                        ALU.subtract, ALU.mult).then_inc(sem(f"{s}_z"), 1)
                    for q in range(2 * NC):
                        dve.wait_ge(sem(f"{s}_xt_hi"), since(s, "xt_hi") + q + 1)
                        at = slice(PAD + HALF * (q % 2), PAD + HALF * (q % 2) + HALF)
                        v.tensor_tensor(xt_lo[:, q // 2, at], ps[:, q, :], xt_hi[:, q // 2, at].bitcast(F32),
                                        ALU.subtract).then_inc(sem(f"{s}_xt_lo"), 1)
                    return
                for t in range(NT):
                    v.tensor_scalar(z[:, t, :], x[:, t, :], mv[:, t, 0:1], rstd[:, 0, t:t + 1],
                                    ALU.subtract, ALU.mult).then_inc(sem("a_zz"), 1)
                dve.wait_ge(sem("padded"), 1)
                for t in range(NT):
                    dve.wait_ge(sem("a_zz"), t + 1)
                    v.tensor_tensor_reduce(out=yt[:, t % 4, 0:D], in0=z[:, t, :], in1=z[:, t, :], scale=1.0 / D,
                                           scalar=0.0, op0=ALU.mult, op1=ALU.add,
                                           accum_out=rsum[:, t:t + 1]).then_inc(sem("a_sq"), 1)
                    dve.wait_ge(sem("a_sq"), t + 1)
                v.tensor_scalar(var[:, 1, :], rsum[:, :], RMS_EPS, None, ALU.add).then_inc(sem("a_var2"), 1)
                for t in range(NT):
                    v.tensor_tensor(x[:, t, :], x[:, t, :], z[:, t, :], ALU.add).then_inc(sem("a_xz"), 1)
                dve.wait_ge(sem("a_rstd2"), 1)
                dve.wait_ge(sem("a_xz"), NT)
                for t in range(NT):
                    v.tensor_scalar(z[:, t, :], z[:, t, :], rstd[:, 1, t:t + 1], None,
                                    ALU.mult).then_inc(sem("a_z"), 1)
                dve.wait_ge(sem("a_consts"), 64)
                for q in range(2 * NC):
                    dve.wait_ge(sem("a_zt"), q + 1)
                    v.tensor_scalar(zt[:, q, :], ps[:, q, :], norm_w[:, q // 2:q // 2 + 1], None,
                                    ALU.mult).then_inc(sem("a_ztw"), 1)
                for q in range(2 * NC):
                    dve.wait_ge(sem("a_xt_hi"), q + 1)
                    at = slice(PAD + HALF * (q % 2), PAD + HALF * (q % 2) + HALF)
                    v.tensor_tensor(xt_lo[:, q // 2, at], zt[:, q, :], xt_hi[:, q // 2, at].bitcast(F32),
                                    ALU.subtract).then_inc(sem("a_xt_lo"), 1)

            def residual(s):
                for n in range(NT // 2):
                    dve.wait_ge(sem(f"{s}_y_turned"), since(s, "y_turned") + n + 1)
                    v.tensor_tensor(x[:, 2 * n:2 * n + 2, :], x[:, 2 * n:2 * n + 2, :],
                                    ps[:, n, :].rearrange("p (t d) -> p t d", t=2),
                                    ALU.add).then_inc(sem(f"{s}_added"), 1)

            def rope_piece(bank, r, half, swaps):
                at = slice(HALF * half, HALF * half + HALF)
                v.tensor_tensor(ra[:, r, :], ps[:, bank, :], rope[:, 0, at], ALU.mult)
                for src, dst, n in swaps:
                    last = v.tensor_tensor(rb[dst:dst + n, r, :], ps[src:src + n, bank, :],
                                           rope[src:src + n, 1, at], ALU.mult)
                return last

            norm("a", None)

            def weff(h, u):
                dve.wait_ge(sem("a_lora"), h + 1)
                dve.wait_ge(sem(f"wa_loaded{u}"), loads(h, u, 32))
                dve.wait_ge(sem("a_w_hi"), h)
                dve.wait_ge(sem("a_w_lo"), h)
                for c in range(NC):
                    last = v.scalar_tensor_tensor(out=wef[:, u, c, :, :].rearrange("p m d -> p (m d)"),
                                                  in0=ps[:, c, 0:3 * P], scalar=LORA_SCALE,
                                                  in1=wa[:, u, c, :, :].rearrange("p m d -> p (m d)"),
                                                  op0=ALU.mult, op1=ALU.add)
                last.then_inc(sem("a_weff"), 1)

            def rope_a(h, piece):
                dve.wait_ge(sem("a_qk"), 4 * h + piece + 1)
                if piece < 2:
                    dve.wait_ge(sem("a_rot"), 4 * h)
                else:
                    dve.wait_ge(sem("a_rot"), 4 * h + piece - 1)
                rope_piece(piece % 2, piece % 2, piece % 2,
                           [(64, 0, 64), (0, 64, 64)]).then_inc(sem("a_mul"), 1)

            def row_max(h, u, n):
                dve.wait_ge(sem("a_scores"), 4 * h + n + 1)
                dve.wait_ge(sem("a_exp"), 4 * h)
                bank = 2 + (n + 2 * u) % 4
                v.tensor_reduce(nmax[:, 2 * n:2 * n + 2], ps[:, bank, 0:2 * KW].rearrange("p (t k) -> p t k", t=2),
                                AX.X, ALU.max, negate=True).then_inc(sem("a_max"), 1)

            def row_inv(h, n):
                dve.wait_ge(sem("a_exp"), 4 * h + n + 1)
                dve.wait_ge(sem("a_pn"), 4 * h)
                v.reciprocal(rinv[:, 2 * n:2 * n + 2], rsum[:, 2 * n:2 * n + 2]).then_inc(sem("a_inv"), 1)

            def head_a(h, u, ahead1, ahead2):
                for n in range(4):
                    row_max(h, u, n)
                if ahead1:
                    rope_a(h + 1, 0)
                row_inv(h, 0)
                row_inv(h, 1)
                if ahead1:
                    rope_a(h + 1, 1)
                row_inv(h, 2)
                row_inv(h, 3)
                if ahead1:
                    rope_a(h + 1, 2)
                    rope_a(h + 1, 3)
                if ahead2:
                    weff(h + 2, u)

            dve.wait_ge(sem("a_consts"), 64)
            weff(0, 0)
            weff(1, 1)
            for piece in range(4):
                rope_a(0, piece)
            with dve.Fori(0, HA // 2 - 1) as i:
                for u in range(2):
                    head_a(2 * i + u, u, True, True)
            head_a(HA - 2, 0, True, False)
            head_a(HA - 1, 1, False, False)

            def out_proj(s, lora):
                def step(h, u):
                    if lora:
                        dve.wait_ge(sem(f"{s}_ol"), h + 1)
                    dve.wait_ge(sem(f"{s}_wo_loaded{u}"), loads(h, u, 32 if lora else 16))
                    dve.wait_ge(sem(f"{s}_wo_hi"), h)
                    dve.wait_ge(sem(f"{s}_wo_lo"), h)
                    if lora:
                        v.scalar_tensor_tensor(out=woe[:, u, :], in0=ps[:, u, 0:D], scalar=LORA_SCALE,
                                               in1=wo[:, u, :], op0=ALU.mult,
                                               op1=ALU.add).then_inc(sem(f"{s}_woe"), 1)
                    else:
                        v.tensor_copy(woe[:, u, :], wo[:, u, :]).then_inc(sem(f"{s}_woe"), 1)
                    dve.wait_ge(sem(f"{s}_ot_hi"), h + 1)
                    v.tensor_tensor(ot_lo[:, u, :], ot[:, h, :], ot_hi[:, u, :].bitcast(F32),
                                    ALU.subtract).then_inc(sem(f"{s}_ot_lo"), 1)

                with dve.Fori(0, HA // 2) as i:
                    for u in range(2):
                        step(2 * i + u, u)

            dve.wait_ge(sem("a_ot"), 2 * HA)
            out_proj("a", True)
            residual("a")

            def router(s):
                me = sem(f"{s}_route")
                n = 0

                def link(ins):
                    nonlocal n
                    n += 1
                    ins.then_inc(me, 1)
                    dve.wait_ge(me, since(s, "route") + n)

                dve.wait_ge(sem(f"{s}_consts"), since(s, "consts") + 48)
                dve.wait_ge(sem(f"{s}_wg_hi"), since(s, "wg_hi") + 1)
                v.tensor_tensor(wg_lo[:, :, :], wg[:, :, :], wg_hi[:, :, :].bitcast(F32),
                                ALU.subtract).then_inc(sem(f"{s}_wg_lo"), 1)
                v.memset(cwb[:, :, :], 0.0)
                v.memset(cw[:, :, :], 1.0)
                dve.wait_ge(sem(f"{s}_logits"), since(s, "logits") + 1)
                link(v.tensor_copy(lg[:, :, :], ps[:, 3, 0:NT * NE].rearrange("p (t e) -> p t e", e=NE)))
                for t in range(NT):
                    ins = v.max(top[:, t, :], lg[:, t, :])
                link(ins)
                for t in range(NT):
                    ins = v.max_index(topi[:, t, :], top[:, t, :], lg[:, t, :])
                link(ins)
                link(v.tensor_copy(topf[:, :, :], topi[:, :, :]))
                link(v.tensor_tensor(hit[:, :, :].rearrange("p (t k) e -> p t k e", t=NT),
                                     iota[:, :, :].rearrange("p (t k) e -> p t k e", t=NT),
                                     topf[:, :, 0:TOPK].unsqueeze(3).broadcast_to([P, NT, TOPK, NE]),
                                     ALU.is_equal))
                link(v.tensor_reduce(chosen[:, :, :], hit[:, :, :].rearrange("p (t k) e -> p t e k", t=NT),
                                     AX.X, ALU.add))
                v.tensor_tensor(lg[:, :, :], lg[:, :, :], top[:, :, 0:1].broadcast_to([P, NT, NE]),
                                ALU.subtract).then_inc(sem(f"{s}_shifted"), 1)
                dve.wait_ge(sem(f"{s}_ex"), since(s, "ex") + 1)
                link(v.tensor_tensor(ex[:, :, :], ex[:, :, :], chosen[:, :, :], ALU.mult))
                link(v.tensor_reduce(csum[:, :], ex[:, :, :], AX.X, ALU.add))
                link(v.reciprocal(cinv[:, :], csum[:, :]))
                link(v.tensor_tensor(cw[:, :, 0:NE], ex[:, :, :],
                                     cinv[:, :].unsqueeze(2).broadcast_to([P, NT, NE]), ALU.mult))
                for part in range(3):
                    at = slice(NW * part, NW * part + NW)
                    src = cw if part == 0 else cwr
                    link(v.tensor_copy(cwb[:, :, at], src[:, :, :]))
                    if part < 2:
                        link(v.tensor_tensor(cwr[:, :, :], src[:, :, :], cwb[:, :, at], ALU.subtract))
                ins = v.tensor_copy(top[:, 0, 0:1], cinv[:, 0:1])
                ins.then_inc(sem(f"{s}_cwb"), 1)
                dve.wait_ge(sem(f"{s}_cwt_turned"), since(s, "cwt_turned") + 1)
                v.tensor_copy(cwt[:, :], ps[:, 3, :].bitcast(BF16)[:, 0:T]).then_inc(sem(f"{s}_cwt"), 1)

            def ffn(s):
                def tile(j, u):
                    for half in range(2):
                        k = 2 * j + half
                        b = half
                        dve.wait_ge(sem(f"{s}_silu"), since(s, "silu") + k + 1)
                        dve.wait_ge(sem(f"{s}_u"), since(s, "u") + k + 1)
                        v.tensor_tensor(gu[:, b, :], ps[:, 1, :], sg[:, b, :], ALU.mult).then_inc(sem(f"{s}_gu"), 1)
                        dve.wait_ge(sem(f"{s}_gu"), since(s, "gu") + k + 1)
                        dve.wait_ge(sem(f"{s}_c"), since(s, "c") + k + 1)
                        dve.wait_ge(sem(f"{s}_h_hi"), since(s, "h_hi") + k)
                        dve.wait_ge(sem(f"{s}_h_lo"), since(s, "h_lo") + k)
                        v.tensor_tensor(hf[:, b, :], ps[:, 2, :], gu[:, b, :], ALU.mult).then_inc(sem(f"{s}_h"), 1)
                        dve.wait_ge(sem(f"{s}_h_hi"), since(s, "h_hi") + k + 1)
                        dve.wait_ge(sem(f"{s}_down"), since(s, "down") + k)
                        v.tensor_tensor(h_lo[:, b, :], hf[:, b, :], h_hi[:, b, :].bitcast(F32),
                                        ALU.subtract).then_inc(sem(f"{s}_h_lo"), 1)

                with dve.Fori(0, NJ // 2) as i:
                    for u in range(2):
                        tile(2 * i + u, u)
                tile(NJ - 1, 0)

            if "f" in STAGES:
                norm("f", "a")
                router("f")
                ffn("f")
                residual("f")

            if "b" in STAGES:
                norm("b", "f")
                dve.wait_ge(sem("b_consts"), 48)
                dve.wait_ge(sem("b_wv_hi"), 1)
                v.tensor_tensor(wvb_lo[:, :, :], wvb[:, :, :], wvb_hi[:, :, :].bitcast(F32),
                                ALU.subtract).then_inc(sem("b_wv_lo"), 1)

                def cos_b(n, piece):
                    dve.wait_ge(sem("b_raw"), n + 1)
                    after(dve, "b_lo", n - 1)
                    half = piece % 2
                    v.tensor_tensor(ra[:, half, :], ps[:, 7, :], rope[:, 0, HALF * half:HALF * half + HALF],
                                    ALU.mult).then_inc(sem("b_cos"), 1)

                def low_b(n, kp, piece):
                    dve.wait_ge(sem("b_hi"), n + 1)
                    half = piece % 2
                    at = slice(HALF * half, HALF * half + HALF)
                    if piece < 2:
                        ins = v.tensor_tensor(kh[:, kp, 1, at], ra[:, half, :], kh[:, kp, 0, at].bitcast(F32),
                                              ALU.subtract)
                    else:
                        pair = piece // 2 - 1
                        v.tensor_tensor(qh[64:128, pair, 0, at], ra[0:64, half, :],
                                        qh[0:64, pair, 0, at].bitcast(F32), ALU.subtract)
                        ins = v.tensor_tensor(qh[0:64, pair, 1, at], ra[64:128, half, :],
                                              qh[64:128, pair, 1, at].bitcast(F32), ALU.subtract)
                    ins.then_inc(sem("b_lo"), 1)

                def row_max_b(h, par, i):
                    t = SCORE_TILES[i]
                    dve.wait_ge(sem("b_scores"), NT * h + i + 1)
                    b = 2 * (i % 2)
                    v.tensor_reduce(nmb[:, par, i:i + 1],
                                    ps[:, b:b + 2, :].rearrange("p b k -> p (b k)")[:, 0:P * (t + 1)],
                                    AX.X, ALU.max, negate=True).then_inc(sem("b_max"), 1)

                def row_inv_b(h, par, i):
                    dve.wait_ge(sem("b_exp"), NT * h + i + 1)
                    after(dve, "b_pn", NT * h + i - 2 * NT + 1)
                    v.reciprocal(rib[:, par, i:i + 1], rsb[:, par, i:i + 1]).then_inc(sem("b_inv"), 1)

                def pt_lo_b(h, s):
                    c = CHB * h + s
                    first, n = chunk_columns(s)
                    dve.wait_ge(sem("b_pt_hi"), c + 1)
                    after(dve, "b_prod", c - 2)
                    at = slice(P * first, P * first + P * n)
                    v.tensor_tensor(pt_lo[:, s % 3, at], ps[:, 4 + s % 2, at], pt_hi[:, s % 3, at].bitcast(F32),
                                    ALU.subtract).then_inc(sem("b_pt_lo"), 1)

                def o_add(h, hh, g, bank):
                    dve.wait_ge(sem("b_o_low"), 2 * h + bank - 6 + 1)
                    half = 7 - bank
                    r = 64 * (hh % 2)
                    v.tensor_tensor(ot[r:r + 64, 2 * g + hh // 2, HALF * half:HALF * half + HALF],
                                    ps[0:64, bank, :], o_low[:, :], ALU.add).then_inc(sem("b_ot"), 1)

                def head(g, gp, hh):
                    for kind, dh, i in steps(("max", "inv", "pt_lo", "o_add", "cos", "low"), g, hh):
                        h = QPG * g + hh + dh
                        piece = 6 * (g + 1 + dh) + i
                        if kind == "max":
                            row_max_b(h, (hh + dh) % 2, i)
                        elif kind == "inv":
                            row_inv_b(h, (hh + dh) % 2, i)
                        elif kind == "pt_lo":
                            pt_lo_b(h, i)
                        elif kind == "o_add":
                            o_add(h, head_at(g, gp, hh, dh)[2], head_at(g, gp, hh, dh)[0], 6 + i)
                        elif kind == "cos":
                            cos_b(piece, i)
                        elif kind == "low":
                            low_b(piece, (gp + 1 + dh) % 2, i)

                def group(g, gp):
                    for hh in range(QPG):
                        head(g, gp, hh)

                for piece in range(6):
                    cos_b(piece, piece)
                    low_b(piece, 0, piece)
                all_groups(dve, group, head)
                out_proj("b", False)
                residual("b")
            if "g" in STAGES:
                norm("g", "b")
                router("g")
                ffn("g")
                residual("g")

        @block.gpsimd
        def _(pool):
            g_ = nc.gpsimd

            def root(s, k=0):
                if k == 0:
                    pool.wait_ge(sem(f"{s}_var"), since(s, "var") + 1)
                else:
                    pool.wait_ge(sem("a_var2"), 1)
                g_.tensor_tensor(rstd[:, k, :], var[:, k, :], negh[:, :],
                                 ALU.pow).then_inc(sem(f"{s}_rstd" if k == 0 else "a_rstd2"), 1)

            pool.wait_ge(sem("padded"), 1)
            root("a")
            root("a", 1)

            def w_lo(h, u):
                pool.wait_ge(sem("a_w_hi"), h + 1)
                pool.wait_ge(sem("a_qk"), 4 * h - 4 if not isinstance(h, int) or h else 0)
                g_.tensor_tensor(wqk_lo[:, u, :, :, :], wef[:, u, :, 0:2, :], wqk_hi[:, u, :, :, :].bitcast(F32),
                                 ALU.subtract)
                g_.tensor_tensor(wv_lo[:, :, u, :], wef[:, u, :, 2, :], wv_hi[:, :, u, :].bitcast(F32),
                                 ALU.subtract).then_inc(sem("a_w_lo"), 1)

            def rot(h, u, piece):
                pool.wait_ge(sem("a_mul"), 4 * h + piece + 1)
                at = HALF * (piece % 2)
                dst = qr[:, u, at:at + HALF] if piece < 2 else kr[:, u, PAD + at:PAD + at + HALF]
                g_.tensor_tensor(dst, ra[:, piece % 2, :], rb[:, piece % 2, :], ALU.add).then_inc(sem("a_rot"), 1)

            def p_norm(h, n):
                pool.wait_ge(sem("a_inv"), 4 * h + n + 1)
                two = slice(2 * n, 2 * n + 2)
                g_.tensor_tensor(pa[:, two, 0:KW], pa[:, two, 0:KW],
                                 rinv[:, two].unsqueeze(2).broadcast_to([P, 2, KW]),
                                 ALU.mult).then_inc(sem("a_pn"), 1)

            def head_a(h, u, ahead1, ahead2):
                if ahead1:
                    pool.wait_ge(sem("a_scores"), 4 * h)
                    rot(h + 1, 1 - u, 0)
                p_norm(h, 0)
                p_norm(h, 1)
                if ahead1:
                    rot(h + 1, 1 - u, 1)
                p_norm(h, 2)
                p_norm(h, 3)
                if ahead1:
                    rot(h + 1, 1 - u, 2)
                    rot(h + 1, 1 - u, 3)
                if ahead2:
                    w_lo(h + 2, u)

            w_lo(0, 0)
            w_lo(1, 1)
            for piece in range(4):
                rot(0, 0, piece)
            with pool.Fori(0, HA // 2 - 1) as i:
                for u in range(2):
                    head_a(2 * i + u, u, True, True)
            head_a(HA - 2, 0, True, False)
            head_a(HA - 1, 1, False, False)

            def out_proj(s):
                def step(h, u):
                    pool.wait_ge(sem(f"{s}_wo_hi"), h + 1)
                    g_.tensor_tensor(wo_lo[:, u, :], woe[:, u, :], wo_hi[:, u, :].bitcast(F32),
                                     ALU.subtract).then_inc(sem(f"{s}_wo_lo"), 1)

                with pool.Fori(0, HA // 2) as i:
                    for u in range(2):
                        step(2 * i + u, u)

            def ffn(s):
                root(s)

                def tile(j, u, first):
                    pool.wait_ge(sem(f"{s}_w_hi"), since(s, "w_hi") + j + 1)
                    g_.tensor_tensor(wf_lo[:, u, :], wf[:, u, :], wf_hi[:, u, :].bitcast(F32),
                                     ALU.subtract).then_inc(sem(f"{s}_w_lo"), 1)

                with pool.Fori(0, NJ // 2) as i:
                    for u in range(2):
                        tile(2 * i + u, u, False)
                tile(NJ - 1, 0, False)

            out_proj("a")
            if "f" in STAGES:
                ffn("f")
            if "b" in STAGES:
                root("b")

                def w_lo_b(g):
                    pool.wait_ge(sem("b_w_hi"), g + 1)
                    after(pool, "b_proj", 6 * g)
                    g_.tensor_tensor(wb_lo[:, :, :], wb[:, :, :], wb_hi[:, :, :].bitcast(F32),
                                     ALU.subtract).then_inc(sem("b_w_lo"), 1)

                def rot_b(n, piece):
                    half = piece % 2
                    pool.wait_ge(sem(f"b_swapped{half}"), 64 * (n // 2 + 1) if isinstance(n, int) else 32 * n + 64 - 32 * half)
                    g_.tensor_tensor(rb[:, half, :], rb[:, half, :], rope[:, 1, HALF * half:HALF * half + HALF],
                                     ALU.mult).then_inc(sem("b_sin"), 1)
                    pool.wait_ge(sem("b_sin"), n + 1)
                    pool.wait_ge(sem("b_cos"), n + 1)
                    g_.tensor_tensor(ra[:, half, :], ra[:, half, :], rb[:, half, :], ALU.add).then_inc(sem("b_rot"), 1)

                def v_lo_b(g, gp):
                    pool.wait_ge(sem("b_v_hi"), g + 1)
                    g_.tensor_tensor(vst[:, gp, :, DB:2 * DB], vb[:, g, :, :],
                                     vst[:, gp, :, 0:DB].bitcast(F32), ALU.subtract).then_inc(sem("b_v_lo"), 1)

                def p_norm_b(h, par, i):
                    pool.wait_ge(sem("b_inv"), NT * h + i + 1)
                    t = SCORE_TILES[i]
                    g_.tensor_tensor(pb(par, t), pb(par, t), rib[:, par, i:i + 1].broadcast_to([P, P * (t + 1)]),
                                     ALU.mult).then_inc(sem("b_pn"), 1)

                def head(g, gp, hh):
                    for kind, dh, i in steps(("norm", "rotate"), g, hh):
                        if kind == "norm":
                            p_norm_b(QPG * g + hh + dh, (hh + dh) % 2, i)
                        else:
                            rot_b(6 * (g + 1 + dh) + i, i)
                        if hh == QPG - 1 and kind == "norm" and not (isinstance(g, int) and not 0 <= g < NG - 1):
                            if i == V_SPLIT_AT:
                                v_lo_b(g + 1, 1 - gp)
                            if i == W_LO_AT and not (isinstance(g, int) and g >= NG - 2):
                                w_lo_b(g + 2)

                def group(g, gp):
                    for hh in range(QPG):
                        head(g, gp, hh)

                w_lo_b(0)
                for piece in range(6):
                    rot_b(piece, piece)
                v_lo_b(0, 0)
                w_lo_b(1)
                all_groups(pool, group, head)
                out_proj("b")
            if "g" in STAGES:
                ffn("g")

        @block.scalar
        def _(act):
            s_ = nc.scalar

            def norm(s):
                for q in range(2 * NC):
                    at = slice(PAD + HALF * (q % 2), PAD + HALF * (q % 2) + HALF)
                    if s == "a":
                        act.wait_ge(sem("a_ztw"), q + 1)
                        src = zt[:, q, :]
                    else:
                        act.wait_ge(sem(f"{s}_zt"), since(s, "zt") + q + 1)
                        src = ps[:, q, :]
                    s_.copy(xt_hi[:, q // 2, at], src).then_inc(sem(f"{s}_xt_hi"), 1)

            def y_out(s, acc, n):
                act.wait_ge(acc, n)
                for q in range(4):
                    s_.copy(yt[:, q, :], ps[:, 4 + q, :]).then_inc(sem(f"{s}_yt"), 1)

            norm("a")

            def w_hi(h, u):
                act.wait_ge(sem("a_weff"), h + 1)
                s_.copy(wqk_hi[:, u, :, :, :], wef[:, u, :, 0:2, :])
                s_.copy(wv_hi[:, :, u, :], wef[:, u, :, 2, :]).then_inc(sem("a_w_hi"), 1)

            def v_out(i, piece):
                act.wait_ge(sem("a_v"), 5 * i + piece + 1)
                act.wait_ge(sem("a_pv"), 8 * i)
                n = 2 if piece < 4 else 1
                s_.copy(va[:, 2 * piece:2 * piece + n, :, :].rearrange("p t u d -> p (t u d)"),
                        ps[:, piece % 2, 0:n * 2 * P]).then_inc(sem("a_vout"), 1)

            def exps(h, u, n):
                act.wait_ge(sem("a_max"), 4 * h + n + 1)
                act.wait_ge(sem("a_turned"), 4 * h)
                bank = 2 + (n + 2 * u) % 4
                for m in range(2):
                    t = 2 * n + m
                    last = s_.activation(pa[:, t, 0:KW], ps[:, bank, KW * m:KW * m + KW], ACT.Exp,
                                         bias=nmax[:, t:t + 1], accum_out=rsum[:, t:t + 1])
                last.then_inc(sem("a_exp"), 1)

            def head_a(i, h, u, ahead1, ahead2):
                for n in range(4):
                    exps(h, u, n)
                if ahead2:
                    w_hi(h + 2, u)
                for n in range(4):
                    act.wait_ge(sem("a_turned"), 4 * h + n + 1)
                    if n < 2:
                        act.wait_ge(sem("a_pv"), 4 * h)
                    else:
                        act.wait_ge(sem("a_pv"), 4 * h + n - 1)
                    s_.copy(pta[:, n % 2, :], ps[:, 6 + n % 2, :]).then_inc(sem("a_pt"), 1)
                    if n == 2:
                        o_out(h, u, 0)
                o_out(h, u, 1)
                if u == 1 and ahead2:
                    for piece in range(5):
                        v_out(i + 1, piece)

            def o_out(h, u, half):
                act.wait_ge(sem("a_pv"), 4 * h + 2 * half + 2)
                s_.copy(ot[:, h, HALF * half:HALF * half + HALF],
                        ps[:, 2 + 2 * u + half, :]).then_inc(sem("a_ot"), 1)

            w_hi(0, 0)
            w_hi(1, 1)
            for piece in range(5):
                v_out(0, piece)
            with act.Fori(0, HA // 2 - 1) as i:
                for u in range(2):
                    head_a(i, 2 * i + u, u, True, True)
            head_a(HA // 2 - 1, HA - 2, 0, True, False)
            head_a(HA // 2 - 1, HA - 1, 1, False, False)

            def out_proj(s):
                def step(h, u):
                    act.wait_ge(sem(f"{s}_oacc"), h - 1 if not isinstance(h, int) or h else 0)
                    s_.copy(ot_hi[:, u, :], ot[:, h, :]).then_inc(sem(f"{s}_ot_hi"), 1)
                    act.wait_ge(sem(f"{s}_woe"), h + 1)
                    s_.copy(wo_hi[:, u, :], woe[:, u, :]).then_inc(sem(f"{s}_wo_hi"), 1)

                step(0, 0)
                step(1, 1)
                with act.Fori(1, HA // 2) as i:
                    for u in range(2):
                        step(2 * i + u, u)

            out_proj("a")
            y_out("a", sem("a_oacc"), HA)

            def ffn(s):
                norm(s)
                act.wait_ge(sem(f"{s}_consts"), since(s, "consts") + 48)
                s_.copy(wg_hi[:, :, :], wg[:, :, :]).then_inc(sem(f"{s}_wg_hi"), 1)

                def w_hi_f(j, u):
                    act.wait_ge(sem(f"{s}_wf_loaded{u}"), since(s, f"wf_loaded{u}") + loads(j, u, 16))
                    act.wait_ge(sem(f"{s}_down"), since(s, "down") + (2 * j - 2 if not isinstance(j, int) or j else 0))
                    s_.copy(wf_hi[:, u, :], wf[:, u, :]).then_inc(sem(f"{s}_w_hi"), 1)

                w_hi_f(0, 0)
                act.wait_ge(sem(f"{s}_shifted"), since(s, "shifted") + 1)
                s_.activation(ex[:, :, :], lg[:, :, :], ACT.Exp).then_inc(sem(f"{s}_ex"), 1)

                def tile(j, u, more):
                    for half in range(2):
                        k = 2 * j + half
                        b = half
                        act.wait_ge(sem(f"{s}_g"), since(s, "g") + k + 1)
                        act.wait_ge(sem(f"{s}_gu"), since(s, "gu") + k)
                        s_.activation(sg[:, b, :], ps[:, 0, :], ACT.Silu).then_inc(sem(f"{s}_silu"), 1)
                        if half == 0 and more:
                            w_hi_f(j + 1, 1 - u)
                        act.wait_ge(sem(f"{s}_h"), since(s, "h") + k + 1)
                        act.wait_ge(sem(f"{s}_down"), since(s, "down") + k)
                        s_.copy(h_hi[:, b, :], hf[:, b, :]).then_inc(sem(f"{s}_h_hi"), 1)

                with act.Fori(0, NJ // 2) as i:
                    for u in range(2):
                        tile(2 * i + u, u, True)
                tile(NJ - 1, 0, False)
                y_out(s, sem(f"{s}_down"), since(s, "down") + 2 * NJ)

            if "f" in STAGES:
                ffn("f")
            if "b" in STAGES:
                norm("b")
                act.wait_ge(sem("b_consts"), 48)
                s_.copy(wvb_hi[:, :, :], wvb[:, :, :]).then_inc(sem("b_wv_hi"), 1)

                def w_hi_b(g):
                    act.wait_ge(sem("wb_loaded"), 16 * (g + 1))
                    after(act, "b_proj", 6 * g)
                    s_.copy(wb_hi[:, :, :], wb[:, :, :]).then_inc(sem("b_w_hi"), 1)

                def raw_b(n, piece):
                    act.wait_ge(sem("b_proj"), n + 1)
                    after(act, "b_rot", n - 1)
                    s_.copy(raw[:, piece % 2, :], ps[:, 7, :]).then_inc(sem("b_raw"), 1)

                def high_b(n, g, kp, piece):
                    act.wait_ge(sem("b_rot"), n + 1)
                    half = piece % 2
                    at = slice(HALF * half, HALF * half + HALF)
                    if piece < 2:
                        after(act, "b_scores", 32 * g - 32)
                        ins = s_.copy(kh[:, kp, 0, at], ra[:, half, :])
                    else:
                        pair = piece // 2 - 1
                        after(act, "b_scores", 32 * g - 16 + 16 * pair)
                        s_.copy(qh[0:64, pair, 0, at], ra[0:64, half, :])
                        ins = s_.copy(qh[64:128, pair, 1, at], ra[64:128, half, :])
                    ins.then_inc(sem("b_hi"), 1)

                def v_hi_b(g, gp):
                    s_.copy(vst[:, gp, :, 0:DB], vb[:, g, :, :]).then_inc(sem("b_v_hi"), 1)

                def exp_b(h, par, i):
                    st = NT * h + i
                    t = SCORE_TILES[i]
                    act.wait_ge(sem("b_max"), st + 1)
                    after(act, "b_inv", st - 2 * NT + 1)
                    after(act, "b_turned", CHB * (h - 2) + 8 if t >= 4 else CHB * (h - 1) + 9 + t)
                    b = 2 * (i % 2)
                    s_.activation(pb(par, t), ps[:, b:b + 2, :].rearrange("p b k -> p (b k)")[:, 0:P * (t + 1)],
                                  ACT.Exp, bias=nmb[:, par, i:i + 1],
                                  accum_out=rsb[:, par, i:i + 1]).then_inc(sem("b_exp"), 1)

                def pt_hi_b(h, s):
                    c = CHB * h + s
                    first, n = chunk_columns(s)
                    at = slice(P * first, P * first + P * n)
                    act.wait_ge(sem("b_turned"), c + 1)
                    after(act, "b_prod", c - 2)
                    s_.copy(pt_hi[:, s % 3, at], ps[:, 4 + s % 2, at]).then_inc(sem("b_pt_hi"), 1)

                def o_low_b(h, bank):
                    act.wait_ge(sem("b_prod"), CHB * h + (8 if bank == 6 else CHB))
                    after(act, "b_ot", 2 * h + bank - 6)
                    s_.copy(o_low[:, :], ps[64:128, bank, :]).then_inc(sem("b_o_low"), 1)

                def head(g, gp, hh):
                    for kind, dh, i in steps(("exp", "pt_hi", "o_low", "raw", "high"), g, hh):
                        h = QPG * g + hh + dh
                        piece = 6 * (g + 1 + dh) + i
                        if kind == "exp":
                            exp_b(h, (hh + dh) % 2, i)
                        elif kind == "pt_hi":
                            pt_hi_b(h, i)
                        elif kind == "o_low":
                            o_low_b(h, 6 + i)
                        elif kind == "raw":
                            raw_b(piece, i)
                        elif kind == "high":
                            high_b(piece, g + 1 + dh, (gp + 1 + dh) % 2, i)
                        if hh == QPG - 1 and not (isinstance(g, int) and not 0 <= g < NG - 1):
                            if (kind, i) == ("exp", V_SPLIT_AT - 1):
                                v_hi_b(g + 1, 1 - gp)
                            if (kind, i) == ("raw", 5) and not (isinstance(g, int) and g >= NG - 2):
                                w_hi_b(g + 2)

                def group(g, gp):
                    for hh in range(QPG):
                        head(g, gp, hh)

                w_hi_b(0)
                for t in range(NT):
                    act.wait_ge(sem("b_v"), t + 1)
                    s_.copy(vb[:, :, t, :], ps[:, t % 4, :].rearrange("p (g d) -> p g d", g=NG)).then_inc(sem("b_vout"), 1)
                raw_b(0, 0)
                for piece in range(6):
                    if piece < 5:
                        raw_b(piece + 1, piece + 1)
                    high_b(piece, 0, 0, piece)
                act.wait_ge(sem("b_vout"), NT)
                v_hi_b(0, 0)
                w_hi_b(1)
                all_groups(act, group, head)
                out_proj("b")
                y_out("b", sem("b_oacc"), HA)
            if "g" in STAGES:
                ffn("g")

        @block.tensor
        def _(pe):
            t_ = nc.tensor

            def mm(o, l, r, start=True, stop=True):
                return t_.matmul(o, l, r, start=start, stop=stop)

            def norm(s):
                for q in range(2 * NC):
                    for m in range(4):
                        t = 4 * (q % 2) + m
                        pe.wait_ge(sem(f"{s}_z"), since(s, "z") + t + 1)
                        last = t_.transpose(ps[:, q, P * m:P * m + P], z[:, t, P * (q // 2):P * (q // 2) + P],
                                            idf[:, :])
                    last.then_inc(sem(f"{s}_zt"), 1)

            def turn_back(s):
                for n in range(NT // 2):
                    for m in range(2):
                        t = 2 * n + m
                        for c in range(NC):
                            pe.wait_ge(sem(f"{s}_yt"), since(s, "yt") + 2 * c + t // 4 + 1)
                            last = t_.transpose(ps[:, n, D * m + P * c:D * m + P * c + P],
                                                yt[:, 2 * c + t // 4, P * (t % 4):P * (t % 4) + P], idf[:, :])
                    last.then_inc(sem(f"{s}_y_turned"), 1)

            def three(o, lhs, rhs, first=True, last=True):
                terms = [(lhs(c, a), rhs(c, b)) for c in range(NC) for a, b in ((0, 0), (0, 1), (1, 0))]
                for n, (l, r) in enumerate(terms):
                    ins = mm(o, l, r, start=first and n == 0, stop=last and n == len(terms) - 1)
                return ins

            def xt(part, c, a, n):
                return (xt_hi, xt_lo)[part][:, c, PAD + a:PAD + a + n]

            pe.wait_ge(sem("ident_loaded"), 32)
            norm("a")
            pe.wait_ge(sem("a_consts"), 64)

            def lora(h, u, busy):
                pe.wait_ge(sem(f"wa_loaded{u}"), loads(h, u, 32))
                for wait in busy:
                    wait()
                for c in range(NC):
                    last = mm(ps[:, c, 0:3 * P], la[:, c, :], lb[:, u, :])
                last.then_inc(sem("a_lora"), 1)

            def qk(h, u, piece):
                w = piece // 2
                at = HALF * (piece % 2)
                three(ps[:, piece % 2, :],
                      lambda c, a: (wqk_hi, wqk_lo)[a][:, u, c, w, :],
                      lambda c, b: xt(b, c, at, HALF)).then_inc(sem("a_qk"), 1)

            def values(i, piece):
                for m in range(2 if piece < 4 else 1):
                    t = 2 * piece + m
                    last = three(ps[:, piece % 2, 2 * P * m:2 * P * m + 2 * P],
                                 lambda c, a: xt(a, c, P * t - PAD, P),
                                 lambda c, b: (wv_hi, wv_lo)[b][:, c, :, :].rearrange("p u d -> p (u d)"))
                last.then_inc(sem("a_v"), 1)

            def head_a(i, h, u, ahead1, ahead2):
                pe.wait_ge(sem("a_rot"), 4 * h + 4)
                pe.wait_ge(sem("a_exp"), 4 * h)
                for n in range(4):
                    if n == 2:
                        pe.wait_ge(sem("a_ot"), 2 * h)
                    bank = 2 + (n + 2 * u) % 4
                    for m in range(2):
                        t = 2 * n + m
                        o = ps[:, bank, KW * m:KW * m + KW]
                        mm(o, qr[:, u, P * t:P * t + P], kr[:, u, P * t:P * t + KW], True, False)
                        last = mm(o, idb[:, :], maska[:, 0 if t == 0 else 1, :], False, True)
                    last.then_inc(sem("a_scores"), 1)
                if ahead1:
                    pe.wait_ge(sem("a_w_lo"), h + 2)
                    if u == 0:
                        pe.wait_ge(sem("a_vout"), 5 * i + 5)
                    for piece in range(4):
                        if piece >= 2:
                            pe.wait_ge(sem("a_mul"), 4 * h + 4 + piece - 1)
                        qk(h + 1, 1 - u, piece)
                if ahead2:
                    lora(h + 2, u, [lambda: pe.wait_ge(sem("a_mul"), 4 * h + 8)])
                for n in range(5):
                    if n < 4:
                        pe.wait_ge(sem("a_pn"), 4 * h + n + 1)
                        if n < 2:
                            pe.wait_ge(sem("a_pt"), 4 * h)
                        else:
                            pe.wait_ge(sem("a_pt"), 4 * h + n - 1)
                        for m in range(4):
                            last = t_.transpose(ps[:, 6 + n % 2, P * m:P * m + P],
                                                pa[:, 2 * n + m // 2, P * (m % 2):P * (m % 2) + P], idf[:, :])
                        last.then_inc(sem("a_turned"), 1)
                    if n > 0:
                        n0 = n - 1
                        pe.wait_ge(sem("a_pt"), 4 * h + n0 + 1)
                        if n0 == 0:
                            pe.wait_ge(sem("a_vout"), 5 * i + 5)
                        for m in range(2):
                            t = 2 * n0 + m
                            o = ps[:, 2 + 2 * u + t // 4, P * (t % 4):P * (t % 4) + P]
                            for b in range(2):
                                last = mm(o, va[:, t + b, u, :], pta[:, n0 % 2, P * (2 * m + b):P * (2 * m + b) + P],
                                          b == 0, b == 1)
                        last.then_inc(sem("a_pv"), 1)
                if u == 1 and ahead2:
                    pe.wait_ge(sem("a_w_lo"), h + 3)
                    for piece in range(5):
                        if piece >= 2:
                            pe.wait_ge(sem("a_vout"), 5 * i + 5 + piece - 1)
                        values(i + 1, piece)

            for q in range(2 * NC):
                pe.wait_ge(sem("a_xt_lo"), q + 1)
            lora(0, 0, [])
            lora(1, 1, [lambda: pe.wait_ge(sem("a_weff"), 1)])
            pe.wait_ge(sem("a_w_lo"), 2)
            pe.wait_ge(sem("a_weff"), 2)
            for piece in range(5):
                if piece >= 2:
                    pe.wait_ge(sem("a_vout"), piece - 1)
                values(0, piece)
            pe.wait_ge(sem("a_vout"), 5)
            for piece in range(4):
                if piece >= 2:
                    pe.wait_ge(sem("a_mul"), piece - 1)
                qk(0, 0, piece)
            with pe.Fori(0, HA // 2 - 1) as i:
                for u in range(2):
                    head_a(i, 2 * i + u, u, True, True)
            head_a(HA // 2 - 1, HA - 2, 0, True, False)
            head_a(HA // 2 - 1, HA - 1, 1, False, False)

            def out_proj(s, has_lora):
                pe.wait_ge(sem(f"{s}_ot"), OT_ALL[s])
                if has_lora:
                    pe.wait_ge(sem(f"{s}_ob_loaded"), 16)

                def low_rank(h, u):
                    if has_lora:
                        pe.wait_ge(sem(f"{s}_wo_loaded{u}"), loads(h, u, 32))
                        pe.wait_ge(sem(f"{s}_woe"), h - 1 if not isinstance(h, int) or h else 0)
                        mm(ps[:, u, 0:D], oa[:, u, :], ob[:, :]).then_inc(sem(f"{s}_ol"), 1)

                def step(h, u, first, last):
                    pe.wait_ge(sem(f"{s}_wo_lo"), h + 1)
                    pe.wait_ge(sem(f"{s}_ot_lo"), h + 1)
                    for c in range(NC):
                        for half in range(2):
                            at = slice(HALF * half, HALF * half + HALF)
                            for n, (a, b) in enumerate(((0, 0), (0, 1), (1, 0))):
                                ins = mm(ps[:, 4 + 2 * c + half, :], (wo_hi, wo_lo)[a][:, u, P * c:P * c + P],
                                         (ot_hi, ot_lo)[b][:, u, at], first and n == 0, last and n == 2)
                    ins.then_inc(sem(f"{s}_oacc"), 1)

                low_rank(0, 0)
                low_rank(1, 1)
                step(0, 0, True, False)
                low_rank(2, 0)
                step(1, 1, False, False)
                low_rank(3, 1)
                with pe.Fori(1, HA // 2 - 1) as i:
                    for u in range(2):
                        step(2 * i + u, u, False, False)
                        low_rank(2 * i + u + 2, u)
                step(HA - 2, 0, False, False)
                step(HA - 1, 1, False, True)

            out_proj("a", True)
            turn_back("a")

            def ffn(s):
                norm(s)
                for q in range(2 * NC):
                    pe.wait_ge(sem(f"{s}_xt_lo"), since(s, "xt_lo") + q + 1)
                pe.wait_ge(sem(f"{s}_wg_lo"), since(s, "wg_lo") + 1)
                for t in range(NT):
                    last = three(ps[:, 3, NE * t:NE * t + NE],
                                 lambda c, a: xt(a, c, P * t, P),
                                 lambda c, b: (wg_hi, wg_lo)[b][:, c, :])
                last.then_inc(sem(f"{s}_logits"), 1)
                pe.wait_ge(sem(f"{s}_cwb"), since(s, "cwb") + 1)
                for t in range(NT):
                    last = t_.transpose(ps[:, 3, :].bitcast(BF16)[:, P * t:P * t + P], cwb[:, t, :], idb[:, :])
                last.then_inc(sem(f"{s}_cwt_turned"), 1)
                pe.wait_ge(sem(f"{s}_cwt"), since(s, "cwt") + 1)

                def up(j, u, half):
                    k = 2 * j + half
                    if half == 0:
                        pe.wait_ge(sem(f"{s}_w_lo"), since(s, "w_lo") + j + 1)
                    at = HALF * half
                    pe.wait_ge(sem(f"{s}_silu"), since(s, "silu") + k)
                    three(ps[:, 0, :], lambda c, a: (wf_hi, wf_lo)[a][:, u, P * c:P * c + P],
                          lambda c, b: xt(b, c, at, HALF)).then_inc(sem(f"{s}_g"), 1)
                    pe.wait_ge(sem(f"{s}_h"), since(s, "h") + k)
                    three(ps[:, 1, :], lambda c, a: (wf_hi, wf_lo)[a][:, u, D + P * c:D + P * c + P],
                          lambda c, b: xt(b, c, at, HALF)).then_inc(sem(f"{s}_u"), 1)
                    mm(ps[:, 2, :], sel[:, P * j:P * j + P] if isinstance(j, int) else sel[:, bass.ts(j, P)],
                       cwt[:, at:at + HALF]).then_inc(sem(f"{s}_c"), 1)

                def down(j, u, half, first, last):
                    k = 2 * j + half
                    pe.wait_ge(sem(f"{s}_h_lo"), since(s, "h_lo") + k + 1)
                    for c in range(NC):
                        for n, (a, b) in enumerate(((0, 0), (0, 1), (1, 0))):
                            ins = mm(ps[:, 4 + 2 * c + half, :],
                                     (wf_hi, wf_lo)[a][:, u, 2 * D + P * c:2 * D + P * c + P],
                                     (h_hi, h_lo)[b][:, half, :], first and n == 0, last and n == 2)
                    ins.then_inc(sem(f"{s}_down"), 1)

                up(0, 0, 0)
                up(0, 0, 1)
                down(0, 0, 0, True, False)
                up(1, 1, 0)
                down(0, 0, 1, True, False)
                up(1, 1, 1)
                down(1, 1, 0, False, False)
                with pe.Fori(1, NJ // 2) as i:
                    for u in range(2):
                        j = 2 * i + u
                        up(j, u, 0)
                        down(j - 1, 1 - u, 1, False, False)
                        up(j, u, 1)
                        down(j, u, 0, False, False)
                j = NJ - 1
                up(j, 0, 0)
                down(j - 1, 1, 1, False, False)
                up(j, 0, 1)
                down(j, 0, 0, False, True)
                down(j, 0, 1, False, True)
                turn_back(s)

            if "f" in STAGES:
                ffn("f")
            if "b" in STAGES:
                norm("b")
                for q in range(2 * NC):
                    pe.wait_ge(sem("b_xt_lo"), q + 1)
                pe.wait_ge(sem("b_wv_lo"), 1)
                for t in range(NT):
                    if t >= 4:
                        pe.wait_ge(sem("b_vout"), t - 3)
                    three(ps[:, t % 4, :], lambda c, a: xt(a, c, P * t, P),
                          lambda c, b: (wvb_hi, wvb_lo)[b][:, c, :]).then_inc(sem("b_v"), 1)
                pe.wait_ge(sem("b_vout"), NT)

                def proj(n, g, piece):
                    if piece == 0:
                        pe.wait_ge(sem("b_w_lo"), g + 1)
                    after(pe, "b_cos", n)
                    at = HALF * (piece % 2)
                    col = (2 * P, 0, P)[piece // 2]
                    three(ps[:, 7, :], lambda c, a: (wb_hi, wb_lo)[a][:, c, col:col + P],
                          lambda c, b: xt(b, c, at, HALF)).then_inc(sem("b_proj"), 1)

                def scores(h, g, kp, hh, i):
                    st = NT * h + i
                    t = SCORE_TILES[i]
                    after(pe, "b_exp", st - 1)
                    if i == 0:
                        pe.wait_ge(sem("b_lo"), 6 * g + (4 if hh < 2 else 6))
                    bank = 2 * (i % 2)
                    for n0 in range(0, t + 1, 4):
                        w = min(4, t + 1 - n0) * P
                        o = ps[:, bank + n0 // 4, 0:w]
                        for b in range(2):
                            mm(o, qh[:, hh // 2, hh % 2, P * t:P * t + P], kh[:, kp, b, P * n0:P * n0 + w],
                               b == 0, b == 1 and n0 + 4 <= t)
                    mm(ps[:, bank + t // 4, P * (t % 4):P * (t % 4) + P],
                       idb[:, :], maskb[:, :], False, True).then_inc(sem("b_scores"), 1)

                def turn(h, par, s):
                    after(pe, "b_pt_lo", CHB * h + s - 1)
                    if s == 0:
                        pe.wait_ge(sem("b_pn"), NT * h + 4)
                    if s == 8:
                        pe.wait_ge(sem("b_pn"), NT * h + NT)
                    block = s % 8
                    first, n = chunk_columns(s)
                    base = 4 if s < 8 else 0
                    for m in range(first, first + n):
                        last = t_.transpose(ps[:, 4 + s % 2, P * m:P * m + P],
                                            pb(par, base + m)[:, P * block:P * block + P], idf[:, :])
                    last.then_inc(sem("b_turned"), 1)

                def products(h, g, gp, hh, s):
                    c = CHB * h + s
                    first, n = chunk_columns(s)
                    bank = 6 if s < 8 else 7
                    pe.wait_ge(sem("b_pt_lo"), c + 1)
                    if s == 0:
                        after(pe, "b_ot", 2 * h - 1)
                        if hh == 0:
                            pe.wait_ge(sem("b_v_lo"), g + 1)
                    if s == 8:
                        after(pe, "b_ot", 2 * h)
                        pe.wait_ge(sem("b_cos"), pieces_before(g, hh))
                    block = s % 8
                    at = slice(P * first, P * first + P * n)
                    mm(ps[:, bank, at], vst[:, gp, block, :], pt_hi[:, s % 3, at], block == 0, False)
                    mm(ps[:, bank, at], vst[:, gp, block, :], pt_lo[:, s % 3, at], False,
                       s in (7, 11)).then_inc(sem("b_prod"), 1)

                def head(g, gp, hh):
                    for kind, dh, i in steps(("scores", "turn", "products", "proj"), g, hh):
                        h = QPG * g + hh + dh
                        if kind == "scores":
                            scores(h, *head_at(g, gp, hh, dh), i)
                        elif kind == "turn":
                            turn(h, (hh + dh) % 2, i)
                        elif kind == "products":
                            products(h, *head_at(g, gp, hh, dh), i)
                        elif kind == "proj":
                            after(pe, "b_ot", 2 * (QPG * g + hh))
                            proj(6 * (g + 1 + dh) + i, g + 1 + dh, i)

                def group(g, gp):
                    for hh in range(QPG):
                        head(g, gp, hh)

                for piece in range(6):
                    proj(piece, 0, piece)
                all_groups(pe, group, head)
                out_proj("b", False)
                turn_back("b")
            if "g" in STAGES:
                ffn("g")


SCORE_TILES = [7, 6, 5, 4, 0, 1, 2, 3]
DUE = {
    "scores": [-9604, -8246, -5656, -5177, -4269, -2735, -2519, -819],
    "max": [-9513, -7786, -7285, -5999, -3761, -2590, -1705, -317],
    "exp": [-9350, -6659, -5353, -4292, -3357, -2734, -1662, -750],
    "inv": [-7753, -7198, -5204, -2699, -2167, -1102, 709, 1621],
    "norm": [-10250, -8130, -7000, -6534, -2740, -2297, -1878, -1871],
    "turn": [471, 846, 3172, 3298, 4350, 4567, 5026, 5290, 6828, 7453, 8399, 9545],
    "pt_hi": [-473, 271, 725, 2422, 3803, 4130, 4992, 5675, 5950, 7772, 8729, 9052],
    "pt_lo": [780, 1317, 2224, 2454, 3371, 3561, 4702, 5835, 7477, 8744, 9756, 10306],
    "products": [3152, 3399, 4467, 4924, 5283, 6337, 7275, 7817, 9313, 9551, 10553, 11503],
    "o_low": [7920, 10343],
    "o_add": [9767, 12122],
    "proj": [3894, 5795, 13390, 24036, 33579, 36174],
    "raw": [3311, 7148, 13222, 23175, 33744, 35881],
    "cos": [3762, 7568, 15289, 22808, 33776, 37408],
    "rotate": [2290, 5094, 15908, 19771, 32046, 34746],
    "high": [11696, 12123, 21683, 27019, 39220, 42428],
    "low": [12394, 21494, 24820, 28481, 42391, 45953],
}
PIECES = ("proj", "raw", "cos", "rotate", "high", "low")


def steps(kinds, g, hh):
    found = []
    for kind in kinds:
        piece = kind in PIECES
        for n, due in enumerate(DUE[kind]):
            if piece:
                behind, at = divmod(due - 10000 * hh, 10000 * QPG)
                if at >= 10000:
                    continue
                exists = not isinstance(g, int) or 0 <= g + behind * -1 < NG - 1
            else:
                behind, at = divmod(due, 10000)
                exists = not isinstance(g, int) or 0 <= QPG * g + hh - behind < QPG * NG
            if exists:
                found.append((at, kind, -behind, n))
    return [step[1:] for step in sorted(found)]


def head_at(g, gp, hh, dh):
    dg, hh = divmod(hh + dh, QPG)
    return g + dg, (gp + dg) % 2, hh


def pieces_before(g, hh):
    done = sum(due < 10000 * hh + DUE["products"][8] for due in DUE["proj"])
    return 6 * g + 6 + (0 if isinstance(g, int) and g == NG - 1 else done)


def chunk_columns(slot):
    first = max(0, slot - 4) if slot < 8 else slot - 8
    return first, 4 - first


V_SPLIT_AT, W_LO_AT = 3, 6

OT_ALL = {"a": 2 * HA, "b": 2 * QPG * NG}


F_TOTAL = {"ln": 2 * NT, "var": 1, "rstd": 1, "z": NT, "zt": 4, "xt_hi": 4, "xt_lo": 4,
           "consts": 48, "wg_hi": 1, "wg_lo": 1, "logits": 1, "route": 15, "shifted": 1, "ex": 1,
           "cwb": 1, "cwt_turned": 1, "cwt": 1,
           "wf_loaded0": 16 * (NJ - NJ // 2), "wf_loaded1": 16 * (NJ // 2), "w_hi": NJ, "w_lo": NJ,
           "g": 2 * NJ, "u": 2 * NJ, "c": 2 * NJ, "silu": 2 * NJ, "gu": 2 * NJ, "h": 2 * NJ,
           "h_hi": 2 * NJ, "h_lo": 2 * NJ, "down": 2 * NJ,
           "yt": 4, "y_turned": 4, "added": 4}


def since(s, name):
    return F_TOTAL[name] if s == "g" else 0


def loads(n, u, each):
    return (each // 2) * n + each - (each // 2) * u


def rope_table(half, copies, scale, by_source):
    inv = (1.0 / 10000.0 ** (np.arange(half, dtype=np.float32) / half)).astype(np.float32)
    ang = (np.arange(T, dtype=np.float32)[:, None] * inv[None, :]).astype(np.float32)
    cos = np.cos(ang.astype(np.float64)).T
    sin = np.sin(ang.astype(np.float64)).T
    c = np.concatenate([cos, cos] * copies)
    s = np.concatenate(([sin, -sin] if by_source else [-sin, sin]) * copies)
    return np.ascontiguousarray(np.stack([c, s], 1) * scale).astype(np.float32)


def kernel(**inputs):
    import ml_dtypes
    import concourse.bacc as _bacc
    from concourse.bass_utils import run_bass_kernel_spmd as _run

    bf16 = ml_dtypes.bfloat16
    a = {k.replace("L0_", ""): np.asarray(v) for k, v in inputs.items()}
    f = np.float32
    m = {}
    m["x"] = a["attn_a_x"].reshape(NT, P, D)
    m["idf"] = np.eye(P, dtype=f)
    m["idb"] = np.eye(P, dtype=f).astype(bf16)
    m["norm_w"] = a["attn_a_norm_w"].reshape(NC, P).T
    w = np.stack([a["attn_a_wq"], a["attn_a_wk"], a["attn_a_wv"]]).reshape(3, HA, P, NC, P)
    m["wa"] = w.transpose(1, 4, 3, 0, 2)
    m["la"] = np.concatenate([a["attn_a_qA"], a["attn_a_kA"], a["attn_a_vA"]]).reshape(3 * RANK, NC, P)
    lb = np.zeros((HA, 3, RANK, 3, P), f)
    for n, key in enumerate(("qB", "kB", "vB")):
        lb[:, n, :, n, :] = a[f"attn_a_{key}"].reshape(HA, P, RANK).transpose(0, 2, 1)
    m["lb"] = lb.reshape(HA, 3 * RANK, 3 * P)
    m["wo_a"] = a["attn_a_wo"].T.reshape(HA, P, D)
    m["oa"] = a["attn_a_oA"].reshape(RANK, HA, P).transpose(1, 0, 2)
    m["ob"] = a["attn_a_oB"].T
    m["rope_a"] = rope_table(64, 1, 128.0 ** -0.25, True)
    m["rope_b"] = rope_table(32, 2, 64.0 ** -0.25, False)
    q, k = np.arange(P)[:, None], np.arange(KW)[None, :]
    seen = (k > q) & (k <= q + WIN)
    NEG = -1e30
    m["maska"] = np.where(np.stack([seen & (k >= WIN), seen], 1), 0.0, NEG).astype(bf16)
    m["maskb"] = np.where(np.arange(P)[None, :] <= q, 0.0, NEG).astype(bf16)
    rows = NJ * P - NE * I_E - I_S
    pad = np.zeros((rows, D), f)
    gate = np.concatenate([a["ffn_w_gate"].reshape(-1, D), a["ffn_sw_gate"], pad]).reshape(NJ, P, NC, P)
    upw = np.concatenate([a["ffn_w_up"].reshape(-1, D), a["ffn_sw_up"], pad]).reshape(NJ, P, NC, P)
    dn = np.concatenate([a["ffn_w_down"].transpose(0, 2, 1).reshape(-1, D), a["ffn_sw_down"].T, pad])
    m["wf"] = np.concatenate([gate.transpose(0, 3, 2, 1).reshape(NJ, P, D),
                              upw.transpose(0, 3, 2, 1).reshape(NJ, P, D), dn.reshape(NJ, P, D)], 2)
    m["wg"] = a["ffn_gate_w"].T.reshape(NC, P, NE).transpose(1, 0, 2)
    expert = np.minimum(np.arange(NJ * P) // I_E, NE)
    one = (np.arange(NW)[:, None] == expert[None, :]).astype(f)
    m["sel"] = np.concatenate([one, one, one, np.zeros((P - 3 * NW, NJ * P), f)]).astype(bf16)
    m["iota"] = np.broadcast_to(np.arange(NE, dtype=f), (P, NT * TOPK, NE))
    wq = a["attn_b_Wq"].reshape(NC, P, NG, QPG * DB)
    wk = a["attn_b_Wk"].reshape(NC, P, NG, DB)
    m["wb"] = np.concatenate([wq, wk, wk], 3).transpose(2, 1, 0, 3)
    m["wvb"] = a["attn_b_Wv"].reshape(NC, P, NG * DB).transpose(1, 0, 2)
    m["wo_b"] = a["attn_b_Wo"].reshape(HA, P, D)

    nc = _bacc.Bacc("TRN2", target_bir_lowering=False, num_devices=1)
    arrays, args = {}, {}
    for name, v in m.items():
        arrays[f"in_{name}"] = np.ascontiguousarray(v)
        args[name] = nc.dram_tensor(f"in_{name}", v.shape, mybir.dt.from_np(v.dtype), kind="ExternalInput").ap()
    out = nc.dram_tensor("out", (NT, P, D), F32, kind="ExternalOutput").ap()
    build(nc, args, out)
    r = _run(nc, [arrays], core_ids=[0])
    return r.results[0]["out"].reshape(1, T, D)
```

```python
from contextlib import ExitStack

import numpy as np

import concourse.bass as bass
from concourse import mybir

F32 = mybir.dt.float32
F32R = mybir.dt.float32r
BF16 = mybir.dt.bfloat16
U32 = mybir.dt.uint32
ALU = mybir.AluOpType
ACT = mybir.ActivationFunctionType
AX = mybir.AxisListType

P = 128
T = 1024
NT = T // P
D = 256
NC = D // P
HALF = 512
LN_EPS = 1e-5
RMS_EPS = 1e-6

HA = 16
WIN = 64
PAD = WIN
TP = PAD + T + PAD
NV = TP // P
KW = WIN + P
RANK = 16
LORA_SCALE = 1.0 / RANK

NG = 8
QPG = 4
DB = 64
CHB = 12

NE = 16
TOPK = 4
I_E = 176
I_S = 352
NJ = (NE * I_E + I_S + P - 1) // P
N_SHARED = I_S // P
NW = NE + 1


class Sems:

    def __init__(self, nc, ctx):
        self.nc, self.ctx, self.made = nc, ctx, {}

    def __call__(self, name):
        if name.startswith("g_"):
            name = "f" + name[1:]
        if name not in self.made:
            self.made[name] = self.ctx.enter_context(self.nc.semaphore(name))
        return self.made[name]


def build(nc, d, out):
    ctx = ExitStack()
    with ctx:
        def sb(name, shape, dt=F32, c=ctx):
            return c.enter_context(nc.sbuf_tensor(name, shape, dt))

        sem = Sems(nc, ctx)
        ps = ctx.enter_context(nc.psum_tensor("ps", [P, 8, HALF], F32))

        x = sb("x_res", [P, NT, D])
        z = sb("z", [P, NT, D])
        xt_hi = sb("xt_hi", [P, NC, TP], F32R)
        xt_lo = sb("xt_lo", [P, NC, TP], F32R)
        ot = sb("ot", [P, HA, T])
        yt = sb("yt", [P, 2 * NC, HALF])
        idf = sb("idf", [P, P])
        idb = sb("idb", [P, P], BF16)
        norm_w = sb("norm_w", [P, NC])
        stats = sb("stats", [P, NT, 6])
        mv = sb("mv", [P, NT, 2])
        var = sb("var", [P, 2, NT])
        rstd = sb("rstd", [P, 2, NT])
        negh = sb("negh", [P, 2, NT])
        rope = sb("rope", [P, 2, T])
        ra = sb("ra", [P, 2, HALF])
        rb = sb("rb", [P, 2, HALF])

        own = ExitStack()
        with own:
            wa = sb("wa", [P, 2, NC, 3, P], c=own)
            lb = sb("lb", [3 * RANK, 2, 3 * P], c=own)
            la = sb("la", [3 * RANK, NC, P], c=own)
            wef = sb("wef", [P, 2, NC, 3, P], c=own)
            wqk_hi = sb("wqk_hi", [P, 2, NC, 2, P], F32R, own)
            wqk_lo = sb("wqk_lo", [P, 2, NC, 2, P], F32R, own)
            wv_hi = sb("wv_hi", [P, NC, 2, P], F32R, own)
            wv_lo = sb("wv_lo", [P, NC, 2, P], F32R, own)
            qr = sb("qr", [P, 2, T], c=own)
            kr = sb("kr", [P, 2, PAD + T], c=own)
            va = sb("va", [P, 2, NV, 2, P], c=own)
            pa = sb("pa", [P, NT, 2 * P], c=own)
            pta = sb("pta", [P, 2, HALF], c=own)
            nmax = sb("nmax", [P, NT], c=own)
            rsum = sb("rsum", [P, NT], c=own)
            rinv = sb("rinv", [P, NT], c=own)
            maska = sb("maska", [P, 2, KW], BF16, own)
        own = ExitStack()
        with own:
            wo = sb("wo", [P, 2, D], c=own)
            oa = sb("oa", [RANK, 2, P], c=own)
            ob = sb("ob", [RANK, D], c=own)
            woe = sb("woe", [P, 2, D], c=own)
            wo_hi = sb("wo_hi", [P, 2, D], F32R, own)
            wo_lo = sb("wo_lo", [P, 2, D], F32R, own)
            ot_hi = sb("ot_hi", [P, 2, T], F32R, own)
            ot_lo = sb("ot_lo", [P, 2, T], F32R, own)
        own = ExitStack()
        with own:
            wf = sb("wf", [P, 2, 3 * D], c=own)
            wf_hi = sb("wf_hi", [P, 2, 3 * D], F32R, own)
            wf_lo = sb("wf_lo", [P, 2, 3 * D], F32R, own)
            sg = sb("sg", [P, 2, HALF], c=own)
            gu = sb("gu", [P, 2, HALF], c=own)
            hf = sb("hf", [P, 2, HALF], c=own)
            h_hi = sb("h_hi", [P, 2, HALF], F32R, own)
            h_lo = sb("h_lo", [P, 2, HALF], F32R, own)
            sel = sb("sel", [P, NJ * P], BF16, own)
            wg = sb("wg", [P, NC, NE], c=own)
            wg_hi = sb("wg_hi", [P, NC, NE], F32R, own)
            wg_lo = sb("wg_lo", [P, NC, NE], F32R, own)
            lgs = sb("lgs", [NE, T], c=own)
            lg = sb("lg", [P, NT, NE], c=own)
            ex = sb("ex", [P, NT, NE], c=own)
            top = sb("top", [P, NT, 8], c=own)
            topi = sb("topi", [P, NT, 8], U32, own)
            topf = sb("topf", [P, NT, 8], c=own)
            iota = sb("iota", [P, NT * TOPK, NE], c=own)
            hit = sb("hit", [P, NT * TOPK, NE], c=own)
            chosen = sb("chosen", [P, NT, NE], c=own)
            cw = sb("cw", [P, NT, NW], c=own)
            cwr = sb("cwr", [P, NT, NW], c=own)
            csum = sb("csum", [P, NT], c=own)
            cinv = sb("cinv", [P, NT], c=own)
            cwb = sb("cwb", [P, NT, P], BF16, own)
            cwt = sb("cwt", [P, T], BF16, own)
        own = ExitStack()
        with own:
            wb = sb("wb", [P, NC, 3 * P], c=own)
            wb_hi = sb("wb_hi", [P, NC, 3 * P], F32R, own)
            wb_lo = sb("wb_lo", [P, NC, 3 * P], F32R, own)
            wvb = yt[:, 0:NC, :]
            vb = ot[:, :, :].rearrange("p (g k) (t d) -> p g k t d", k=2, d=DB)[:, :, 1, 0:NT, :]
            raw = sb("raw", [P, 2, HALF], c=own)
            qh = sb("qh", [P, 2, 2, T], F32R, own)
            kh = sb("kh", [P, 2, 2, T], F32R, own)
            wvb_hi = qh[:, 1, 0, :].rearrange("p (c n) -> p c n", c=NC)
            wvb_lo = qh[:, 1, 1, :].rearrange("p (c n) -> p c n", c=NC)
            vst = sb("vst", [P, 2, NT, 2 * DB], F32R, own)
            pb_low = sb("pb_low", [P, 6, P], c=own)
            pb_odd = sb("pb_odd", [P, 26, P], c=own)
            pt_hi = sb("pt_hi", [P, 3, HALF], F32R, own)
            pt_lo = sb("pt_lo", [P, 3, HALF], F32R, own)
            o_low = sb("o_low", [DB, HALF], c=own)
            nmb = sb("nmb", [P, 2, NT], c=own)
            rsb = sb("rsb", [P, 2, NT], c=own)
            rib = sb("rib", [P, 2, NT], c=own)
            maskb = sb("maskb", [P, P], BF16, own)

        def pb(par, t):
            if t < 3:
                flat, at = pb_low[:, :, :].rearrange("p n k -> p (n k)"), (0, 1, 3)[t]
            elif t == 3:
                flat, at = yt[:, :, :].rearrange("p a n -> p (a n)"), 11
            elif par:
                flat, at = pb_odd[:, :, :].rearrange("p n k -> p (n k)"), (0, 5, 11, 18)[t - 4]
            elif t < 6:
                flat, at = yt[:, :, :].rearrange("p a n -> p (a n)"), (0, 5)[t - 4]
            else:
                flat, at = z[:, :, :].rearrange("p a n -> p (a n)"), (0, 7)[t - 6]
            return flat[:, P * at:P * (at + t + 1)]

        def after(engine, name, n):
            if not isinstance(n, int) or n > 0:
                engine.wait_ge(sem(name), n)

        def all_pairs(engine, head):
            for h in range(-3, 4):
                head(h // 2, h // 2 % 2, h % 2)
            with engine.Fori(1, HA // 4 - 1) as quad:
                for k in range(2):
                    for u in range(2):
                        head(2 * quad + k, k, u)
            for h in range(HA - 4, HA + 3):
                head(h // 2, h // 2 % 2, h % 2)

        def all_groups(engine, group):
            group(0, 0)
            group(1, 1)
            with engine.Fori(1, NG // 2 - 1) as i:
                for gp in range(2):
                    group(2 * i + gp, gp)
            group(NG - 2, 0)
            group(NG - 1, 1)

        block = ctx.enter_context(nc.Block())


        @block.sync
        def _(sp):
            for n in range(NT // 2):
                sp.dma_start(x[:, 2 * n:2 * n + 2, :],
                             d["x"][2 * n:2 * n + 2].rearrange("t p d -> p t d")).then_inc(sem(f"x_loaded{n}"), 16)
            sp.dma_start(idf[:, :], d["idf"]).then_inc(sem("ident_loaded"), 16)
            sp.dma_start(idb[:, :], d["idb"]).then_inc(sem("ident_loaded"), 16)
            sp.dma_start(norm_w[:, :], d["norm_w"]).then_inc(sem("ident_loaded"), 16)
            sp.dma_start(la[:, :, :], d["la"]).then_inc(sem("a_consts"), 16)
            sp.dma_start(maska[:, :, :], d["maska"]).then_inc(sem("a_consts"), 16)
            sp.dma_start(rope[:, :, :], d["rope_a"]).then_inc(sem("a_consts"), 16)

            def load_head(h, u, guard):
                if guard:
                    sp.wait_ge(sem("a_weff"), h - 1)
                sp.dma_start(wa[:, u, :, :, :], d["wa"][h]).then_inc(sem(f"wa_loaded{u}"), 16)
                sp.dma_start(lb[:, u, :], d["lb"][h]).then_inc(sem(f"wa_loaded{u}"), 16)

            load_head(0, 0, False)
            load_head(1, 1, False)
            with sp.Fori(1, HA // 2) as i:
                for u in range(2):
                    load_head(2 * i + u, u, True)

            def out_proj(s, w, lora):
                if s == "a":
                    sp.wait_ge(sem("a_weff"), HA)
                else:
                    sp.wait_ge(sem("b_rot"), 6 * NG)
                if lora:
                    sp.dma_start(ob[:, :], d["ob"]).then_inc(sem(f"{s}_ob_loaded"), 16)

                def load(h, u, guard):
                    if guard:
                        sp.wait_ge(sem(f"{s}_woe"), h - 1)
                    sp.dma_start(wo[:, u, :], d[w][h]).then_inc(sem(f"{s}_wo_loaded{u}"), 16)
                    if lora:
                        sp.dma_start(oa[:, u, :], d["oa"][h]).then_inc(sem(f"{s}_wo_loaded{u}"), 16)

                load(0, 0, False)
                load(1, 1, False)
                with sp.Fori(1, HA // 2) as i:
                    for u in range(2):
                        load(2 * i + u, u, True)

            def ffn(s, before):
                sp.wait_ge(sem(f"{before}_yt"), since(before, "yt") + 4)
                sp.dma_start(wg[:, :, :], d["wg"]).then_inc(sem(f"{s}_consts"), 16)
                sp.dma_start(sel[:, :], d["sel"]).then_inc(sem(f"{s}_consts"), 16)
                sp.dma_start(iota[:, :, :], d["iota"]).then_inc(sem(f"{s}_consts"), 16)

                def load(j, u, guard):
                    if guard:
                        sp.wait_ge(sem(f"{s}_w_hi"), since(s, "w_hi") + j - 1)
                        sp.wait_ge(sem(f"{s}_w_lo"), since(s, "w_lo") + j - 1)
                    sp.dma_start(wf[:, u, :], d["wf"][j]).then_inc(sem(f"{s}_wf_loaded{u}"), 16)

                load(0, 0, False)
                load(1, 1, False)
                with sp.Fori(1, NJ // 2) as i:
                    for u in range(2):
                        load(2 * i + u, u, True)
                load(NJ - 1, 0, True)

            out_proj("a", "wo_a", True)
            ffn("f", "a")
            sp.wait_ge(sem("f_yt"), 4)
            sp.dma_start(wb[:, :, :], d["wb"][0]).then_inc(sem("wb_loaded"), 16)
            sp.dma_start(rope[:, :, :], d["rope_b"]).then_inc(sem("b_consts"), 16)
            sp.dma_start(maskb[:, :], d["maskb"]).then_inc(sem("b_consts"), 16)
            sp.wait_ge(sem("f_y_turned"), 4)
            sp.dma_start(wvb[:, :, :], d["wvb"]).then_inc(sem("b_wv_loaded"), 16)

            def load_group(g):
                sp.wait_ge(sem("b_w_hi"), g)
                sp.wait_ge(sem("b_w_lo"), g)
                sp.dma_start(wb[:, :, :], d["wb"][g]).then_inc(sem("wb_loaded"), 16)

            def swap(n, r):
                sp.wait_ge(sem("b_raw"), n + 1)
                for src, dst in ((32, 0), (0, 32), (96, 64), (64, 96)):
                    sp.dma_start(rb[dst:dst + 32, r, :], raw[src:src + 32, r, :]).then_inc(
                        sem(f"b_swapped{r}"), 16)

            def group(g, gp):
                if not (isinstance(g, int) and g >= NG - 2):
                    load_group(g + 2)
                if not (isinstance(g, int) and g == NG - 1):
                    for piece in range(6):
                        swap(6 * (g + 1) + piece, piece % 2)

            load_group(1)
            for piece in range(6):
                swap(piece, piece % 2)
            all_groups(sp, group)
            out_proj("b", "wo_b", False)
            ffn("g", "b")
            sp.wait_ge(sem("g_added"), since("g", "added") + NT // 2)
            sp.dma_start(out.rearrange("t p d -> p t d"), x[:, :, :]).then_inc(sem("stored"), 16)
            sp.wait_ge(sem("stored"), 16)

        @block.vector
        def _(dve):
            v = nc.vector
            v.memset(xt_hi[:, :, 0:PAD].bitcast(F32), 0.0)
            v.memset(xt_hi[:, :, PAD + T:TP].bitcast(F32), 0.0)
            v.memset(xt_lo[:, :, 0:PAD].bitcast(F32), 0.0)
            v.memset(xt_lo[:, :, PAD + T:TP].bitcast(F32), 0.0)
            v.memset(kr[:, :, 0:PAD], 0.0)
            v.memset(pa[:, :, KW:2 * P], 0.0)
            v.memset(negh[:, :, :], -0.5).then_inc(sem("padded"), 1)

            def norm(s, before):
                me = sem(f"{s}_ln")
                for half in range(2):
                    tiles = range(4 * half, 4 * half + 4)
                    if before is not None:
                        residual(before, half)
                    for t in tiles:
                        if before is None:
                            dve.wait_ge(sem(f"x_loaded{t // 2}"), 16)
                        else:
                            dve.wait_ge(sem(f"{before}_added"), since(before, "added") + t // 2 + 1)
                        v.bn_stats(stats[:, t, :], x[:, t, :]).then_inc(me, 1)
                    for t in tiles:
                        dve.wait_ge(me, since(s, "ln") + 4 * half + t + 1)
                        v.bn_aggr(mv[:, t, :], stats[:, t, :]).then_inc(me, 1)
                    dve.wait_ge(me, since(s, "ln") + 8 * half + 8)
                    four = slice(4 * half, 4 * half + 4)
                    ins = v.tensor_scalar(var[:, 0, four], mv[:, four, 1], LN_EPS, None, ALU.add)
                    if s == "a":
                        ins.then_inc(sem("a_var_eps"), 1)
                        dve.wait_ge(sem("a_var_eps"), half + 1)
                        ins = v.scalar_tensor_tensor(out=var[:, 1, four], in0=var[:, 0, four], scalar=RMS_EPS,
                                                     in1=mv[:, four, 1], op0=ALU.mult, op1=ALU.add)
                    ins.then_inc(sem(f"{s}_var"), 1)
                for t in range(NT):
                    if t % 4 == 0:
                        dve.wait_ge(sem(f"{s}_rstd"), since(s, "rstd") + t // 4 + 1)
                    v.tensor_scalar(z[:, t, :], x[:, t, :], mv[:, t, 0:1],
                                    rstd[:, 1 if s == "a" else 0, t:t + 1],
                                    ALU.subtract, ALU.mult).then_inc(sem(f"{s}_z"), 1)

            def norm_lo(s):
                for q in range(2 * NC):
                    dve.wait_ge(sem(f"{s}_xt_hi"), since(s, "xt_hi") + q + 1)
                    at = slice(PAD + HALF * (q // 2), PAD + HALF * (q // 2) + HALF)
                    hi = xt_hi[:, q % 2, at].bitcast(F32)
                    if s == "a":
                        ins = v.scalar_tensor_tensor(out=xt_lo[:, q % 2, at], in0=ps[:, q, :],
                                                     scalar=norm_w[:, q % 2:q % 2 + 1], in1=hi,
                                                     op0=ALU.mult, op1=ALU.subtract)
                    else:
                        ins = v.tensor_tensor(xt_lo[:, q % 2, at], ps[:, q, :], hi, ALU.subtract)
                    ins.then_inc(sem(f"{s}_xt_lo"), 1)

            def residual(s, half):
                for n in range(2 * half, 2 * half + 2):
                    dve.wait_ge(sem(f"{s}_y_turned"), since(s, "y_turned") + n + 1)
                    v.tensor_tensor(x[:, 2 * n:2 * n + 2, :], x[:, 2 * n:2 * n + 2, :],
                                    ps[:, n, :].rearrange("p (t d) -> p t d", t=2),
                                    ALU.add).then_inc(sem(f"{s}_added"), 1)

            def add_norm(h):
                if h == 0:
                    dve.wait_ge(sem("a_zt"), 4)
                for t in (2 * h, 2 * h + 1):
                    v.tensor_scalar(z[:, t, :], x[:, t, :], mv[:, t, 0:1], rstd[:, 0, t:t + 1],
                                    ALU.subtract, ALU.mult).then_inc(sem("a_zz"), 1)
                for t in (2 * h, 2 * h + 1):
                    dve.wait_ge(sem("a_zz"), t + 1)
                    v.tensor_tensor(x[:, t, :], x[:, t, :], z[:, t, :], ALU.add).then_inc(sem("a_xz"), 1)

            def rope_piece(bank, r, half, swaps):
                at = slice(HALF * half, HALF * half + HALF)
                v.tensor_tensor(ra[:, r, :], ps[:, bank, :], rope[:, 0, at], ALU.mult)
                for src, dst, n in swaps:
                    last = v.tensor_tensor(rb[dst:dst + n, r, :], ps[src:src + n, bank, :],
                                           rope[src:src + n, 1, at], ALU.mult)
                return last

            norm("a", None)
            dve.wait_ge(sem("ident_loaded"), 48)
            norm_lo("a")

            def weff(h, u):
                dve.wait_ge(sem("a_lora"), h + 1)
                dve.wait_ge(sem(f"wa_loaded{u}"), loads(h, u, 32))
                after(dve, "a_w_hi", h - 1)
                after(dve, "a_w_lo", h - 1)
                for c in range(NC):
                    last = v.scalar_tensor_tensor(out=wef[:, u, c, :, :].rearrange("p m d -> p (m d)"),
                                                  in0=ps[:, c, 0:3 * P], scalar=LORA_SCALE,
                                                  in1=wa[:, u, c, :, :].rearrange("p m d -> p (m d)"),
                                                  op0=ALU.mult, op1=ALU.add)
                last.then_inc(sem("a_weff"), 1)

            def rope_a(h, piece):
                dve.wait_ge(sem("a_qk"), 4 * h + piece + 1)
                after(dve, "a_rot", 4 * h + piece - 1)
                rope_piece(piece % 2, piece % 2, piece % 2,
                           [(64, 0, 64), (0, 64, 64)]).then_inc(sem("a_mul"), 1)

            def row_max(h, u, n):
                dve.wait_ge(sem("a_scores"), 4 * h + n + 1)
                after(dve, "a_exp", 4 * h + n - 3)
                bank = 2 + (n + 2 * u) % 4
                v.tensor_reduce(nmax[:, 2 * n:2 * n + 2], ps[:, bank, 0:2 * KW].rearrange("p (t k) -> p t k", t=2),
                                AX.X, ALU.max, negate=True).then_inc(sem("a_max"), 1)

            def row_inv(h, n):
                dve.wait_ge(sem("a_exp"), 4 * h + n + 1)
                after(dve, "a_pn", 4 * h + n - 3)
                v.reciprocal(rinv[:, 2 * n:2 * n + 2], rsum[:, 2 * n:2 * n + 2]).then_inc(sem("a_inv"), 1)

            def head_a(i, ip, u):
                for kind, dh, n in steps_a(("weff", "rope", "max", "inv"), i, u):
                    h = 2 * i + u + dh
                    if kind == "weff":
                        weff(h, (u + dh) % 2)
                    elif kind == "rope":
                        rope_a(h, n)
                    elif kind == "max":
                        row_max(h, (u + dh) % 2, n)
                    elif kind == "inv":
                        row_inv(h, n)
                if isinstance(i, int) and 0 <= 2 * i + u < 4:
                    add_norm(2 * i + u)

            dve.wait_ge(sem("a_consts"), 48)
            all_pairs(dve, head_a)

            def out_proj(s, lora):
                def step(h, u):
                    if lora:
                        dve.wait_ge(sem(f"{s}_ol"), h + 1)
                    dve.wait_ge(sem(f"{s}_wo_loaded{u}"), loads(h, u, 32 if lora else 16))
                    after(dve, f"{s}_wo_hi", h)
                    after(dve, f"{s}_wo_lo", h)
                    if lora:
                        v.scalar_tensor_tensor(out=woe[:, u, :], in0=ps[:, u, 0:D], scalar=LORA_SCALE,
                                               in1=wo[:, u, :], op0=ALU.mult,
                                               op1=ALU.add).then_inc(sem(f"{s}_woe"), 1)
                    else:
                        v.tensor_copy(woe[:, u, :], wo[:, u, :]).then_inc(sem(f"{s}_woe"), 1)
                    dve.wait_ge(sem(f"{s}_ot_hi"), h + 1)
                    v.tensor_tensor(ot_lo[:, u, :], ot[:, h, :], ot_hi[:, u, :].bitcast(F32),
                                    ALU.subtract).then_inc(sem(f"{s}_ot_lo"), 1)

                step(0, 0)
                step(1, 1)
                with dve.Fori(1, HA // 2) as i:
                    for u in range(2):
                        step(2 * i + u, u)

            out_proj("a", True)
            dve.wait_ge(sem("a_xz"), NT)

            def ffn(s, before):
                me = sem(f"{s}_route")
                n = 0

                def link(ins):
                    nonlocal n
                    n += 1
                    ins.then_inc(me, 1)
                    dve.wait_ge(me, since(s, "route") + n)

                norm(s, before)
                dve.wait_ge(sem(f"{s}_wg_hi"), since(s, "wg_hi") + 1)
                v.tensor_tensor(wg_lo[:, :, :], wg[:, :, :], wg_hi[:, :, :].bitcast(F32),
                                ALU.subtract).then_inc(sem(f"{s}_wg_lo"), 1)
                norm_lo(s)
                v.memset(cwb[:, :, :], 0.0)
                v.memset(cw[:, :, :], 1.0)

                def route_top():
                    dve.wait_ge(sem(f"{s}_logits"), since(s, "logits") + 1)
                    link(v.tensor_copy(lg[:, :, :], ps[:, 3, 0:NT * NE].rearrange("p (t e) -> p t e", e=NE)))
                    for t in range(NT):
                        ins = v.max(top[:, t, :], lg[:, t, :])
                    link(ins)
                    for t in range(NT):
                        ins = v.max_index(topi[:, t, :], top[:, t, :], lg[:, t, :])
                    link(ins)
                    link(v.tensor_copy(topf[:, :, :], topi[:, :, :]))

                def route_chosen():
                    link(v.tensor_tensor(hit[:, :, :].rearrange("p (t k) e -> p t k e", t=NT),
                                         iota[:, :, :].rearrange("p (t k) e -> p t k e", t=NT),
                                         topf[:, :, 0:TOPK].unsqueeze(3).broadcast_to([P, NT, TOPK, NE]),
                                         ALU.is_equal))
                    link(v.tensor_reduce(chosen[:, :, :], hit[:, :, :].rearrange("p (t k) e -> p t e k", t=NT),
                                         AX.X, ALU.add))
                    v.tensor_tensor(lg[:, :, :], lg[:, :, :], top[:, :, 0:1].broadcast_to([P, NT, NE]),
                                    ALU.subtract).then_inc(sem(f"{s}_shifted"), 1)

                def route_weights():
                    dve.wait_ge(sem(f"{s}_ex"), since(s, "ex") + 1)
                    link(v.tensor_tensor(ex[:, :, :], ex[:, :, :], chosen[:, :, :], ALU.mult))
                    link(v.tensor_reduce(csum[:, :], ex[:, :, :], AX.X, ALU.add))
                    link(v.reciprocal(cinv[:, :], csum[:, :]))
                    link(v.tensor_tensor(cw[:, :, 0:NE], ex[:, :, :],
                                         cinv[:, :].unsqueeze(2).broadcast_to([P, NT, NE]), ALU.mult))

                def route_parts():
                    for part in range(3):
                        at = slice(NW * part, NW * part + NW)
                        src = cw if part == 0 else cwr
                        ins = v.tensor_copy(cwb[:, :, at], src[:, :, :])
                        if part < 2:
                            link(ins)
                            link(v.tensor_tensor(cwr[:, :, :], src[:, :, :], cwb[:, :, at], ALU.subtract))
                    ins.then_inc(sem(f"{s}_cwb"), 1)

                route = [route_top, route_chosen, route_weights, route_parts]

                def tile(j):
                    shared = isinstance(j, int) and j < N_SHARED
                    for half in range(2):
                        k = 2 * j + half
                        b = half
                        dve.wait_ge(sem(f"{s}_silu"), since(s, "silu") + k + 1)
                        dve.wait_ge(sem(f"{s}_u"), since(s, "u") + k + 1)
                        if not shared:
                            v.tensor_tensor(gu[:, b, :], ps[:, 1, :], sg[:, b, :], ALU.mult).then_inc(sem(f"{s}_gu"), 1)
                            dve.wait_ge(sem(f"{s}_gu"), since(s, "gu") + k + 1 - 2 * N_SHARED)
                            dve.wait_ge(sem(f"{s}_c"), since(s, "c") + k + 1 - 2 * N_SHARED)
                        if not shared or k > 0:
                            dve.wait_ge(sem(f"{s}_h_hi"), since(s, "h_hi") + k)
                            dve.wait_ge(sem(f"{s}_h_lo"), since(s, "h_lo") + k)
                        if shared:
                            v.tensor_tensor(hf[:, b, :], ps[:, 1, :], sg[:, b, :], ALU.mult).then_inc(sem(f"{s}_h"), 1)
                            route[k]()
                        else:
                            v.tensor_tensor(hf[:, b, :], ps[:, 2, :], gu[:, b, :], ALU.mult).then_inc(sem(f"{s}_h"), 1)
                        dve.wait_ge(sem(f"{s}_h_hi"), since(s, "h_hi") + k + 1)
                        if not shared or k > 0:
                            dve.wait_ge(sem(f"{s}_down"), since(s, "down") + k)
                        v.tensor_tensor(h_lo[:, b, :], hf[:, b, :], h_hi[:, b, :].bitcast(F32),
                                        ALU.subtract).then_inc(sem(f"{s}_h_lo"), 1)

                tile(0)
                tile(1)
                dve.wait_ge(sem(f"{s}_cwt_turned"), since(s, "cwt_turned") + 1)
                v.tensor_copy(cwt[:, :], ps[:, 3, :].bitcast(BF16)[:, 0:T]).then_inc(sem(f"{s}_cwt"), 1)
                with dve.Fori(1, NJ // 2) as i:
                    for u in range(2):
                        tile(2 * i + u)
                tile(NJ - 1)

            ffn("f", "a")

            norm("b", "f")
            norm_lo("b")
            dve.wait_ge(sem("b_consts"), 32)
            dve.wait_ge(sem("b_wv_hi"), 1)
            v.tensor_tensor(wvb_lo[:, :, :], wvb[:, :, :], wvb_hi[:, :, :].bitcast(F32),
                            ALU.subtract).then_inc(sem("b_wv_lo"), 1)

            def cos_b(n, piece):
                dve.wait_ge(sem("b_raw"), n + 1)
                after(dve, "b_lo", n - 1)
                half = piece % 2
                v.tensor_tensor(ra[:, half, :], ps[:, 7, :], rope[:, 0, HALF * half:HALF * half + HALF],
                                ALU.mult).then_inc(sem("b_cos"), 1)

            def low_b(n, kp, piece):
                dve.wait_ge(sem("b_hi"), n + 1)
                half = piece % 2
                at = slice(HALF * half, HALF * half + HALF)
                if piece < 2:
                    ins = v.tensor_tensor(kh[:, kp, 1, at], ra[:, half, :], kh[:, kp, 0, at].bitcast(F32),
                                          ALU.subtract)
                else:
                    pair = piece // 2 - 1
                    v.tensor_tensor(qh[64:128, pair, 0, at], ra[0:64, half, :],
                                    qh[0:64, pair, 0, at].bitcast(F32), ALU.subtract)
                    ins = v.tensor_tensor(qh[0:64, pair, 1, at], ra[64:128, half, :],
                                          qh[64:128, pair, 1, at].bitcast(F32), ALU.subtract)
                ins.then_inc(sem("b_lo"), 1)

            def row_max_b(h, par, i):
                t = SCORE_TILES[i]
                dve.wait_ge(sem("b_scores"), NT * h + i + 1)
                b = 2 * (i % 2)
                v.tensor_reduce(nmb[:, par, i:i + 1],
                                ps[:, b:b + 2, :].rearrange("p b k -> p (b k)")[:, 0:P * (t + 1)],
                                AX.X, ALU.max, negate=True).then_inc(sem("b_max"), 1)

            def row_inv_b(h, par, i):
                dve.wait_ge(sem("b_exp"), NT * h + i + 1)
                after(dve, "b_pn", NT * h + i - 2 * NT + 1)
                v.reciprocal(rib[:, par, i:i + 1], rsb[:, par, i:i + 1]).then_inc(sem("b_inv"), 1)

            def pt_lo_b(h, s):
                c = CHB * h + s
                first, n = chunk_columns(s)
                dve.wait_ge(sem("b_pt_hi"), c + 1)
                after(dve, "b_prod", c - 2)
                at = slice(P * first, P * first + P * n)
                v.tensor_tensor(pt_lo[:, s % 3, at], ps[:, 4 + s % 2, at], pt_hi[:, s % 3, at].bitcast(F32),
                                ALU.subtract).then_inc(sem("b_pt_lo"), 1)

            def o_add(h, hh, g, bank):
                dve.wait_ge(sem("b_o_low"), 2 * h + bank - 6 + 1)
                half = 7 - bank
                r = 64 * (hh % 2)
                v.tensor_tensor(ot[r:r + 64, 2 * g + hh // 2, HALF * half:HALF * half + HALF],
                                ps[0:64, bank, :], o_low[:, :], ALU.add).then_inc(sem("b_ot"), 1)

            def head(g, gp, hh):
                for kind, dh, i in steps(("max", "inv", "pt_lo", "o_add", "cos", "low"), g, hh):
                    h = QPG * g + hh + dh
                    piece = 6 * (g + 1 + dh) + i
                    if kind == "max":
                        row_max_b(h, (hh + dh) % 2, i)
                    elif kind == "inv":
                        row_inv_b(h, (hh + dh) % 2, i)
                    elif kind == "pt_lo":
                        pt_lo_b(h, i)
                    elif kind == "o_add":
                        o_add(h, head_at(g, gp, hh, dh)[2], head_at(g, gp, hh, dh)[0], 6 + i)
                    elif kind == "cos":
                        cos_b(piece, i)
                    elif kind == "low":
                        low_b(piece, (gp + 1 + dh) % 2, i)

            def group(g, gp):
                for hh in range(QPG):
                    head(g, gp, hh)

            cos_b(0, 0)
            for piece in range(6):
                if piece < 5:
                    cos_b(piece + 1, piece + 1)
                if piece < 4:
                    low_b(piece, 0, piece)
            head(-1, 1, QPG - 2)
            head(-1, 1, QPG - 1)
            low_b(4, 0, 4)
            low_b(5, 0, 5)
            all_groups(dve, group)
            head(NG, 0, 0)
            head(NG, 0, 1)
            out_proj("b", False)
            ffn("g", "b")
            for half in range(2):
                residual("g", half)

        @block.gpsimd
        def _(pool):
            g_ = nc.gpsimd

            def norm(s):
                parts = 2 if s == "a" else 1
                for half in range(2):
                    pool.wait_ge(sem(f"{s}_var"), since(s, "var") + half + 1)
                    four = slice(4 * half, 4 * half + 4)
                    g_.tensor_tensor(rstd[:, 0:parts, four], var[:, 0:parts, four], negh[:, 0:parts, four],
                                     ALU.pow).then_inc(sem(f"{s}_rstd"), 1)

            pool.wait_ge(sem("padded"), 1)
            norm("a")

            def w_lo(h, u):
                pool.wait_ge(sem("a_w_hi"), h + 1)
                g_.tensor_tensor(wqk_lo[:, u, :, :, :], wef[:, u, :, 0:2, :], wqk_hi[:, u, :, :, :].bitcast(F32),
                                 ALU.subtract)
                g_.tensor_tensor(wv_lo[:, :, u, :], wef[:, u, :, 2, :], wv_hi[:, :, u, :].bitcast(F32),
                                 ALU.subtract).then_inc(sem("a_w_lo"), 1)

            def rot(h, u, piece):
                pool.wait_ge(sem("a_mul"), 4 * h + piece + 1)
                if piece == 0:
                    after(pool, "a_scores", 4 * h - 4)
                at = HALF * (piece % 2)
                dst = qr[:, u, at:at + HALF] if piece < 2 else kr[:, u, PAD + at:PAD + at + HALF]
                g_.tensor_tensor(dst, ra[:, piece % 2, :], rb[:, piece % 2, :], ALU.add).then_inc(sem("a_rot"), 1)

            def p_norm(h, n):
                pool.wait_ge(sem("a_inv"), 4 * h + n + 1)
                two = slice(2 * n, 2 * n + 2)
                g_.tensor_tensor(pa[:, two, 0:KW], pa[:, two, 0:KW],
                                 rinv[:, two].unsqueeze(2).broadcast_to([P, 2, KW]),
                                 ALU.mult).then_inc(sem("a_pn"), 1)

            def head_a(i, ip, u):
                for kind, dh, n in steps_a(("w_lo", "rotate", "norm"), i, u):
                    h = 2 * i + u + dh
                    if kind == "w_lo":
                        w_lo(h, (u + dh) % 2)
                    elif kind == "rotate":
                        rot(h, (u + dh) % 2, n)
                    elif kind == "norm":
                        p_norm(h, n)

            all_pairs(pool, head_a)

            def out_proj(s):
                def step(h, u):
                    pool.wait_ge(sem(f"{s}_wo_hi"), h + 1)
                    g_.tensor_tensor(wo_lo[:, u, :], woe[:, u, :], wo_hi[:, u, :].bitcast(F32),
                                     ALU.subtract).then_inc(sem(f"{s}_wo_lo"), 1)

                with pool.Fori(0, HA // 2) as i:
                    for u in range(2):
                        step(2 * i + u, u)

            def ffn(s):
                norm(s)

                def tile(j, u, first):
                    pool.wait_ge(sem(f"{s}_w_hi"), since(s, "w_hi") + j + 1)
                    g_.tensor_tensor(wf_lo[:, u, :], wf[:, u, :], wf_hi[:, u, :].bitcast(F32),
                                     ALU.subtract).then_inc(sem(f"{s}_w_lo"), 1)

                with pool.Fori(0, NJ // 2) as i:
                    for u in range(2):
                        tile(2 * i + u, u, False)
                tile(NJ - 1, 0, False)

            out_proj("a")
            ffn("f")
            norm("b")

            def w_lo_b(g):
                pool.wait_ge(sem("b_w_hi"), g + 1)
                after(pool, "b_proj", 6 * g)
                g_.tensor_tensor(wb_lo[:, :, :], wb[:, :, :], wb_hi[:, :, :].bitcast(F32),
                                 ALU.subtract).then_inc(sem("b_w_lo"), 1)

            def rot_b(n, piece):
                half = piece % 2
                pool.wait_ge(sem(f"b_swapped{half}"), 64 * (n // 2 + 1) if isinstance(n, int) else 32 * n + 64 - 32 * half)
                g_.tensor_tensor(rb[:, half, :], rb[:, half, :], rope[:, 1, HALF * half:HALF * half + HALF],
                                 ALU.mult).then_inc(sem("b_sin"), 1)
                pool.wait_ge(sem("b_sin"), n + 1)
                pool.wait_ge(sem("b_cos"), n + 1)
                g_.tensor_tensor(ra[:, half, :], ra[:, half, :], rb[:, half, :], ALU.add).then_inc(sem("b_rot"), 1)

            def v_lo_b(g, gp):
                pool.wait_ge(sem("b_v_hi"), g + 1)
                g_.tensor_tensor(vst[:, gp, :, DB:2 * DB], vb[:, g, :, :],
                                 vst[:, gp, :, 0:DB].bitcast(F32), ALU.subtract).then_inc(sem("b_v_lo"), 1)

            def p_norm_b(h, par, i):
                pool.wait_ge(sem("b_inv"), NT * h + i + 1)
                t = SCORE_TILES[i]
                g_.tensor_tensor(pb(par, t), pb(par, t), rib[:, par, i:i + 1].broadcast_to([P, P * (t + 1)]),
                                 ALU.mult).then_inc(sem("b_pn"), 1)

            def head(g, gp, hh):
                for kind, dh, i in steps(("norm", "rotate"), g, hh):
                    if kind == "norm":
                        p_norm_b(QPG * g + hh + dh, (hh + dh) % 2, i)
                    else:
                        rot_b(6 * (g + 1 + dh) + i, i)
                    if hh == QPG - 1 and kind == "norm" and not (isinstance(g, int) and not 0 <= g < NG - 1):
                        if i == V_SPLIT_AT:
                            v_lo_b(g + 1, 1 - gp)
                        if i == W_LO_AT and not (isinstance(g, int) and g >= NG - 2):
                            w_lo_b(g + 2)

            def group(g, gp):
                for hh in range(QPG):
                    head(g, gp, hh)

            w_lo_b(0)
            for piece in range(6):
                rot_b(piece, piece)
            v_lo_b(0, 0)
            head(-1, 1, QPG - 2)
            head(-1, 1, QPG - 1)
            w_lo_b(1)
            all_groups(pool, group)
            head(NG, 0, 0)
            head(NG, 0, 1)
            out_proj("b")
            ffn("g")

        @block.scalar
        def _(act):
            s_ = nc.scalar

            def norm(s):
                for q in range(2 * NC):
                    at = slice(PAD + HALF * (q // 2), PAD + HALF * (q // 2) + HALF)
                    act.wait_ge(sem(f"{s}_zt"), since(s, "zt") + q + 1)
                    if s == "a":
                        ins = s_.activation(xt_hi[:, q % 2, at], ps[:, q, :], ACT.Copy, scale=norm_w[:, q % 2:q % 2 + 1])
                    else:
                        ins = s_.copy(xt_hi[:, q % 2, at], ps[:, q, :])
                    ins.then_inc(sem(f"{s}_xt_hi"), 1)

            def y_out(s, acc, n):
                for half in range(2):
                    act.wait_ge(acc, n + half + 1)
                    for c in range(NC):
                        q = 2 * c + half
                        s_.copy(yt[:, q, :], ps[:, 4 + q, :]).then_inc(sem(f"{s}_yt"), 1)

            act.wait_ge(sem("ident_loaded"), 48)
            norm("a")

            def w_hi(h, i, u):
                act.wait_ge(sem("a_weff"), h + 1)
                after(act, "a_qk", 4 * h - 4)
                after(act, "a_v", 5 * i)
                s_.copy(wqk_hi[:, u, :, :, :], wef[:, u, :, 0:2, :])
                s_.copy(wv_hi[:, :, u, :], wef[:, u, :, 2, :]).then_inc(sem("a_w_hi"), 1)

            def v_out(i, ip, piece):
                act.wait_ge(sem("a_v"), 5 * i + piece + 1)
                after(act, "a_pv", 8 * i - 8)
                n = 2 if piece < 4 else 1
                s_.copy(va[:, ip, 2 * piece:2 * piece + n, :, :].rearrange("p t u d -> p (t u d)"),
                        ps[:, piece % 2, 0:n * 2 * P]).then_inc(sem("a_vout"), 1)

            def exps(h, u, n):
                act.wait_ge(sem("a_max"), 4 * h + n + 1)
                after(act, "a_turned", 4 * h + n - 3)
                after(act, "a_inv", 4 * h + n - 3)
                bank = 2 + (n + 2 * u) % 4
                for m in range(2):
                    t = 2 * n + m
                    last = s_.activation(pa[:, t, 0:KW], ps[:, bank, KW * m:KW * m + KW], ACT.Exp,
                                         bias=nmax[:, t:t + 1], accum_out=rsum[:, t:t + 1])
                last.then_inc(sem("a_exp"), 1)

            def pt_out(h, n):
                act.wait_ge(sem("a_turned"), 4 * h + n + 1)
                after(act, "a_pv", 4 * h + n - 1)
                s_.copy(pta[:, n % 2, :], ps[:, 6 + n % 2, :]).then_inc(sem("a_pt"), 1)

            def o_out(h, u, half):
                act.wait_ge(sem("a_pv"), 4 * h + 2 * half + 2)
                s_.copy(ot[:, h, HALF * half:HALF * half + HALF],
                        ps[:, 2 + 2 * u + half, :]).then_inc(sem("a_ot"), 1)

            def head_a(i, ip, u):
                for kind, dh, n in steps_a(("w_hi", "v_out", "exp", "pt", "o_out"), i, u):
                    h = 2 * i + u + dh
                    if kind == "w_hi":
                        w_hi(h, i + (u + dh) // 2, (u + dh) % 2)
                    elif kind == "v_out":
                        v_out(i + dh, (ip + dh) % 2, n)
                    elif kind == "exp":
                        exps(h, (u + dh) % 2, n)
                    elif kind == "pt":
                        pt_out(h, n)
                    elif kind == "o_out":
                        o_out(h, (u + dh) % 2, n)

            all_pairs(act, head_a)

            def out_proj(s):
                def step(h, u):
                    after(act, f"{s}_oacc", h - 1)
                    s_.copy(ot_hi[:, u, :], ot[:, h, :]).then_inc(sem(f"{s}_ot_hi"), 1)
                    act.wait_ge(sem(f"{s}_woe"), h + 1)
                    s_.copy(wo_hi[:, u, :], woe[:, u, :]).then_inc(sem(f"{s}_wo_hi"), 1)

                step(0, 0)
                step(1, 1)
                with act.Fori(1, HA // 2) as i:
                    for u in range(2):
                        step(2 * i + u, u)

            out_proj("a")
            y_out("a", sem("a_oacc"), HA - 1)

            def ffn(s):
                def w_hi_f(j, u):
                    act.wait_ge(sem(f"{s}_wf_loaded{u}"), since(s, f"wf_loaded{u}") + loads(j, u, 16))
                    if not (isinstance(j, int) and j < 2):
                        act.wait_ge(sem(f"{s}_down"), since(s, "down") + 2 * j - 2)
                    s_.copy(wf_hi[:, u, :], wf[:, u, :]).then_inc(sem(f"{s}_w_hi"), 1)

                act.wait_ge(sem(f"{s}_consts"), since(s, "consts") + 48)
                s_.copy(wg_hi[:, :, :], wg[:, :, :]).then_inc(sem(f"{s}_wg_hi"), 1)
                w_hi_f(0, 0)
                norm(s)
                for half in range(2):
                    act.wait_ge(sem(f"{s}_logits_t"), since(s, "logits_t") + half + 1)
                    s_.copy(lgs[:, HALF * half:HALF * half + HALF],
                            ps[0:NE, 3 - half, :]).then_inc(sem(f"{s}_lgs"), 1)

                def tile(j, u, more):
                    shared = isinstance(j, int) and j < N_SHARED
                    for half in range(2):
                        k = 2 * j + half
                        b = half
                        act.wait_ge(sem(f"{s}_g"), since(s, "g") + k + 1)
                        if not shared or k > 1:
                            act.wait_ge(sem(f"{s}_h"), since(s, "h") + k - 1)
                        s_.activation(sg[:, b, :], ps[:, 0, :], ACT.Silu).then_inc(sem(f"{s}_silu"), 1)
                        if half == 0 and more:
                            w_hi_f(j + 1, 1 - u)
                        act.wait_ge(sem(f"{s}_h"), since(s, "h") + k + 1)
                        if not shared or k > 0:
                            act.wait_ge(sem(f"{s}_down"), since(s, "down") + k)
                        s_.copy(h_hi[:, b, :], hf[:, b, :]).then_inc(sem(f"{s}_h_hi"), 1)
                        if shared and k == 1:
                            act.wait_ge(sem(f"{s}_shifted"), since(s, "shifted") + 1)
                            s_.activation(ex[:, :, :], lg[:, :, :], ACT.Exp).then_inc(sem(f"{s}_ex"), 1)

                tile(0, 0, True)
                tile(1, 1, True)
                with act.Fori(1, NJ // 2) as i:
                    for u in range(2):
                        tile(2 * i + u, u, True)
                tile(NJ - 1, 0, False)
                y_out(s, sem(f"{s}_down"), since(s, "down") + 2 * NJ - 2)

            ffn("f")
            def w_hi_b(g):
                act.wait_ge(sem("wb_loaded"), 16 * (g + 1))
                after(act, "b_proj", 6 * g)
                s_.copy(wb_hi[:, :, :], wb[:, :, :]).then_inc(sem("b_w_hi"), 1)

            def raw_b(n, piece):
                act.wait_ge(sem("b_proj"), n + 1)
                after(act, "b_rot", n - 1)
                s_.copy(raw[:, piece % 2, :], ps[:, 7, :]).then_inc(sem("b_raw"), 1)

            def high_b(n, g, kp, piece):
                act.wait_ge(sem("b_rot"), n + 1)
                half = piece % 2
                at = slice(HALF * half, HALF * half + HALF)
                if piece < 2:
                    after(act, "b_scores", 32 * g - 32)
                    ins = s_.copy(kh[:, kp, 0, at], ra[:, half, :])
                else:
                    pair = piece // 2 - 1
                    after(act, "b_scores", 32 * g - 16 + 16 * pair)
                    s_.copy(qh[0:64, pair, 0, at], ra[0:64, half, :])
                    ins = s_.copy(qh[64:128, pair, 1, at], ra[64:128, half, :])
                ins.then_inc(sem("b_hi"), 1)

            def v_hi_b(g, gp):
                s_.copy(vst[:, gp, :, 0:DB], vb[:, g, :, :]).then_inc(sem("b_v_hi"), 1)

            def exp_b(h, par, i):
                st = NT * h + i
                t = SCORE_TILES[i]
                act.wait_ge(sem("b_max"), st + 1)
                after(act, "b_inv", st - 2 * NT + 1)
                after(act, "b_turned", CHB * (h - 2) + 8 if t >= 4 else CHB * (h - 1) + 9 + t)
                b = 2 * (i % 2)
                s_.activation(pb(par, t), ps[:, b:b + 2, :].rearrange("p b k -> p (b k)")[:, 0:P * (t + 1)],
                              ACT.Exp, bias=nmb[:, par, i:i + 1],
                              accum_out=rsb[:, par, i:i + 1]).then_inc(sem("b_exp"), 1)

            def pt_hi_b(h, s):
                c = CHB * h + s
                first, n = chunk_columns(s)
                at = slice(P * first, P * first + P * n)
                act.wait_ge(sem("b_turned"), c + 1)
                after(act, "b_prod", c - 2)
                s_.copy(pt_hi[:, s % 3, at], ps[:, 4 + s % 2, at]).then_inc(sem("b_pt_hi"), 1)

            def o_low_b(h, bank):
                act.wait_ge(sem("b_prod"), CHB * h + (8 if bank == 6 else CHB))
                after(act, "b_ot", 2 * h + bank - 6)
                s_.copy(o_low[:, :], ps[64:128, bank, :]).then_inc(sem("b_o_low"), 1)

            def head(g, gp, hh):
                for kind, dh, i in steps(("exp", "pt_hi", "o_low", "raw", "high"), g, hh):
                    h = QPG * g + hh + dh
                    piece = 6 * (g + 1 + dh) + i
                    if kind == "exp":
                        exp_b(h, (hh + dh) % 2, i)
                    elif kind == "pt_hi":
                        pt_hi_b(h, i)
                    elif kind == "o_low":
                        o_low_b(h, 6 + i)
                    elif kind == "raw":
                        raw_b(piece, i)
                    elif kind == "high":
                        high_b(piece, g + 1 + dh, (gp + 1 + dh) % 2, i)
                    if hh == QPG - 1 and not (isinstance(g, int) and not 0 <= g < NG - 1):
                        if (kind, i) == ("exp", V_SPLIT_AT - 1):
                            v_hi_b(g + 1, 1 - gp)
                        if (kind, i) == ("raw", 5) and not (isinstance(g, int) and g >= NG - 2):
                            w_hi_b(g + 2)

            def group(g, gp):
                for hh in range(QPG):
                    head(g, gp, hh)

            def v_out_b(tiles):
                for t in tiles:
                    act.wait_ge(sem("b_v"), t + 1)
                    s_.copy(vb[:, :, t, :],
                            ps[:, t % 4, :].rearrange("p (g d) -> p g d", g=NG)).then_inc(sem("b_vout"), 1)

            w_hi_b(0)
            norm("b")
            act.wait_ge(sem("b_wv_loaded"), 16)
            s_.copy(wvb_hi[:, :, :], wvb[:, :, :]).then_inc(sem("b_wv_hi"), 1)
            raw_b(0, 0)
            raw_b(1, 1)
            v_out_b(range(4))
            high_b(0, 0, 0, 0)
            raw_b(2, 2)
            v_out_b((4, 5))
            high_b(1, 0, 0, 1)
            raw_b(3, 3)
            v_out_b((6, 7))
            high_b(2, 0, 0, 2)
            raw_b(4, 4)
            high_b(3, 0, 0, 3)
            raw_b(5, 5)
            act.wait_ge(sem("b_vout"), NT)
            v_hi_b(0, 0)
            head(-1, 1, QPG - 2)
            head(-1, 1, QPG - 1)
            high_b(4, 0, 0, 4)
            high_b(5, 0, 0, 5)
            w_hi_b(1)
            all_groups(act, group)
            head(NG, 0, 0)
            head(NG, 0, 1)
            out_proj("b")
            y_out("b", sem("b_oacc"), HA - 1)
            ffn("g")

        @block.tensor
        def _(pe):
            t_ = nc.tensor

            def mm(o, l, r, start=True, stop=True):
                return t_.matmul(o, l, r, start=start, stop=stop)

            def norm(s):
                for q in range(2 * NC):
                    for m in range(4):
                        t = 4 * (q // 2) + m
                        pe.wait_ge(sem(f"{s}_z"), since(s, "z") + t + 1)
                        last = t_.transpose(ps[:, q, P * m:P * m + P], z[:, t, P * (q % 2):P * (q % 2) + P],
                                            idf[:, :])
                    last.then_inc(sem(f"{s}_zt"), 1)

            def turn_back(s):
                for n in range(NT // 2):
                    pe.wait_ge(sem(f"{s}_yt"), since(s, "yt") + 2 * (n // 2) + 2)
                    for m in range(2):
                        t = 2 * n + m
                        for c in range(NC):
                            last = t_.transpose(ps[:, n, D * m + P * c:D * m + P * c + P],
                                                yt[:, 2 * c + t // 4, P * (t % 4):P * (t % 4) + P], idf[:, :])
                    last.then_inc(sem(f"{s}_y_turned"), 1)

            def three(o, lhs, rhs, first=True, last=True):
                terms = [(lhs(c, a), rhs(c, b)) for c in range(NC) for a, b in ((0, 0), (0, 1), (1, 0))]
                for n, (l, r) in enumerate(terms):
                    ins = mm(o, l, r, start=first and n == 0, stop=last and n == len(terms) - 1)
                return ins

            def xt(part, c, a, n):
                return (xt_hi, xt_lo)[part][:, c, PAD + a:PAD + a + n]

            pe.wait_ge(sem("ident_loaded"), 48)
            norm("a")
            pe.wait_ge(sem("a_consts"), 48)

            def lora(h, i, u):
                pe.wait_ge(sem(f"wa_loaded{u}"), loads(h, u, 32))
                after(pe, "a_mul", 4 * h - 4)
                if u == 0:
                    after(pe, "a_vout", 5 * i)
                elif isinstance(h, int) and h == 1:
                    pe.wait_ge(sem("a_weff"), 1)
                for c in range(NC):
                    last = mm(ps[:, c, 0:3 * P], la[:, c, :], lb[:, u, :])
                last.then_inc(sem("a_lora"), 1)

            def qk(h, u, piece):
                if piece == 0:
                    pe.wait_ge(sem("a_w_lo"), h + 1)
                if piece >= 2:
                    pe.wait_ge(sem("a_mul"), 4 * h + piece - 1)
                elif not (isinstance(h, int) and h == HA - 1):
                    pe.wait_ge(sem("a_weff"), h + 2)
                else:
                    pe.wait_ge(sem("a_vout"), 5 * (HA // 2))
                w = piece // 2
                at = HALF * (piece % 2)
                three(ps[:, piece % 2, :],
                      lambda c, a: (wqk_hi, wqk_lo)[a][:, u, c, w, :],
                      lambda c, b: xt(b, c, at, HALF)).then_inc(sem("a_qk"), 1)

            def values(i, piece):
                if piece == 0:
                    pe.wait_ge(sem("a_w_lo"), 2 * i + 2)
                if piece < 2:
                    pe.wait_ge(sem("a_mul"), 8 * i + 3 + piece)
                else:
                    pe.wait_ge(sem("a_vout"), 5 * i + piece - 1)
                for m in range(2 if piece < 4 else 1):
                    t = 2 * piece + m
                    last = three(ps[:, piece % 2, 2 * P * m:2 * P * m + 2 * P],
                                 lambda c, a: xt(a, c, P * t - PAD, P),
                                 lambda c, b: (wv_hi, wv_lo)[b][:, c, :, :].rearrange("p u d -> p (u d)"))
                last.then_inc(sem("a_v"), 1)

            def scores_a(h, u, n):
                if n == 0:
                    pe.wait_ge(sem("a_rot"), 4 * h + 4)
                if n < 2:
                    after(pe, "a_exp", 4 * h + n - 1)
                else:
                    after(pe, "a_ot", 2 * h + n - 3)
                bank = 2 + (n + 2 * u) % 4
                for m in range(2):
                    t = 2 * n + m
                    o = ps[:, bank, KW * m:KW * m + KW]
                    mm(o, qr[:, u, P * t:P * t + P], kr[:, u, P * t:P * t + KW], True, False)
                    last = mm(o, idb[:, :], maska[:, 0 if t == 0 else 1, :], False, True)
                last.then_inc(sem("a_scores"), 1)

            def turn_a(h, n):
                pe.wait_ge(sem("a_pn"), 4 * h + n + 1)
                after(pe, "a_pt", 4 * h + n - 1)
                for m in range(4):
                    last = t_.transpose(ps[:, 6 + n % 2, P * m:P * m + P],
                                        pa[:, 2 * n + m // 2, P * (m % 2):P * (m % 2) + P], idf[:, :])
                last.then_inc(sem("a_turned"), 1)

            def products_a(h, i, ip, u, n):
                pe.wait_ge(sem("a_pt"), 4 * h + n + 1)
                pe.wait_ge(sem("a_vout"), 5 * i + n + 2)
                for m in range(2):
                    t = 2 * n + m
                    o = ps[:, 2 + 2 * u + t // 4, P * (t % 4):P * (t % 4) + P]
                    for b in range(2):
                        last = mm(o, va[:, ip, t + b, u, :], pta[:, n % 2, P * (2 * m + b):P * (2 * m + b) + P],
                                  b == 0, b == 1)
                last.then_inc(sem("a_pv"), 1)

            def low_rank_a(h, u):
                pe.wait_ge(sem(f"a_wo_loaded{u}"), loads(h, u, 32))
                after(pe, "a_woe", h - 1)
                mm(ps[:, u, 0:D], oa[:, u, :], ob[:, :]).then_inc(sem("a_ol"), 1)

            def head_a(i, ip, u):
                if isinstance(i, int) and 2 * i + u == HA:
                    pe.wait_ge(sem("a_mul"), 4 * HA)
                    pe.wait_ge(sem("a_ob_loaded"), 16)
                    low_rank_a(0, 0)
                    low_rank_a(1, 1)
                for kind, dh, n in steps_a(("lora", "qk", "values", "scores", "turn", "products"), i, u):
                    h = 2 * i + u + dh
                    if kind == "lora":
                        lora(h, i + (u + dh) // 2, (u + dh) % 2)
                    elif kind == "qk":
                        qk(h, (u + dh) % 2, n)
                    elif kind == "values":
                        values(i + dh, n)
                    elif kind == "scores":
                        scores_a(h, (u + dh) % 2, n)
                    elif kind == "turn":
                        turn_a(h, n)
                    elif kind == "products":
                        products_a(h, i + (u + dh) // 2, (ip + (u + dh) // 2) % 2, (u + dh) % 2, n)

            for q in range(2 * NC):
                pe.wait_ge(sem("a_xt_lo"), q + 1)
            all_pairs(pe, head_a)

            def out_proj(s, has_lora):
                pe.wait_ge(sem(f"{s}_ot"), OT_ALL[s])

                def low_rank(h, u):
                    if has_lora:
                        low_rank_a(h, u)

                def step(h, u, first, last):
                    pe.wait_ge(sem(f"{s}_wo_lo"), h + 1)
                    pe.wait_ge(sem(f"{s}_ot_lo"), h + 1)
                    for half in range(2):
                        at = slice(HALF * half, HALF * half + HALF)
                        for c in range(NC):
                            for n, (a, b) in enumerate(((0, 0), (0, 1), (1, 0))):
                                ins = mm(ps[:, 4 + 2 * c + half, :], (wo_hi, wo_lo)[a][:, u, P * c:P * c + P],
                                         (ot_hi, ot_lo)[b][:, u, at], first and n == 0, last and n == 2)
                        if half == 1 or last:
                            ins.then_inc(sem(f"{s}_oacc"), 1)

                step(0, 0, True, False)
                low_rank(2, 0)
                step(1, 1, False, False)
                low_rank(3, 1)
                with pe.Fori(1, HA // 2 - 1) as i:
                    for u in range(2):
                        step(2 * i + u, u, False, False)
                        low_rank(2 * i + u + 2, u)
                step(HA - 2, 0, False, False)
                step(HA - 1, 1, False, True)

            out_proj("a", True)
            turn_back("a")

            def ffn(s):
                norm(s)
                for q in range(2 * NC):
                    pe.wait_ge(sem(f"{s}_xt_lo"), since(s, "xt_lo") + q + 1)
                pe.wait_ge(sem(f"{s}_wg_lo"), since(s, "wg_lo") + 1)
                for half in range(2):
                    three(ps[0:NE, 3 - half, :], lambda c, a: (wg_hi, wg_lo)[a][:, c, :],
                          lambda c, b: xt(b, c, HALF * half, HALF)).then_inc(sem(f"{s}_logits_t"), 1)

                def up(j, u, half):
                    k = 2 * j + half
                    if half == 0:
                        pe.wait_ge(sem(f"{s}_w_lo"), since(s, "w_lo") + j + 1)
                    at = HALF * half
                    if not (isinstance(j, int) and k == 0):
                        pe.wait_ge(sem(f"{s}_silu"), since(s, "silu") + k)
                    three(ps[:, 0, :], lambda c, a: (wf_hi, wf_lo)[a][:, u, P * c:P * c + P],
                          lambda c, b: xt(b, c, at, HALF)).then_inc(sem(f"{s}_g"), 1)
                    if not (isinstance(j, int) and k == 0):
                        pe.wait_ge(sem(f"{s}_h"), since(s, "h") + k)
                    three(ps[:, 1, :], lambda c, a: (wf_hi, wf_lo)[a][:, u, D + P * c:D + P * c + P],
                          lambda c, b: xt(b, c, at, HALF)).then_inc(sem(f"{s}_u"), 1)
                    if isinstance(j, int) and j < N_SHARED:
                        return
                    mm(ps[:, 2, :], sel[:, P * j:P * j + P] if isinstance(j, int) else sel[:, bass.ts(j, P)],
                       cwt[:, at:at + HALF]).then_inc(sem(f"{s}_c"), 1)

                def down(j, u, half, first, last):
                    k = 2 * j + half
                    pe.wait_ge(sem(f"{s}_h_lo"), since(s, "h_lo") + k + 1)
                    for c in range(NC):
                        for n, (a, b) in enumerate(((0, 0), (0, 1), (1, 0))):
                            ins = mm(ps[:, 4 + 2 * c + half, :],
                                     (wf_hi, wf_lo)[a][:, u, 2 * D + P * c:2 * D + P * c + P],
                                     (h_hi, h_lo)[b][:, half, :], first and n == 0, last and n == 2)
                    ins.then_inc(sem(f"{s}_down"), 1)

                up(0, 0, 0)
                pe.wait_ge(sem(f"{s}_lgs"), since(s, "lgs") + 2)
                for t in range(NT):
                    last = t_.transpose(ps[:, 3, NE * t:NE * t + NE], lgs[:, P * t:P * t + P], idf[0:NE, 0:NE])
                last.then_inc(sem(f"{s}_logits"), 1)
                up(0, 0, 1)
                down(0, 0, 0, True, False)
                up(1, 1, 0)
                down(0, 0, 1, True, False)
                up(1, 1, 1)
                pe.wait_ge(sem(f"{s}_cwb"), since(s, "cwb") + 1)
                for t in range(NT):
                    last = t_.transpose(ps[:, 3, :].bitcast(BF16)[:, P * t:P * t + P], cwb[:, t, :], idb[:, :])
                last.then_inc(sem(f"{s}_cwt_turned"), 1)
                down(1, 1, 0, False, False)
                pe.wait_ge(sem(f"{s}_cwt"), since(s, "cwt") + 1)
                with pe.Fori(1, NJ // 2) as i:
                    for u in range(2):
                        j = 2 * i + u
                        up(j, u, 0)
                        down(j - 1, 1 - u, 1, False, False)
                        up(j, u, 1)
                        down(j, u, 0, False, False)
                j = NJ - 1
                up(j, 0, 0)
                down(j - 1, 1, 1, False, False)
                up(j, 0, 1)
                down(j, 0, 0, False, True)
                down(j, 0, 1, False, True)
                turn_back(s)

            ffn("f")
            norm("b")
            for q in range(2 * NC):
                pe.wait_ge(sem("b_xt_lo"), q + 1)

            def values_b(tiles):
                for t in tiles:
                    if t >= 4:
                        pe.wait_ge(sem("b_vout"), t - 3)
                    three(ps[:, t % 4, :], lambda c, a: xt(a, c, P * t, P),
                          lambda c, b: (wvb_hi, wvb_lo)[b][:, c, :]).then_inc(sem("b_v"), 1)

            def proj(n, g, piece):
                if piece == 0:
                    pe.wait_ge(sem("b_w_lo"), g + 1)
                after(pe, "b_cos", n)
                at = HALF * (piece % 2)
                col = (2 * P, 0, P)[piece // 2]
                three(ps[:, 7, :], lambda c, a: (wb_hi, wb_lo)[a][:, c, col:col + P],
                      lambda c, b: xt(b, c, at, HALF)).then_inc(sem("b_proj"), 1)

            def scores(h, g, kp, hh, i):
                st = NT * h + i
                t = SCORE_TILES[i]
                after(pe, "b_exp", st - 1)
                if i == 0:
                    pe.wait_ge(sem("b_lo"), 6 * g + (4 if hh < 2 else 6))
                bank = 2 * (i % 2)
                for n0 in range(0, t + 1, 4):
                    w = min(4, t + 1 - n0) * P
                    o = ps[:, bank + n0 // 4, 0:w]
                    for b in range(2):
                        mm(o, qh[:, hh // 2, hh % 2, P * t:P * t + P], kh[:, kp, b, P * n0:P * n0 + w],
                           b == 0, b == 1 and n0 + 4 <= t)
                mm(ps[:, bank + t // 4, P * (t % 4):P * (t % 4) + P],
                   idb[:, :], maskb[:, :], False, True).then_inc(sem("b_scores"), 1)

            def turn(h, par, s):
                after(pe, "b_pt_lo", CHB * h + s - 1)
                if s == 0:
                    pe.wait_ge(sem("b_pn"), NT * h + 4)
                if s == 8:
                    pe.wait_ge(sem("b_pn"), NT * h + NT)
                block = s % 8
                first, n = chunk_columns(s)
                base = 4 if s < 8 else 0
                for m in range(first, first + n):
                    last = t_.transpose(ps[:, 4 + s % 2, P * m:P * m + P],
                                        pb(par, base + m)[:, P * block:P * block + P], idf[:, :])
                last.then_inc(sem("b_turned"), 1)

            def products(h, g, gp, hh, s):
                c = CHB * h + s
                first, n = chunk_columns(s)
                bank = 6 if s < 8 else 7
                pe.wait_ge(sem("b_pt_lo"), c + 1)
                if s == 0:
                    after(pe, "b_ot", 2 * h - 1)
                    if hh == 0:
                        pe.wait_ge(sem("b_v_lo"), g + 1)
                if s == 8:
                    after(pe, "b_ot", 2 * h)
                    pe.wait_ge(sem("b_cos"), pieces_before(g, hh))
                block = s % 8
                at = slice(P * first, P * first + P * n)
                mm(ps[:, bank, at], vst[:, gp, block, :], pt_hi[:, s % 3, at], block == 0, False)
                mm(ps[:, bank, at], vst[:, gp, block, :], pt_lo[:, s % 3, at], False,
                   s in (7, 11)).then_inc(sem("b_prod"), 1)

            def head(g, gp, hh):
                for kind, dh, i in steps(("scores", "turn", "products", "proj"), g, hh):
                    h = QPG * g + hh + dh
                    if kind == "scores":
                        scores(h, *head_at(g, gp, hh, dh), i)
                    elif kind == "turn":
                        turn(h, (hh + dh) % 2, i)
                    elif kind == "products":
                        products(h, *head_at(g, gp, hh, dh), i)
                    elif kind == "proj":
                        after(pe, "b_ot", 2 * (QPG * g + hh))
                        proj(6 * (g + 1 + dh) + i, g + 1 + dh, i)

            def group(g, gp):
                for hh in range(QPG):
                    head(g, gp, hh)

            proj(0, 0, 0)
            proj(1, 0, 1)
            pe.wait_ge(sem("b_wv_lo"), 1)
            values_b(range(4))
            proj(2, 0, 2)
            values_b((4, 5))
            proj(3, 0, 3)
            values_b((6, 7))
            proj(4, 0, 4)
            proj(5, 0, 5)
            pe.wait_ge(sem("b_vout"), NT)
            head(-1, 1, QPG - 2)
            head(-1, 1, QPG - 1)
            all_groups(pe, group)
            head(NG, 0, 0)
            head(NG, 0, 1)
            out_proj("b", False)
            turn_back("b")
            ffn("g")


SCORE_TILES = [7, 6, 5, 4, 0, 1, 2, 3]
DUE = {
    "scores": [-9894, -8798, -6493, -5372, -4565, -2890, -2016, -789],
    "max": [-9444, -7440, -7069, -4009, -2847, -2053, -1607, -675],
    "exp": [-6480, -5178, -3291, -2808, -561, 35, 907, 2323],
    "inv": [-7333, -5571, -3963, -1688, -1674, -694, 44, 2103],
    "norm": [-8960, -8753, -8258, -5953, -5213, -1683, -690, 24],
    "turn": [225, 302, 1489, 2414, 4364, 4676, 5579, 6681, 6819, 7498, 8647, 9574],
    "pt_hi": [3282, 3372, 3689, 4056, 6406, 6850, 7043, 7937, 9937, 10221, 11092, 11249],
    "pt_lo": [673, 2143, 2647, 2921, 5181, 6125, 6452, 7556, 8136, 9242, 9746, 9869],
    "products": [1776, 4108, 4621, 5155, 6016, 6875, 7334, 8480, 9540, 9878, 10239, 11038],
    "o_low": [10888, 13488],
    "o_add": [9944, 12180],
    "proj": [4050, 6387, 13340, 23376, 32419, 35804],
    "raw": [5061, 8175, 14963, 24274, 34484, 37311],
    "cos": [5490, 7815, 16560, 23953, 33469, 37563],
    "rotate": [4038, 4409, 12260, 21398, 33400, 40508],
    "high": [11758, 16133, 21385, 30749, 41417, 47021],
    "low": [13396, 17882, 27446, 29557, 44833, 47488],
}
PIECES = ("proj", "raw", "cos", "rotate", "high", "low")


def steps(kinds, g, hh):
    found = []
    for kind in kinds:
        piece = kind in PIECES
        for n, due in enumerate(DUE[kind]):
            if piece:
                behind, at = divmod(due - 10000 * hh, 10000 * QPG)
                if at >= 10000:
                    continue
                exists = not isinstance(g, int) or 0 <= g - behind < NG - 1
            else:
                behind, at = divmod(due, 10000)
                exists = not isinstance(g, int) or 0 <= QPG * g + hh - behind < QPG * NG
            if exists:
                found.append((at, kind, -behind, n))
    return [step[1:] for step in sorted(found)]


DUE_A = {
    "scores": [-2814, -2697, 374, 3456],
    "max": [-5526, -2751, -703, 2846],
    "exp": [-3466, -584, -433, 2074],
    "inv": [-3918, -2077, 933, 3313],
    "norm": [-1286, 252, 5740, 8099],
    "turn": [3024, 3161, 3794, 7608],
    "pt": [1207, 1472, 2634, 7879],
    "products": [3717, 5961, 10934, 11408],
    "qk": [-11595, -10158, -8812, -6881],
    "rope": [-12107, -11071, -10381, -8168],
    "rotate": [-10532, -8716, -2282, -2146],
    "o_out": [6909, 10401],
    "lora": [-23336],
    "weff": [-26505],
    "w_hi": [-22148],
    "w_lo": [-20996],
    "values": [-5947, -5197, -5193, -4867, -4660],
    "v_out": [-6442, -5984, -5916, -4629, -3917],
}
PAIRED = ("values", "v_out")


def steps_a(kinds, i, u):
    found = []
    for kind in kinds:
        for n, due in enumerate(DUE_A[kind]):
            if kind in PAIRED:
                behind, at = divmod(due - 10000 * u, 20000)
                if at >= 10000:
                    continue
                exists = not isinstance(i, int) or 0 <= i - behind < HA // 2
            else:
                behind, at = divmod(due, 10000)
                exists = not isinstance(i, int) or 0 <= 2 * i + u - behind < HA
            if exists:
                found.append((at, kind, -behind, n))
    return [step[1:] for step in sorted(found)]


def head_at(g, gp, hh, dh):
    dg, hh = divmod(hh + dh, QPG)
    return g + dg, (gp + dg) % 2, hh


def pieces_before(g, hh):
    done = sum(due < 10000 * hh + DUE["products"][8] for due in DUE["proj"])
    return 6 * g + 6 + (0 if isinstance(g, int) and g == NG - 1 else done)


def chunk_columns(slot):
    first = max(0, slot - 4) if slot < 8 else slot - 8
    return first, 4 - first


V_SPLIT_AT, W_LO_AT = 3, 6

OT_ALL = {"a": 2 * HA, "b": 2 * QPG * NG}


F_TOTAL = {"ln": 2 * NT, "var": 2, "rstd": 2, "z": NT, "zt": 4, "xt_hi": 4, "xt_lo": 4,
           "consts": 48, "wg_hi": 1, "wg_lo": 1, "logits_t": 2, "lgs": 2, "logits": 1, "route": 14, "shifted": 1, "ex": 1,
           "cwb": 1, "cwt_turned": 1, "cwt": 1,
           "wf_loaded0": 16 * (NJ - NJ // 2), "wf_loaded1": 16 * (NJ // 2), "w_hi": NJ, "w_lo": NJ,
           "g": 2 * NJ, "u": 2 * NJ, "c": 2 * (NJ - N_SHARED), "silu": 2 * NJ, "gu": 2 * (NJ - N_SHARED), "h": 2 * NJ,
           "h_hi": 2 * NJ, "h_lo": 2 * NJ, "down": 2 * NJ,
           "yt": 4, "y_turned": 4, "added": 4}


def since(s, name):
    return F_TOTAL[name] if s == "g" else 0


def loads(n, u, each):
    return (each // 2) * n + each - (each // 2) * u


def rope_table(half, copies, scale, by_source):
    inv = (1.0 / 10000.0 ** (np.arange(half, dtype=np.float32) / half)).astype(np.float32)
    ang = (np.arange(T, dtype=np.float32)[:, None] * inv[None, :]).astype(np.float32)
    cos = np.cos(ang.astype(np.float64)).T
    sin = np.sin(ang.astype(np.float64)).T
    c = np.concatenate([cos, cos] * copies)
    s = np.concatenate(([sin, -sin] if by_source else [-sin, sin]) * copies)
    return np.ascontiguousarray(np.stack([c, s], 1) * scale).astype(np.float32)


def kernel(**inputs):
    import ml_dtypes
    import concourse.bacc as _bacc
    from concourse.bass_utils import run_bass_kernel_spmd as _run

    bf16 = ml_dtypes.bfloat16
    a = {k.replace("L0_", ""): np.asarray(v) for k, v in inputs.items()}
    f = np.float32
    m = {}
    m["x"] = a["attn_a_x"].reshape(NT, P, D)
    m["idf"] = np.eye(P, dtype=f)
    m["idb"] = np.eye(P, dtype=f).astype(bf16)
    m["norm_w"] = a["attn_a_norm_w"].reshape(NC, P).T
    w = np.stack([a["attn_a_wq"], a["attn_a_wk"], a["attn_a_wv"]]).reshape(3, HA, P, NC, P)
    m["wa"] = w.transpose(1, 4, 3, 0, 2)
    m["la"] = np.concatenate([a["attn_a_qA"], a["attn_a_kA"], a["attn_a_vA"]]).reshape(3 * RANK, NC, P)
    lb = np.zeros((HA, 3, RANK, 3, P), f)
    for n, key in enumerate(("qB", "kB", "vB")):
        lb[:, n, :, n, :] = a[f"attn_a_{key}"].reshape(HA, P, RANK).transpose(0, 2, 1)
    m["lb"] = lb.reshape(HA, 3 * RANK, 3 * P)
    m["wo_a"] = a["attn_a_wo"].T.reshape(HA, P, D)
    m["oa"] = a["attn_a_oA"].reshape(RANK, HA, P).transpose(1, 0, 2)
    m["ob"] = a["attn_a_oB"].T
    m["rope_a"] = rope_table(64, 1, 128.0 ** -0.25, True)
    m["rope_b"] = rope_table(32, 2, 64.0 ** -0.25, False)
    q, k = np.arange(P)[:, None], np.arange(KW)[None, :]
    seen = (k > q) & (k <= q + WIN)
    NEG = -1e30
    m["maska"] = np.where(np.stack([seen & (k >= WIN), seen], 1), 0.0, NEG).astype(bf16)
    m["maskb"] = np.where(np.arange(P)[None, :] <= q, 0.0, NEG).astype(bf16)
    rows = NJ * P - NE * I_E - I_S
    pad = np.zeros((rows, D), f)
    gate = np.concatenate([a["ffn_sw_gate"], a["ffn_w_gate"].reshape(-1, D), pad]).reshape(NJ, P, NC, P)
    upw = np.concatenate([a["ffn_sw_up"], a["ffn_w_up"].reshape(-1, D), pad]).reshape(NJ, P, NC, P)
    dn = np.concatenate([a["ffn_sw_down"].T, a["ffn_w_down"].transpose(0, 2, 1).reshape(-1, D), pad])
    m["wf"] = np.concatenate([gate.transpose(0, 3, 2, 1).reshape(NJ, P, D),
                              upw.transpose(0, 3, 2, 1).reshape(NJ, P, D), dn.reshape(NJ, P, D)], 2)
    m["wg"] = a["ffn_gate_w"].T.reshape(NC, P, NE).transpose(1, 0, 2)
    unit = np.arange(NJ * P)
    expert = np.where(unit < I_S, NE, np.minimum((unit - I_S) // I_E, NE - 1))
    one = (np.arange(NW)[:, None] == expert[None, :]).astype(f)
    m["sel"] = np.concatenate([one, one, one, np.zeros((P - 3 * NW, NJ * P), f)]).astype(bf16)
    m["iota"] = np.broadcast_to(np.arange(NE, dtype=f), (P, NT * TOPK, NE))
    wq = a["attn_b_Wq"].reshape(NC, P, NG, QPG * DB)
    wk = a["attn_b_Wk"].reshape(NC, P, NG, DB)
    m["wb"] = np.concatenate([wq, wk, wk], 3).transpose(2, 1, 0, 3)
    m["wvb"] = a["attn_b_Wv"].reshape(NC, P, NG * DB).transpose(1, 0, 2)
    m["wo_b"] = a["attn_b_Wo"].reshape(HA, P, D)

    nc = _bacc.Bacc("TRN2", target_bir_lowering=False, num_devices=1)
    arrays, args = {}, {}
    for name, v in m.items():
        arrays[f"in_{name}"] = np.ascontiguousarray(v)
        args[name] = nc.dram_tensor(f"in_{name}", v.shape, mybir.dt.from_np(v.dtype), kind="ExternalInput").ap()
    out = nc.dram_tensor("out", (NT, P, D), F32, kind="ExternalOutput").ap()
    build(nc, args, out)
    r = _run(nc, [arrays], core_ids=[0])
    return r.results[0]["out"].reshape(1, T, D)
```
